# Optimizing a Trainium2 kernel written in Bass

```python
import numpy as np
import jax
import jax.numpy as jnp

def _softmax(x, axis=-1):
    return jax.nn.softmax(x, axis=axis)
def _gelu(x):
    return jax.nn.gelu(x, approximate=True)
def _silu(x):
    return jax.nn.silu(x)
def _sigmoid(x):
    return jax.nn.sigmoid(x)
def _layernorm(x, axis=-1, eps=1e-5):
    m = jnp.mean(x, axis=axis, keepdims=True)
    v = jnp.var(x, axis=axis, keepdims=True)
    return (x - m) / jnp.sqrt(v + eps)
def _scatter_add(tgt, idx, src, axis=0):
    return tgt.at[idx].add(src)
def _segment_sum(src, seg, n):
    return jax.ops.segment_sum(src, seg, n)

kernel_name = 'mk_conv_attn_hybrid_d2_conv_nchw256_db76d6'

def setup_inputs(seed: int = 0):
    np.random.seed(seed)
    _w = jnp.asarray
    def _rec_inputs():
        import jax
        import jax.numpy as jnp
        _gk = jax.random.key(seed)
        x = -0.0005207 + 1.001 * jax.random.normal(jax.random.fold_in(_gk, 1), (8, 256, 32, 32), jnp.float32)
        return x
    x = _rec_inputs()
    def _L0_conv_setup():
        import jax, jax.numpy as jnp
        import numpy as np
        NUM_HEADS = 8
        K_STEPS = 3

        def _laplacian(H, W):
            yy, xx = jnp.meshgrid(jnp.arange(H, dtype=jnp.float32), jnp.arange(W, dtype=jnp.float32), indexing='ij')
            coords = jnp.stack([yy.ravel(), xx.ravel()], axis=-1)
            d2 = jnp.sum((coords[:, None, :] - coords[None, :, :]) ** 2, axis=-1)
            A = jnp.exp(-d2 / 2.0)
            L = jnp.diag(A.sum(axis=1)) - A
            return L
        key = jax.random.key(seed)
        ks = jax.random.split(key, 5)
        B, C, H, W = (8, 256, 32, 32)
        s = 0.02
        return {'x': jax.random.normal(ks[0], (B, C, H, W), dtype=jnp.float32), 'qkv_w': jax.random.normal(ks[1], (3 * C, C), dtype=jnp.float32) * s, 'qkv_b': jax.random.normal(ks[2], (3 * C,), dtype=jnp.float32) * s, 'proj_w': jax.random.normal(ks[3], (C, C), dtype=jnp.float32) * s, 'proj_b': jax.random.normal(ks[4], (C,), dtype=jnp.float32) * s, 'alpha': jnp.array(0.5, dtype=jnp.float32)}
    _L0_conv_all = _L0_conv_setup()
    _L0_conv_in = {k: v for k, v in _L0_conv_all.items() if k in ('qkv_w', 'qkv_b', 'proj_w', 'proj_b', 'alpha', )}
    del _L0_conv_all

    def _L1_attn_setup():
        import jax, jax.numpy as jnp
        import numpy as np
        W = 3
        key = jax.random.key(seed)
        ks = jax.random.split(key, 7)
        B, N, D = (8, 4096, 256)
        s = 1.0 / np.sqrt(D)
        return {'x': jax.random.normal(ks[0], (B, N, D), jnp.float32), 'Wq': jax.random.normal(ks[1], (D, D), jnp.float32) * s, 'bq': jax.random.normal(ks[2], (D,), jnp.float32) * 0.01, 'Wk': jax.random.normal(ks[3], (D, D), jnp.float32) * s, 'bk': jax.random.normal(ks[4], (D,), jnp.float32) * 0.01, 'Wv': jax.random.normal(ks[5], (D, D), jnp.float32) * s, 'bv': jax.random.normal(ks[6], (D,), jnp.float32) * 0.01}
    _L1_attn_all = _L1_attn_setup()
    _L1_attn_in = {k: v for k, v in _L1_attn_all.items() if k in ('Wq', 'bq', 'Wk', 'bk', 'Wv', 'bv', )}
    del _L1_attn_all

    def _L1_ffn_setup():
        import jax, jax.numpy as jnp
        import numpy as np
        BN_EPS = 0.001

        def _bn(h, g, b, m, v):
            return g * (h - m) * jax.lax.rsqrt(v + BN_EPS) + b
        key = jax.random.key(seed)
        ks = jax.random.split(key, 8)
        B, F, Df = (256, 64, 256)
        E, H, D = (8, 256, 256)
        s1 = 1.0 / np.sqrt(Df)
        s2 = 1.0 / np.sqrt(H)
        return {'x': jax.random.normal(ks[0], (B, F, Df), jnp.float32), 'Wr': jax.random.normal(ks[1], (Df, E), jnp.float32) * s1, 'br': jnp.zeros((E,), jnp.float32), 'W1': jax.random.normal(ks[2], (E, Df, H), jnp.float32) * s1, 'b1': jnp.zeros((E, H), jnp.float32), 'g1': jnp.ones((E, H), jnp.float32), 'be1': jnp.zeros((E, H), jnp.float32), 'm1': jnp.zeros((E, H), jnp.float32), 'v1': jnp.ones((E, H), jnp.float32), 'W2': jax.random.normal(ks[3], (E, H, H), jnp.float32) * s2, 'b2': jnp.zeros((E, H), jnp.float32), 'g2': jnp.ones((E, H), jnp.float32), 'be2': jnp.zeros((E, H), jnp.float32), 'm2': jnp.zeros((E, H), jnp.float32), 'v2': jnp.ones((E, H), jnp.float32), 'Wo': jax.random.normal(ks[4], (E, H, D), jnp.float32) * s2, 'bo': jnp.zeros((E, D), jnp.float32)}
    _L1_ffn_all = _L1_ffn_setup()
    _L1_ffn_in = {k: v for k, v in _L1_ffn_all.items() if k in ('Wr', 'br', 'W1', 'b1', 'g1', 'be1', 'm1', 'v1', 'W2', 'b2', 'g2', 'be2', 'm2', 'v2', 'Wo', 'bo', )}
    del _L1_ffn_all

    return {
        "x": x,
        "L0_conv_qkv_w": _L0_conv_in["qkv_w"],
        "L0_conv_qkv_b": _L0_conv_in["qkv_b"],
        "L0_conv_proj_w": _L0_conv_in["proj_w"],
        "L0_conv_proj_b": _L0_conv_in["proj_b"],
        "L0_conv_alpha": _L0_conv_in["alpha"],
        "L1_attn_Wq": _L1_attn_in["Wq"],
        "L1_attn_bq": _L1_attn_in["bq"],
        "L1_attn_Wk": _L1_attn_in["Wk"],
        "L1_attn_bk": _L1_attn_in["bk"],
        "L1_attn_Wv": _L1_attn_in["Wv"],
        "L1_attn_bv": _L1_attn_in["bv"],
        "L1_ffn_Wr": _L1_ffn_in["Wr"],
        "L1_ffn_br": _L1_ffn_in["br"],
        "L1_ffn_W1": _L1_ffn_in["W1"],
        "L1_ffn_b1": _L1_ffn_in["b1"],
        "L1_ffn_g1": _L1_ffn_in["g1"],
        "L1_ffn_be1": _L1_ffn_in["be1"],
        "L1_ffn_m1": _L1_ffn_in["m1"],
        "L1_ffn_v1": _L1_ffn_in["v1"],
        "L1_ffn_W2": _L1_ffn_in["W2"],
        "L1_ffn_b2": _L1_ffn_in["b2"],
        "L1_ffn_g2": _L1_ffn_in["g2"],
        "L1_ffn_be2": _L1_ffn_in["be2"],
        "L1_ffn_m2": _L1_ffn_in["m2"],
        "L1_ffn_v2": _L1_ffn_in["v2"],
        "L1_ffn_Wo": _L1_ffn_in["Wo"],
        "L1_ffn_bo": _L1_ffn_in["bo"],
    }

def reference(x, L0_conv_qkv_w, L0_conv_qkv_b, L0_conv_proj_w, L0_conv_proj_b, L0_conv_alpha, L1_attn_Wq, L1_attn_bq, L1_attn_Wk, L1_attn_bk, L1_attn_Wv, L1_attn_bv, L1_ffn_Wr, L1_ffn_br, L1_ffn_W1, L1_ffn_b1, L1_ffn_g1, L1_ffn_be1, L1_ffn_m1, L1_ffn_v1, L1_ffn_W2, L1_ffn_b2, L1_ffn_g2, L1_ffn_be2, L1_ffn_m2, L1_ffn_v2, L1_ffn_Wo, L1_ffn_bo):
    import jax
    import jax.numpy as jnp
    def _L0_conv_ref(x, qkv_w, qkv_b, proj_w, proj_b, alpha):
        import jax, jax.numpy as jnp
        import numpy as np
        NUM_HEADS = 8
        K_STEPS = 3

        def _laplacian(H, W):
            yy, xx = jnp.meshgrid(jnp.arange(H, dtype=jnp.float32), jnp.arange(W, dtype=jnp.float32), indexing='ij')
            coords = jnp.stack([yy.ravel(), xx.ravel()], axis=-1)
            d2 = jnp.sum((coords[:, None, :] - coords[None, :, :]) ** 2, axis=-1)
            A = jnp.exp(-d2 / 2.0)
            L = jnp.diag(A.sum(axis=1)) - A
            return L
        B, C, H, W = x.shape
        hd = C // NUM_HEADS
        N = H * W
        qkv = jnp.einsum('bchw,oc->bohw', x, qkv_w) + qkv_b[None, :, None, None]
        q, k, v = jnp.split(qkv, 3, axis=1)

        def to_heads(t):
            return t.reshape(B, NUM_HEADS, hd, N).transpose(0, 1, 3, 2).reshape(B * NUM_HEADS, N, hd)
        q, k, v = (to_heads(q), to_heads(k), to_heads(v))
        attn = jax.nn.softmax(jnp.einsum('bnd,bmd->bnm', q, k) / jnp.sqrt(jnp.float32(hd)), axis=-1)
        attn_out = jnp.einsum('bnm,bmd->bnd', attn, v)
        attn_out = attn_out.reshape(B, NUM_HEADS, N, hd).transpose(0, 2, 1, 3).reshape(B, N, C)
        L = _laplacian(H, W)
        lam_max = jnp.linalg.eigvalsh(L).max()
        L_hat = 2.0 / lam_max * L - jnp.eye(N, dtype=L.dtype)
        v_diff = v
        for _ in range(K_STEPS):
            v_diff = jnp.einsum('nm,bmd->bnd', L_hat, v_diff)
        v_diff = v_diff.reshape(B, NUM_HEADS, N, hd).transpose(0, 2, 1, 3).reshape(B, N, C)
        out = alpha * attn_out + (1.0 - alpha) * v_diff
        out = out.transpose(0, 2, 1).reshape(B, C, H, W)
        out = jnp.einsum('bchw,oc->bohw', out, proj_w) + proj_b[None, :, None, None]
        return out

    def _L1_attn_ref(x, Wq, bq, Wk, bk, Wv, bv):
        import jax, jax.numpy as jnp
        import numpy as np
        W = 3
        B, N, D = x.shape
        scale = jnp.asarray(np.sqrt(D), x.dtype)
        Q = x @ Wq.T + bq
        K = x @ Wk.T + bk
        V = x @ Wv.T + bv
        offsets = jnp.arange(-W, W + 1)
        pos = jnp.arange(N)[:, None] + offsets[None, :]
        valid = (pos >= 0) & (pos < N)
        idx = jnp.clip(pos, 0, N - 1)
        Kw = K[:, idx]
        Vw = V[:, idx]
        scores = jnp.einsum('bnd,bnwd->bnw', Q, Kw) / scale
        scores = jnp.where(valid[None], scores, jnp.asarray(-jnp.inf, scores.dtype))
        probs = jax.nn.softmax(scores, axis=-1)
        return jnp.einsum('bnw,bnwd->bnd', probs, Vw)

    def _L1_ffn_ref(x, Wr, br, W1, b1, g1, be1, m1, v1, W2, b2, g2, be2, m2, v2, Wo, bo):
        import jax, jax.numpy as jnp
        import numpy as np
        BN_EPS = 0.001

        def _bn(h, g, b, m, v):
            return g * (h - m) * jax.lax.rsqrt(v + BN_EPS) + b
        feat = jnp.mean(x, axis=0)
        w = jax.nn.softmax(feat @ Wr + br, axis=-1)
        h = jnp.einsum('bfd,edh->bfeh', x, W1) + b1
        h = jax.nn.relu(_bn(h, g1, be1, m1, v1))
        h = jnp.einsum('bfeh,ehk->bfek', h, W2) + b2
        h = jax.nn.relu(_bn(h, g2, be2, m2, v2))
        y = jnp.einsum('bfeh,ehd->bfed', h, Wo) + bo
        return jnp.einsum('bfed,fe->bfd', y, w)

    def _gn(v, G=32, eps=1e-5):
        B_, C_, H_, W_ = v.shape
        g = v.reshape(B_, G, C_ // G, H_, W_)
        m = jnp.mean(g, axis=(2, 3, 4), keepdims=True)
        s = jnp.var(g, axis=(2, 3, 4), keepdims=True)
        return ((g - m) / jnp.sqrt(s + eps)).reshape(v.shape)

    def _ln_c(v, eps=1e-6):
        m = jnp.mean(v, axis=1, keepdims=True)
        s = jnp.var(v, axis=1, keepdims=True)
        return (v - m) / jnp.sqrt(s + eps)

    def _ln_t(v, eps=1e-5):
        m = jnp.mean(v, axis=-1, keepdims=True)
        s = jnp.var(v, axis=-1, keepdims=True)
        return (v - m) / jnp.sqrt(s + eps)

    def _to_tokens(v):
        B_, C_, H_, W_ = v.shape
        return v.reshape(B_, C_, H_ * W_).transpose(0, 2, 1)
    def _from_tokens(t, like):
        B_, C_, H_, W_ = like.shape
        return t.transpose(0, 2, 1).reshape(B_, C_, H_, W_)

    x = x + _L0_conv_ref(_gn(x), L0_conv_qkv_w, L0_conv_qkv_b, L0_conv_proj_w, L0_conv_proj_b, L0_conv_alpha)
    t = _to_tokens(x)
    t = t + _L1_attn_ref(_ln_t(t), L1_attn_Wq, L1_attn_bq, L1_attn_Wk, L1_attn_bk, L1_attn_Wv, L1_attn_bv)
    t = t + _L1_ffn_ref(_ln_t(t), L1_ffn_Wr, L1_ffn_br, L1_ffn_W1, L1_ffn_b1, L1_ffn_g1, L1_ffn_be1, L1_ffn_m1, L1_ffn_v1, L1_ffn_W2, L1_ffn_b2, L1_ffn_g2, L1_ffn_be2, L1_ffn_m2, L1_ffn_v2, L1_ffn_Wo, L1_ffn_bo)
    x = _from_tokens(t, x)
    return x


_drawn_inputs = setup_inputs


def setup_inputs(seed=0):
    import zlib

    import numpy as np

    out = dict(_drawn_inputs(seed))
    spreads = {'L1_ffn_br': (0.0, 0.583),
     'L1_ffn_b1': (0.0, 0.441),
     'L1_ffn_g1': (1.0, 0.2),
     'L1_ffn_be1': (0.0, 0.485),
     'L1_ffn_m1': (0.0, 0.451),
     'L1_ffn_v1': (1.0, 0.6),
     'L1_ffn_b2': (0.0, 0.322),
     'L1_ffn_g2': (1.0, 0.2),
     'L1_ffn_be2': (0.0, 0.37),
     'L1_ffn_m2': (0.0, 0.319),
     'L1_ffn_v2': (1.0, 0.6),
     'L1_ffn_bo': (0.0, 0.1)}
    factors = {'L0_conv_qkv_b': 8.0, 'L1_attn_bq': 8.0, 'L1_attn_bk': 8.0, 'L1_attn_bv': 6.081}
    for name, (base, spread) in spreads.items():
        noise = np.random.default_rng([zlib.crc32(name.encode()), seed]).standard_normal(out[name].shape)
        drawn = base * np.exp(spread * noise) if base else spread * noise
        out[name] = jnp.asarray(drawn.astype(out[name].dtype))
    for name, factor in factors.items():
        out[name] = (out[name] * factor).astype(out[name].dtype)
    return out
```

```python
from contextlib import ExitStack

import concourse.bass as bass
from concourse import mybir

F32 = mybir.dt.float32
F32R = mybir.dt.float32r
ALU = mybir.AluOpType
ACT = mybir.ActivationFunctionType
AXX = mybir.AxisListType.X

P = 128
B, C, H, W = 8, 256, 32, 32
N = H * W
CT = C // P
HALF = N // 2
NH = 8
HD = C // NH
QUAD = P // HD
NT = N // P
PAIRS = NH // 2
UNITS = 2 * NT
SHIFT = 3 * HD
STACK = SHIFT + 16
GROUP = C // 32
HH, HW = H // 2, W // 2
FT = HH * HW // P
WIN = 3
NBLK = -(-N // (P - 2 * WIN))
BLK = -(-N // NBLK)
E = 8
EPS = 1e-5
BN_EPS = 1e-3
HEAD_SCALE = float(HD) ** -0.5
WIN_SCALE = float(C) ** -0.5
NEXT_QUAD_AT = (0, 8)
TURN_AT = NT + 2
DRAIN_AT = NT + 2
MIX_AT = ((1, 13), (2, 3), (3, 13), (4, 0))
MIX_HI_AT = ((2, 0), (2, 9), (4, 0), (4, 0))
MIX_LO_AT = ((2, 4), (2, 13), (4, 0), (4, 0))
FREE, FREE_DMA = 1, 16
FRONT_LINKS = 11
HEAD_LINKS = NH
FAR = -1e30


class Uses:

    def __init__(self, ready, free, tile, keys):
        self.ready, self.free, self.tile = ready, free, tile
        self.at = {k: n for n, k in enumerate(keys)}
        self.per = len(keys)

    def wait_free(self, eng, b, key):
        eng.wait_ge(self.free, b * self.per + self.at[key] + 1)

    def wait_ready(self, eng, b, key):
        eng.wait_ge(self.ready, b * self.per + self.at[key] + 1)

    def wait_drained(self, eng, b, key):
        eng.wait_ge(self.free, b * self.per + self.at[key] + 2)


class Link:

    def __init__(self, eng, sem, base):
        self.eng, self.sem, self.base, self.n = eng, sem, base, 0

    def done(self, ins):
        self.n += 1
        ins.then_inc(self.sem, 1)

    def wait(self):
        self.eng.wait_ge(self.sem, self.base + self.n)



def attention_phase(nc, x, qkv_wT, qkv_b, proj_wT, proj_b, alpha, window_wT, window_b,
                    diffusion, t_d, n_d, feat_d):
    x_v = x.rearrange("b (c p) n -> b p c n", p=P)

    with ExitStack() as ctx:
        def sb(name, shape, dt=F32):
            return ctx.enter_context(nc.sbuf_tensor(name, shape, dt))

        def sem(name):
            return ctx.enter_context(nc.semaphore(name))

        ident = sb("ident", [P, P])
        ones = sb("ones", [P, P])
        mean_c = sb("mean_c", [P, P])
        group_mean = sb("group_mean", [P, P])
        minus_half = sb("minus_half", [P, NT])
        win_mask = sb("win_mask", [P, 3, P])
        tile_mask = sb("tile_mask", [16, NT])
        low_rows = sb("low_rows", [16, 1])
        wh = sb("qkv_w_hi", [P, CT, 3 * C], F32R)
        wl = sb("qkv_w_lo", [P, CT, 3 * C], F32R)
        ph = sb("proj_w_hi", [P, CT, C], F32R)
        pl = sb("proj_w_lo", [P, CT, C], F32R)
        mh = sb("diffusion_hi", [P, 4, FT, HH * HW], F32R)
        ml = sb("diffusion_lo", [P, 4, FT, HH * HW], F32R)
        w1 = sb("window_w", [P, 3, CT, C])
        qkb = sb("qkv_bias", [P, 6])
        pb = sb("proj_bias", [P, CT])
        vcol = sb("v_bias_scaled", [P, CT])
        wb = sb("window_bias", [P, 3, CT])
        al = sb("alphas", [P, 3])

        xin = sb("xin", [P, CT, N])
        stats = sb("stats", [P, CT, 2, 6])
        aggr = sb("aggr", [P, CT, 2])
        gstat = sb("gstat", [P, 2, CT])
        gmean = sb("gmean", [P, 2, CT])
        gtmp = sb("gtmp", [P, 2, CT])
        gvar = sb("gvar", [P, CT])
        grstd = sb("grstd", [P, CT])
        gbias = sb("gbias", [P, CT])
        xh = sb("xn_hi", [P, CT, N], F32R)
        xl = sb("xn_lo", [P, CT, N], F32R)
        ysum = sb("y_folded_or_parities", [P, 2, CT, N // 2])
        fh = sb("fold_or_mix_hi", [P, CT, N], F32R)
        fl = sb("fold_or_mix_lo", [P, CT, N], F32R)
        qk = sb("qk_parts", [P, 4, N], F32R)
        stack = [sb(f"stack{s}", [P, 2, N], F32R) for s in range(QUAD)]
        v = sb("v", [P, NT, C])
        unfold = sb("unfolded_y", [P, 2, H, HW])
        vd = sb("v_diffused", [P, CT, N])
        mx = sb("row_max", [P, 2, NT, 2])
        mx2 = sb("row_max_twice", [P, 2, 2, NT])
        th = sb("shift_hi", [16, P], F32R)
        td = sb("shift_parts", [16, P])
        at0 = -(-nc.sbuf_base // 32) * 32
        sb("room", [P, 4 * N])
        vf = [nc.alloc_sbuf_tensor_at(f"v_folded_{s}", [P, 4, FT, C], F32R, offset=at0 + k * 8192)
              for k, s in enumerate(("hi", "lo"))]
        prob = nc.alloc_sbuf_tensor_at("prob", [P, 2, 2, HALF], F32, offset=at0)
        att = nc.alloc_sbuf_tensor_at("attended", [P, N], F32, offset=at0 + 8192)
        den = nc.alloc_sbuf_tensor_at("denominators", [P, N], F32, offset=at0 + 12288)

        x2 = sb("x2", [P, CT, N])
        xw = sb("xn_padded", [P, CT, N + 8])
        sq = sb("squares_or_block", [P, CT * N])
        lnv = sb("ln_var", [P, NT])
        lnr = sb("ln_rstd", [P, NT])
        wneg = sb("win_minus_max", [P, 2])
        wden = sb("win_den", [P, 2])
        squares = sq[:, :].rearrange("p (c n) -> p c n", c=CT)
        diag = sq[:, 0:NT * P].rearrange("p (t n) -> p t n", t=NT)
        kb = sq[:, 0:256].rearrange("p (m n) -> p m n", m=CT)
        qb = sq[:, 256:512].rearrange("p (m n) -> p m n", m=CT)
        vb = sq[:, 512:768]
        sm = sq[:, 768:896]
        pm = sq[:, 896:1024]
        pt = sq[:, 1024:1152]

        bank = [ctx.enter_context(nc.psum_tensor(f"bank{k}", [P, HALF], F32)) for k in range(8)]

        def split_store(eng, hi, lo, src, s_hi, n):
            eng.tensor_copy(hi, src).then_inc(s_hi, 1)
            eng.wait_ge(s_hi, n)
            return eng.tensor_tensor(lo, src, hi.bitcast(F32), ALU.subtract)

        s_in = {k: sem(f"in_{k}") for k in ("w", "p", "m", "b", "mid")}
        s_made, s_hi, s_lo, s_al, s_vb, s_pbp, s_zero, s_fz = (
            sem(k) for k in ("const_made", "w_hi", "w_lo", "alpha_made", "vbias_made",
                             "pbias_ready", "feat_zero", "feat_zeroed"))
        with nc.Block() as block:
            @block.sync
            def _(sp):
                sp.dma_start(squares[:, :, 0:3 * C], qkv_wT.rearrange("(c p) o -> p c o", p=P)).then_inc(s_in["w"], 16)
                sp.dma_start(vd[:, :, 0:C], proj_wT.rearrange("(c p) o -> p c o", p=P)).then_inc(s_in["p"], 16)
                sp.dma_start(x2[:, :, :].rearrange("p c n -> p (c n)").rearrange("p (a u m) -> p a u m", a=4, u=FT),
                             diffusion.rearrange("a (u p) m -> p a u m", p=P)).then_inc(s_in["m"], 16)
                sp.dma_start(w1[:, :, :, :], window_wT.rearrange("a (c p) o -> p a c o", p=P)).then_inc(s_in["b"], 16)
                sp.dma_start(qkb[:, :], qkv_b).then_inc(s_in["b"], 16)
                sp.dma_start(pb[:, :], proj_b).then_inc(s_in["b"], 16)
                sp.dma_start(wb[:, :, :], window_b).then_inc(s_in["b"], 16)
                sp.dma_start(al[:, 0:1], alpha.partition_broadcast(P)).then_inc(s_in["b"], 16)
                sp.wait_ge(s_zero, 1)
                sp.dma_start(feat_d, xin[:, :, :]).then_inc(s_fz, 16)
                sp.wait_ge(s_fz, 16)

            @block.gpsimd
            def _(pool):
                link = Link(pool, s_made, 0)
                link.done(pool.memset(xin[:, :, :], 0.0))
                link.done(pool.memset(ones[:, :], 1.0))
                link.done(pool.memset(ident[:, :], 0.0))
                link.done(pool.memset(mean_c[:, :], 1.0 / C))
                link.done(pool.memset(group_mean[:, :], 1.0 / GROUP))
                link.done(pool.memset(minus_half[:, :], -0.5))
                link.done(pool.memset(win_mask[:, :, :], 0.0))
                link.done(pool.memset(tile_mask[:, :], 0.0))
                link.done(pool.memset(low_rows[:, :], 0.0))
                link.done(pool.memset(xw[:, :, :], 0.0))
                link.wait()
                pool.sem_inc(s_zero, 1)

                def cut(ap, cmp, fill, base, pattern, mult):
                    link.done(pool.affine_select(out=ap, in_=ap, compare_op=cmp, fill=fill, base=base,
                                                 pattern=pattern, channel_multiplier=mult))
                    link.wait()

                cut(ident[:, :], ALU.not_equal, 1.0, 0, [[-1, P]], 1)
                gm = group_mean[:, :].rearrange("p (g k) -> p g k", k=GROUP)
                cut(gm, ALU.is_ge, 0.0, 0, [[-GROUP, P // GROUP], [0, GROUP]], 1)
                cut(gm, ALU.is_ge, 0.0, GROUP - 1, [[GROUP, P // GROUP], [0, GROUP]], -1)
                wm = win_mask[:, :, :]
                cut(wm, ALU.is_ge, FAR, 0, [[0, 3], [1, P]], -1)
                cut(wm, ALU.is_ge, FAR, 2 * WIN, [[0, 3], [-1, P]], 1)
                cut(win_mask[:, 0, :], ALU.is_ge, FAR, -WIN, [[1, P]], 0)
                cut(win_mask[:, 2, :], ALU.is_ge, FAR, N - (NBLK - 1) * BLK + WIN - 1, [[-1, P]], 0)
                cut(tile_mask[:, :], ALU.not_equal, -1.0, 0, [[-1, NT]], 1)
                cut(tile_mask[:, :], ALU.not_equal, -1.0, -NT, [[-1, NT]], 1)
                cut(low_rows[:, :], ALU.is_ge, -1.0, NT - 1, [[0, 1]], -1)

            @block.vector
            def _(dve):
                link = Link(dve, s_hi, 0)
                for name, hi, lo, src in (
                        ("w", wh[:, :, :], wl[:, :, :], squares[:, :, 0:3 * C]),
                        ("p", ph[:, :, :], pl[:, :, :], vd[:, :, 0:C]),
                        ("m", mh[:, :, :, :], ml[:, :, :, :],
                         x2[:, :, :].rearrange("p c n -> p (c n)").rearrange("p (a u m) -> p a u m", a=4, u=FT))):
                    dve.wait_ge(s_in[name], 16)
                    link.done(dve.tensor_copy(hi, src))
                    link.wait()
                    dve.tensor_tensor(lo, src, hi.bitcast(F32), ALU.subtract).then_inc(s_lo, 1)
                dve.wait_ge(s_in["b"], 5 * 16)
                dve.tensor_scalar(al[:, 1:2], al[:, 0:1], -1.0, 1.0, ALU.mult, ALU.add).then_inc(s_al, 1)
                dve.tensor_scalar(al[:, 2:3], al[:, 0:1], 2.0, -1.0, ALU.mult, ALU.add).then_inc(s_al, 1)
                dve.wait_ge(s_al, 2)
                dve.tensor_scalar(vcol[:, :], qkb[:, 4:6], al[:, 2:3], None, ALU.mult).then_inc(s_vb, 1)
                dve.wait_ge(s_pbp, 1)
                dve.tensor_tensor(pb[:, :], bank[0][:, 0:CT], pb[:, :], ALU.add).then_inc(s_al, 1)
                dve.wait_ge(s_made, 2)
                for s in range(QUAD):
                    for h in range(NT):
                        link.done(dve.tensor_copy(stack[s][SHIFT:P, 1, h * P:(h + 1) * P], ones[SHIFT:P, :]))

            @block.tensor
            def _(pe):
                pe.wait_ge(s_vb, 1)
                pe.wait_ge(s_in["p"], 16)
                for m in range(CT):
                    for k in range(CT):
                        last = pe.matmul(bank[0][:, m:m + 1], vd[:, k, m * P:(m + 1) * P], vcol[:, k:k + 1],
                                         start=k == 0, stop=k == CT - 1)
                last.then_inc(s_pbp, 1)

        def smax_keys():
            keys = (["gn"], [])
            for h in range(NH):
                for t in range(NT):
                    for half in range(2):
                        keys[half].append(("smax", h, t))
                    if h > 1 and h % 2 and t == TURN_AT - NT:
                        keys[0].append(("turn", h - 1))
                if h < 2 or h % 2:
                    keys[h % 2].append(("turn", h))
            return keys

        def score_keys():
            keys, n = ([], []), 0
            for key in (["q0h0", "q0h1", "k0h0", "k0h1"] + [("v", g) for g in range(4)]
                        + [("fold", a) for a in range(4)] + [("diffuse", c, s) for c in range(CT) for s in range(2)]):
                keys[n % 2].append(key)
                n += 1
            for pair in range(PAIRS):
                for u in range(UNITS):
                    if (pair, u) == NEXT_QUAD_AT:
                        for n, key in enumerate(["q1h0", "q1h1", "k1h0", "k1h1"]):
                            keys[n % 2].append(key)
                    for ab in range(2):
                        keys[ab].append(("score", pair, u))
            return keys

        def post_keys():
            keys = ([], [])
            for half in range(2):
                for m in range(CT):
                    keys[m].append(("proj", half))
            for ln in range(2):
                for half in range(2):
                    keys[half].append(("mean", ln))
                keys[0].append(("var", ln))
                for half in range(2):
                    keys[half].append(("rstd", ln))
                if ln == 0:
                    for j in range(NBLK):
                        keys[0].extend([("kq", j), ("ws", j), ("wo", j)])
                        keys[1].extend([("wv", j), ("wt", j)])
            return keys

        def ring(name, first, keys):
            return [Uses(sem(f"{name}{k}_ready"), sem(f"{name}{k}_free"), bank[first + k], keys[k]) for k in range(2)]

        M = ring("max", 0, smax_keys())
        T = ring("score", 2, score_keys())
        O = ring("attend", 4, [list(range(PAIRS))] * 2)
        Q = ring("post", 6, post_keys())

        x_landed = sem("x_landed")
        stats_made = sem("stats_made")
        feat_asked = sem("feat_asked")
        gstat_made = sem("gstat_made")
        gvar_made = sem("gvar_made")
        grstd_made = sem("grstd_made")
        xn_made = sem("xn_made")
        xh_made = sem("xh_made")
        xl_made = sem("xl_made")
        fold_made = sem("fold_made")
        fh_made = sem("fh_made")
        fl_made = sem("fl_made")
        qkh_made = sem("qkh_made")
        stacked = [sem(f"stacked{s}") for s in range(QUAD)]
        vfh_made = sem("vfh_made")
        vd_made = sem("vd_made")
        rowmax_made = sem("rowmax_made")
        shift_made = sem("shift_made")
        prob_used = sem("prob_used")
        mix_made = sem("mix_made")
        mixh_made = sem("mixh_made")
        mixl_made = sem("mixl_made")
        x_again = sem("x_again")
        sq_made = sem("sq_made")
        rstd_made = sem("rstd_made")
        diag_made = sem("diag_made")
        neg_made = sem("neg_made")
        wexp_made = sem("wexp_made")
        wprob_made = sem("wprob_made")
        t_stored = sem("t_stored")
        n_stored = sem("n_stored")
        feat_added = sem("feat_added")
        feat_done = sem("feat_done")
        dve_front, dve_heads, dve_mix, dve_post = (sem(f"dve_{k}_chain") for k in ("front", "heads", "mix", "post"))
        pool_front = sem("pool_front")

        def unit_of(u):
            return u // NT, u % NT

        def block_size(j):
            return min(BLK, N - j * BLK)

        block = ctx.enter_context(nc.Block())

        @block.sync
        def _(sp):
            with sp.Fori(0, B) as b:
                sp.wait_ge(fl_made, FREE + b * CT)
                sp.dma_start(xin[:, :, :], x_v[b]).then_inc(x_landed, 16)
                for quad in range(2):
                    for s in range(QUAD):
                        rows = slice(HD * s, HD * (s + 1))
                        if quad == 0 and s == 0:
                            T[1].wait_drained(sp, b, "k0h1")
                        elif quad == 1 and s % 2 == 0:
                            T[1].wait_drained(sp, b, ("score", s // 2, UNITS - 1))
                        sp.dma_start(stack[s][0:HD, :, :].bitcast(F32), qk[rows, 1:3, :].bitcast(F32)).then_inc(stacked[s], 16)
                        sp.dma_start(stack[s][HD:2 * HD, :, :].bitcast(F32), qk[rows, 0:3:2, :].bitcast(F32)).then_inc(stacked[s], 16)
                        sp.dma_start(stack[s][2 * HD:3 * HD, :, :].bitcast(F32), qk[rows, 1:4:2, :].bitcast(F32)).then_inc(stacked[s], 16)
                sp.wait_ge(t_stored, FREE_DMA + b * 16)
                sp.dma_start(x2[:, :, :], x_v[b]).then_inc(x_again, 16)
                Q[0].wait_drained(sp, b, ("wo", NBLK - 1))
                sp.dma_start(t_d[b], x2[:, :, :]).then_inc(t_stored, 16)
                Q[1].wait_drained(sp, b, ("rstd", 1))
                sp.dma_start(n_d[b], xw[:, :, 4:4 + N]).then_inc(n_stored, 16)
            sp.wait_ge(t_stored, FREE_DMA + B * 16)
            sp.wait_ge(n_stored, FREE_DMA + B * 16)

        @block.gpsimd
        def _(pool):
            def front(b):
                link = Link(pool, pool_front, b * 10)
                pool.wait_ge(gvar_made, b + 1)
                pool.tensor_tensor(grstd[:, :], gvar[:, :], minus_half[:, 0:CT], ALU.pow).then_inc(grstd_made, 1)
                pool.wait_ge(xn_made, (b + 1) * CT)
                grid = xin[:, :, :].rearrange("p c (y x) -> p c y x", y=H)
                for s, op in enumerate((ALU.add, ALU.subtract)):
                    link.done(pool.tensor_tensor(ysum[:, s].rearrange("p c (y x) -> p c y x", y=HH),
                                                 grid[:, :, 0:HH, :], grid[:, :, H - 1:HH - 1:-1, :], op))
                link.wait()
                pool.wait_ge(xl_made, (b + 1) * CT)
                for s in range(2):
                    rows = ysum[:, s].rearrange("p c (y x) -> p c y x", y=HH)
                    for r, op in enumerate((ALU.add, ALU.subtract)):
                        to = xin[:, :, (2 * s + r) * HH * HW:(2 * s + r + 1) * HH * HW]
                        link.done(pool.tensor_tensor(to.rearrange("p c (y x) -> p c y x", y=HH),
                                                     rows[:, :, :, 0:HW], rows[:, :, :, W - 1:HW - 1:-1], op))
                link.wait()
                pool.sem_inc(fold_made, 1)
                for c in range(CT):
                    for s in range(2):
                        T[s].wait_drained(pool, b, ("diffuse", c, s))
                    plus = ysum[:, c, 0].rearrange("p (r y x) -> p r y x", r=2, y=HH)
                    minus = ysum[:, c, 1].rearrange("p (r y x) -> p r y x", r=2, y=HH)
                    link.done(pool.tensor_tensor(unfold[:, :, 0:HH, :], plus, minus, ALU.add))
                    link.done(pool.tensor_tensor(unfold[:, :, H - 1:HH - 1:-1, :], plus, minus, ALU.subtract))
                    link.wait()
                    if c == 0:
                        pool.wait_ge(mixl_made, FREE + b * 4)
                    to = vd[:, c, :].rearrange("p (y x) -> p y x", y=H)
                    pool.tensor_tensor(to[:, :, 0:HW], unfold[:, 0], unfold[:, 1], ALU.add).then_inc(vd_made, 1)
                    pool.tensor_tensor(to[:, :, W - 1:HW - 1:-1], unfold[:, 0], unfold[:, 1], ALU.subtract).then_inc(vd_made, 1)
                    if c == 0:
                        pool.wait_ge(vd_made, b * 4 + 2)

            def post(b):
                for ln in range(2):
                    Q[0].wait_drained(pool, b, ("var", ln))
                    pool.tensor_tensor(lnr[:, :], lnv[:, :], minus_half[:, :], ALU.pow).then_inc(rstd_made, 1)
                Q[1].wait_drained(pool, b, ("rstd", 1))
                pool.sem_inc(feat_asked, 1)
                pool.dma_start(feat_d, xw[:, :, 4:4 + N], accum_op=ALU.add).then_inc(feat_added, 16)
                pool.wait_ge(feat_added, (b + 1) * 16)
                pool.sem_inc(feat_done, 1)

            for s in [u.free for u in M + T + O + Q] + [mixl_made, fl_made, prob_used, mix_made, rowmax_made, shift_made,
                                                     feat_done]:
                pool.sem_inc(s, FREE)
            for s in stacked + [n_stored, t_stored]:
                pool.sem_inc(s, FREE_DMA)
            with pool.Fori(0, B) as b:
                front(b)
                post(b)

        @block.tensor
        def _(pe):
            def three(out, pairs, n):
                for k, (ah, a_l, bh, bl) in enumerate(pairs):
                    for j, (l, r) in enumerate(((ah, bh), (a_l, bh), (ah, bl))):
                        last = pe.matmul(out, l, r, start=n + k == 0 and j == 0, stop=k == len(pairs) - 1 and j == 2)
                return last

            def project_qk(b, quad):
                for which in range(2):
                    for half in range(2):
                        key = "qk"[which] + f"{quad}h{half}"
                        o = slice(which * C + quad * P, which * C + (quad + 1) * P)
                        n = slice(half * HALF, (half + 1) * HALF)
                        T[half].wait_free(pe, b, key)
                        three(T[half].tile[:, :], [(wh[:, k, o], wl[:, k, o], xh[:, k, n], xl[:, k, n]) for k in range(CT)], 0)\
                            .then_inc(T[half].ready, 1)

            def front(b):
                pe.wait_ge(gstat_made, b + 1)
                M[0].wait_free(pe, b, "gn")
                pe.matmul(M[0].tile[:, 0:2 * CT], group_mean[:, :], gstat[:, :, :].rearrange("p a c -> p (a c)"),
                          start=True, stop=True).then_inc(M[0].ready, 1)
                pe.wait_ge(xl_made, (b + 1) * CT)
                project_qk(b, 0)
                for g in range(4):
                    T[g % 2].wait_free(pe, b, ("v", g))
                    for t in range(2):
                        n = slice((2 * g + t) * P, (2 * g + t + 1) * P)
                        last = three(T[g % 2].tile[:, t * C:(t + 1) * C],
                                     [(xh[:, k, n], xl[:, k, n], wh[:, k, 2 * C:], wl[:, k, 2 * C:]) for k in range(CT)], 0)
                    last.then_inc(T[g % 2].ready, 1)
                pe.wait_ge(fl_made, FREE + (b + 1) * CT)
                for a in range(4):
                    T[a % 2].wait_free(pe, b, ("fold", a))
                    for u in range(FT):
                        n = slice((a * FT + u) * P, (a * FT + u + 1) * P)
                        last = three(T[a % 2].tile[:, u * C:(u + 1) * C],
                                     [(fh[:, k, n], fl[:, k, n], wh[:, k, 2 * C:], wl[:, k, 2 * C:]) for k in range(CT)], 0)
                    last.then_inc(T[a % 2].ready, 1)
                for a in (2, 3):
                    T[a % 2].wait_drained(pe, b, ("fold", a))
                for c in range(CT):
                    for s in range(2):
                        T[s].wait_free(pe, b, ("diffuse", c, s))
                        for r in range(2):
                            a = 2 * s + r
                            last = three(T[s].tile[:, r * HH * HW:(r + 1) * HH * HW],
                                         [(vf[0][:, a, u, c * P:(c + 1) * P], vf[1][:, a, u, c * P:(c + 1) * P],
                                           mh[:, a, u, :], ml[:, a, u, :]) for u in range(FT)], 0)
                        last.then_inc(T[s].ready, 1)

            def row_scores(b, h, t):
                s = h % QUAD
                if t == 0:
                    pe.wait_ge(stacked[s], FREE_DMA + b * 96 + (h // QUAD + 1) * 48)
                for half in range(2):
                    M[half].wait_free(pe, b, ("smax", h, t))
                    pe.matmul(M[half].tile[:, :], stack[s][0:SHIFT, 0, t * P:(t + 1) * P],
                              stack[s][0:SHIFT, 1, half * HALF:(half + 1) * HALF], start=True, stop=True)\
                        .then_inc(M[half].ready, 1)

            def turn(b, h):
                pe.wait_ge(rowmax_made, FREE + b * NH + h + 1)
                M[h % 2].wait_free(pe, b, ("turn", h))
                pe.transpose(M[h % 2].tile[0:16, 0:P], mx2[:, h % 2].rearrange("p a t -> p (a t)"), ident[:, :])\
                    .then_inc(M[h % 2].ready, 1)

            def attend(b, pair, u):
                half, t = unit_of(u)
                for ab in range(2):
                    T[ab].wait_drained(pe, b, ("score", pair, u))
                if t == 0:
                    O[half].wait_free(pe, b, pair)
                for ab in range(2):
                    h = 2 * pair + ab
                    for k, lhs in enumerate((v[:, t, h * HD:(h + 1) * HD], ones[:, 0:HD])):
                        col = (2 * ab + k) * HD
                        last = pe.matmul(O[half].tile[col:col + HD, :], lhs, prob[:, u % 2, ab, :],
                                         start=t == 0, stop=t == NT - 1, tile_position=(0, col))
                last.then_inc(prob_used, 1)

            def heads(b):
                for h in range(2):
                    for t in range(NT):
                        row_scores(b, h, t)
                    turn(b, h)
                for g in (2, 3):
                    T[g % 2].wait_drained(pe, b, ("v", g))
                for pair in range(PAIRS):
                    for u in range(UNITS):
                        if (pair, u) == NEXT_QUAD_AT:
                            project_qk(b, 1)
                        half, t = unit_of(u)
                        for ab in range(2):
                            s = (2 * pair + ab) % QUAD
                            if u == 0:
                                pe.wait_ge(shift_made, FREE + b * NH + 2 * pair + ab + 1)
                            T[ab].wait_free(pe, b, ("score", pair, u))
                            pe.matmul(T[ab].tile[:, :], stack[s][0:STACK, 1, t * P:(t + 1) * P],
                                      stack[s][0:STACK, 0, half * HALF:(half + 1) * HALF], start=True, stop=True)\
                                .then_inc(T[ab].ready, 1)
                        if u:
                            attend(b, pair, u - 1)
                        if pair + 1 < PAIRS:
                            row_scores(b, 2 * pair + 2 + u // NT, u % NT)
                            if u == TURN_AT:
                                turn(b, 2 * pair + 2)
                    attend(b, pair, UNITS - 1)
                    if pair + 1 < PAIRS:
                        turn(b, 2 * pair + 3)

            def post(b):
                for half in range(2):
                    n = slice(half * HALF, (half + 1) * HALF)
                    pe.wait_ge(mixl_made, FREE + (b + 1) * 4)
                    for m in range(CT):
                        o = slice(m * P, (m + 1) * P)
                        Q[m].wait_free(pe, b, ("proj", half))
                        three(Q[m].tile[:, :], [(ph[:, k, o], pl[:, k, o], fh[:, k, n], fl[:, k, n]) for k in range(CT)], 0)\
                            .then_inc(Q[m].ready, 1)
                layer_norm(b, 0)
                for j in range(NBLK):
                    window_block(b, j)
                layer_norm(b, 1)

            def layer_norm(b, ln):
                for half in range(2):
                    if ln == 0:
                        for m in range(CT):
                            Q[m].wait_drained(pe, b, ("proj", half))
                    elif half == 0:
                        Q[0].wait_drained(pe, b, ("wo", NBLK - 1))
                    Q[half].wait_free(pe, b, ("mean", ln))
                    for c in range(CT):
                        last = pe.matmul(Q[half].tile[:, :], mean_c[:, :], x2[:, c, half * HALF:(half + 1) * HALF],
                                         start=c == 0, stop=c == CT - 1)
                    last.then_inc(Q[half].ready, 1)
                pe.wait_ge(sq_made, b * 4 + ln * 2 + 2)
                Q[0].wait_free(pe, b, ("var", ln))
                for t in range(NT):
                    for c in range(CT):
                        last = pe.matmul(Q[0].tile[:, t:t + 1], squares[:, c, t * P:(t + 1) * P], mean_c[:, 0:1],
                                         start=c == 0, stop=c == CT - 1)
                last.then_inc(Q[0].ready, 1)
                pe.wait_ge(diag_made, b * 2 + ln + 1)
                for half in range(2):
                    Q[half].wait_free(pe, b, ("rstd", ln))
                    pe.matmul(Q[half].tile[:, :], ones[:, :], sq[:, half * HALF:(half + 1) * HALF], start=True, stop=True)\
                        .then_inc(Q[half].ready, 1)

            def window_block(b, j):
                nn = block_size(j)
                mm = nn + 2 * WIN
                k0 = j * BLK + 4 - WIN
                if j == 0:
                    for half in range(2):
                        Q[half].wait_drained(pe, b, ("rstd", 0))
                Q[0].wait_free(pe, b, ("kq", j))
                for col, which, start, n in ((0, 1, k0, mm), (2 * P, 0, k0 + WIN, nn)):
                    for m in range(CT):
                        for k in range(CT):
                            last = pe.matmul(Q[0].tile[:, col + m * P:col + m * P + n], w1[:, which, k, m * P:(m + 1) * P],
                                             xw[:, k, start:start + n], start=k == 0, stop=k == CT - 1)
                last.then_inc(Q[0].ready, 1)
                Q[1].wait_free(pe, b, ("wv", j))
                for k in range(CT):
                    last = pe.matmul(Q[1].tile[0:mm, 0:C], xw[:, k, k0:k0 + mm], w1[:, 2, k, :], start=k == 0, stop=k == CT - 1)
                last.then_inc(Q[1].ready, 1)
                Q[0].wait_drained(pe, b, ("kq", j))
                Q[0].wait_free(pe, b, ("ws", j))
                for k in range(CT):
                    last = pe.matmul(Q[0].tile[0:nn, 0:mm], qb[:, k, 0:nn], kb[:, k, 0:mm], start=k == 0, stop=k == CT - 1)
                last.then_inc(Q[0].ready, 1)
                pe.wait_ge(wprob_made, b * NBLK + j + 1)
                Q[1].wait_free(pe, b, ("wt", j))
                pe.transpose(Q[1].tile[0:mm, 0:nn], pm[0:nn, 0:mm], ident[0:nn, 0:nn]).then_inc(Q[1].ready, 1)
                Q[1].wait_drained(pe, b, ("wt", j))
                Q[0].wait_free(pe, b, ("wo", j))
                for m in range(CT):
                    last = pe.matmul(Q[0].tile[:, m * P:m * P + nn], vb[0:mm, m * P:(m + 1) * P], pt[0:mm, 0:nn],
                                     start=True, stop=True)
                last.then_inc(Q[0].ready, 1)

            with pe.Fori(0, B) as b:
                front(b)
                heads(b)
                post(b)

        @block.scalar
        def _(act):
            def qk_hi(b, quad):
                if quad == 1:
                    for s in range(QUAD):
                        act.wait_ge(stacked[s], FREE_DMA + b * 96 + 48)
                else:
                    for s in range(QUAD):
                        act.wait_ge(stacked[s], FREE_DMA + b * 96)
                for which in range(2):
                    for half in range(2):
                        T[half].wait_ready(act, b, "qk"[which] + f"{quad}h{half}")
                        col = 2 * which + quad
                        act.activation(qk[:, 1 + which, half * HALF:(half + 1) * HALF], T[half].tile[:, :], ACT.Identity,
                                       bias=qkb[:, col:col + 1]).then_inc(qkh_made, 1)

            def front(b):
                for c in range(CT):
                    act.wait_ge(xn_made, b * CT + c + 1)
                    act.activation(xh[:, c, :], xin[:, c, :], ACT.Copy).then_inc(xh_made, 1)
                qk_hi(b, 0)
                T[1].wait_ready(act, b, ("v", 3))
                act.wait_ge(fold_made, b + 1)
                for c in range(CT):
                    act.activation(fh[:, c, :], xin[:, c, :], ACT.Copy).then_inc(fh_made, 1)
                for a in range(4):
                    if a == 0:
                        act.wait_ge(mixl_made, FREE + b * 4)
                        act.wait_ge(prob_used, FREE + b * PAIRS * UNITS)
                    T[a % 2].wait_ready(act, b, ("fold", a))
                    act.activation(vf[0][:, a].rearrange("p u o -> p (u o)"), T[a % 2].tile[:, :], ACT.Copy).then_inc(vfh_made, 1)
                for c in range(CT):
                    for s in range(2):
                        T[s].wait_ready(act, b, ("diffuse", c, s))
                        act.activation(ysum[:, c, s], T[s].tile[:, :], ACT.Copy, scale=al[:, 1:2]).then_inc(T[s].free, 1)

            def drain_attended(b, pair, half):
                act.wait_ge(prob_used, FREE + b * PAIRS * UNITS + pair * UNITS + (half + 1) * NT)
                n = slice(half * HALF, (half + 1) * HALF)
                if pair % 2 == 0:
                    act.wait_ge(mix_made, FREE + b * 4 + pair)
                for ab in range(2):
                    to = HD * ((2 * pair + ab) % QUAD)
                    act.activation(att[to:to + HD, n], O[half].tile[2 * ab * HD:(2 * ab + 1) * HD, :], ACT.Copy,
                                   scale=al[2 * ab * HD:(2 * ab + 1) * HD, 0:1])
                    last = act.activation(den[to:to + HD, n], O[half].tile[(2 * ab + 1) * HD:(2 * ab + 2) * HD, :], ACT.Copy)
                last.then_inc(O[half].free, 1)

            def mix_hi(b, quad, half):
                act.wait_ge(mix_made, FREE + b * 4 + quad * 2 + half + 1)
                n = slice(half * HALF, (half + 1) * HALF)
                act.activation(fh[:, quad, n], vd[:, quad, n], ACT.Copy).then_inc(mixh_made, 1)

            def mixes_hi(b, pair, u):
                for k, at in enumerate(MIX_HI_AT):
                    if at == (pair, u):
                        mix_hi(b, k // 2, k % 2)

            def heads(b):
                for pair in range(PAIRS):
                    for u in range(UNITS):
                        if (pair, u) == NEXT_QUAD_AT:
                            qk_hi(b, 1)
                        mixes_hi(b, pair, u)
                        for ab in range(2):
                            T[ab].wait_ready(act, b, ("score", pair, u))
                            n = b * PAIRS * UNITS + pair * UNITS + u
                            if ab == 0:
                                act.wait_ge(prob_used, FREE + (n - 1 if pair or u else n))
                            act.activation(prob[:, u % 2, ab, :], T[ab].tile[:, :], ACT.Exp, scale=HEAD_SCALE)\
                                .then_inc(T[ab].free, 1)
                        if u == DRAIN_AT:
                            drain_attended(b, pair, 0)
                    drain_attended(b, pair, 1)
                mixes_hi(b, PAIRS, 0)

            def post(b):
                layer_norm(b, 0)
                for j in range(NBLK):
                    window_block(b, j)
                layer_norm(b, 1)

            def layer_norm(b, ln):
                for half in range(2):
                    Q[half].wait_drained(act, b, ("mean", ln))
                    n = slice(half * HALF, (half + 1) * HALF)
                    act.activation(squares[:, :, n], xw[:, :, 4 + half * HALF:4 + (half + 1) * HALF], ACT.Square)\
                        .then_inc(sq_made, 1)

            def window_block(b, j):
                nn = block_size(j)
                mm = nn + 2 * WIN
                Q[0].wait_ready(act, b, ("kq", j))
                for col, which, to, n in ((0, 1, kb, mm), (2 * P, 0, qb, nn)):
                    for m in range(CT):
                        last = act.activation(to[:, m, 0:n], Q[0].tile[:, col + m * P:col + m * P + n], ACT.Identity,
                                              bias=wb[:, which, m:m + 1])
                last.then_inc(Q[0].free, 1)
                act.wait_ge(neg_made, b * NBLK + j + 1)
                act.activation(pm[0:nn, 0:mm], sm[0:nn, 0:mm], ACT.Exp, scale=WIN_SCALE, bias=wneg[0:nn, 1:2],
                               accum_out=wden[0:nn, 0:1]).then_inc(wexp_made, 1)
                Q[1].wait_ready(act, b, ("wt", j))
                act.activation(pt[0:mm, 0:nn], Q[1].tile[0:mm, 0:nn], ACT.Copy).then_inc(Q[1].free, 1)

            with act.Fori(0, B) as b:
                front(b)
                heads(b)
                post(b)

        @block.vector
        def _(dve):
            def qk_lo(b, quad):
                for which in range(2):
                    for half in range(2):
                        n = slice(half * HALF, (half + 1) * HALF)
                        dve.wait_ge(qkh_made, b * 8 + quad * 4 + which * 2 + half + 1)
                        col = 2 * which + quad
                        dve.scalar_tensor_tensor(qk[:, 3 * which, n], T[half].tile[:, :], qkb[:, col:col + 1],
                                                 qk[:, 1 + which, n].bitcast(F32), ALU.add, ALU.subtract)\
                            .then_inc(T[half].free, 1)

            def front(b):
                link = Link(dve, dve_front, b * FRONT_LINKS)
                dve.wait_ge(x_landed, (b + 1) * 16)
                for c in range(CT):
                    for half in range(2):
                        link.done(dve.bn_stats(stats[:, c, half, :], xin[:, c, half * HALF:(half + 1) * HALF]))
                link.wait()
                dve.sem_inc(stats_made, 1)
                for c in range(CT):
                    link.done(dve.bn_aggr(aggr[:, c, :], stats[:, c, :, :].rearrange("p h s -> p (h s)")))
                link.wait()
                link.done(dve.tensor_copy(gstat[:, 0, :], aggr[:, :, 0]))
                link.done(dve.tensor_tensor(gtmp[:, 0, :], aggr[:, :, 0], aggr[:, :, 0], ALU.mult))
                link.wait()
                dve.tensor_tensor(gstat[:, 1, :], gtmp[:, 0, :], aggr[:, :, 1], ALU.add).then_inc(gstat_made, 1)
                M[0].wait_ready(dve, b, "gn")
                dve.tensor_copy(gmean[:, :, :], M[0].tile[:, 0:2 * CT].rearrange("p (a c) -> p a c", a=2)).then_inc(M[0].free, 1)
                M[0].wait_drained(dve, b, "gn")
                link.done(dve.tensor_tensor(gtmp[:, 0, :], gmean[:, 0, :], gmean[:, 0, :], ALU.mult))
                link.wait()
                link.done(dve.tensor_tensor(gtmp[:, 1, :], gmean[:, 1, :], gtmp[:, 0, :], ALU.subtract))
                link.wait()
                dve.tensor_scalar(gvar[:, :], gtmp[:, 1, :], 0.0, EPS, ALU.max, ALU.add).then_inc(gvar_made, 1)
                dve.wait_ge(grstd_made, b + 1)
                link.done(dve.scalar_tensor_tensor(gbias[:, :], gmean[:, 0, :], -1.0, grstd[:, :], ALU.mult, ALU.mult))
                link.wait()
                for c in range(CT):
                    dve.tensor_scalar(xin[:, c, :], xin[:, c, :], grstd[:, c:c + 1], gbias[:, c:c + 1], ALU.mult, ALU.add)\
                        .then_inc(xn_made, 1)
                for c in range(CT):
                    dve.wait_ge(xh_made, b * CT + c + 1)
                    dve.tensor_tensor(xl[:, c, :], xin[:, c, :], xh[:, c, :].bitcast(F32), ALU.subtract).then_inc(xl_made, 1)
                qk_lo(b, 0)
                for g in range(4):
                    if g == 0:
                        dve.wait_ge(prob_used, FREE + b * PAIRS * UNITS)
                    T[g % 2].wait_ready(dve, b, ("v", g))
                    dve.tensor_copy(v[:, 2 * g:2 * g + 2, :].rearrange("p t o -> p (t o)"), T[g % 2].tile[:, :])\
                        .then_inc(T[g % 2].free, 1)
                for c in range(CT):
                    dve.wait_ge(fh_made, b * CT + c + 1)
                    dve.tensor_tensor(fl[:, c, :], xin[:, c, :], fh[:, c, :].bitcast(F32), ALU.subtract).then_inc(fl_made, 1)
                for a in range(4):
                    dve.wait_ge(vfh_made, b * 4 + a + 1)
                    dve.tensor_tensor(vf[1][:, a].rearrange("p u o -> p (u o)"), T[a % 2].tile[:, :],
                                      vf[0][:, a].rearrange("p u o -> p (u o)").bitcast(F32), ALU.subtract)\
                        .then_inc(T[a % 2].free, 1)
                assert link.n == FRONT_LINKS, link.n

            def row_max(b, h, t):
                for half in range(2):
                    M[half].wait_ready(dve, b, ("smax", h, t))
                    if t == 0 and half == 0:
                        dve.wait_ge(rowmax_made, FREE + b * NH + h)
                    dve.tensor_reduce(mx[:, h % 2, t, half:half + 1], M[half].tile[:, :], AXX, ALU.max)\
                        .then_inc(M[half].free, 1)
                if t == NT - 1:
                    for half in range(2):
                        M[half].wait_drained(dve, b, ("smax", h, t))
                    both = [mx[:, h % 2, :, half].unsqueeze(1).broadcast_to([P, 2, NT]) for half in range(2)]
                    dve.tensor_tensor(mx2[:, h % 2], both[0], both[1], ALU.max).then_inc(rowmax_made, 1)

            def shift(b, h):
                link = Link(dve, dve_heads, b * HEAD_LINKS + h)
                tile = M[h % 2].tile[0:16, 0:P]
                M[h % 2].wait_ready(dve, b, ("turn", h))
                dve.wait_ge(shift_made, FREE + b * NH + h)
                link.done(dve.tensor_copy(th[:, :], tile))
                link.wait()
                dve.scalar_tensor_tensor(td[:, :], th[:, :].bitcast(F32), low_rows[:, 0:1], tile, ALU.mult, ALU.add)\
                    .then_inc(M[h % 2].free, 1)
                M[h % 2].wait_drained(dve, b, ("turn", h))
                to = stack[h % QUAD][SHIFT:STACK, 0, :].rearrange("p (t n) -> p t n", t=NT)
                dve.tensor_tensor(to, td[:, :].unsqueeze(1).broadcast_to([16, NT, P]),
                                  tile_mask[:, :].unsqueeze(2).broadcast_to([16, NT, P]), ALU.mult).then_inc(shift_made, 1)

            def mix(b, quad, half):
                n = slice(half * HALF, (half + 1) * HALF)
                link = Link(dve, dve_mix, b * 8 + (quad * 2 + half) * 2)
                O[half].wait_drained(dve, b, 2 * quad + 1)
                link.done(dve.reciprocal(den[:, n], den[:, n]))
                link.wait()
                link.done(dve.tensor_tensor(att[:, n], att[:, n], den[:, n], ALU.mult))
                link.wait()
                dve.wait_ge(vd_made, (b + 1) * 4)
                dve.tensor_tensor(vd[:, quad, n], att[:, n], vd[:, quad, n], ALU.add).then_inc(mix_made, 1)

            def mix_lo(b, quad, half):
                n = slice(half * HALF, (half + 1) * HALF)
                dve.wait_ge(mixh_made, b * 4 + quad * 2 + half + 1)
                dve.tensor_tensor(fl[:, quad, n], vd[:, quad, n], fh[:, quad, n].bitcast(F32), ALU.subtract).then_inc(mixl_made, 1)

            def mixes(b, pair, u):
                for k in range(4):
                    if MIX_AT[k] == (pair, u):
                        mix(b, k // 2, k % 2)
                for k in range(4):
                    if MIX_LO_AT[k] == (pair, u):
                        mix_lo(b, k // 2, k % 2)

            def heads(b):
                for h in range(2):
                    for t in range(NT):
                        row_max(b, h, t)
                    shift(b, h)
                for pair in range(PAIRS):
                    for u in range(UNITS):
                        if (pair, u) == NEXT_QUAD_AT:
                            qk_lo(b, 1)
                        mixes(b, pair, u)
                        if pair + 1 < PAIRS:
                            row_max(b, 2 * pair + 2 + u // NT, u % NT)
                            if u == TURN_AT:
                                shift(b, 2 * pair + 2)
                    if pair + 1 < PAIRS:
                        shift(b, 2 * pair + 3)
                mixes(b, PAIRS, 0)

            def post(b):
                for half in range(2):
                    n = slice(half * HALF, (half + 1) * HALF)
                    for m in range(CT):
                        Q[m].wait_ready(dve, b, ("proj", half))
                        if half == 0 and m == 0:
                            dve.wait_ge(x_again, (b + 1) * 16)
                        dve.scalar_tensor_tensor(x2[:, m, n], Q[m].tile[:, :], pb[:, m:m + 1], x2[:, m, n], ALU.add, ALU.add)\
                            .then_inc(Q[m].free, 1)
                layer_norm(b, 0)
                for j in range(NBLK):
                    window_block(b, j)
                layer_norm(b, 1)

            def layer_norm(b, ln):
                for half in range(2):
                    n = slice(half * HALF, (half + 1) * HALF)
                    to = xw[:, :, 4 + half * HALF:4 + (half + 1) * HALF]
                    Q[half].wait_ready(dve, b, ("mean", ln))
                    if ln == 0 and half == 0:
                        dve.wait_ge(n_stored, FREE_DMA + b * 16)
                        dve.wait_ge(feat_done, FREE + b)
                    dve.tensor_tensor(to, x2[:, :, n], Q[half].tile[:, :].unsqueeze(1).broadcast_to([P, CT, HALF]),
                                      ALU.subtract).then_inc(Q[half].free, 1)
                Q[0].wait_ready(dve, b, ("var", ln))
                dve.tensor_scalar(lnv[:, :], Q[0].tile[:, 0:NT], EPS, None, ALU.add).then_inc(Q[0].free, 1)
                dve.wait_ge(rstd_made, b * 2 + ln + 1)
                dve.tensor_tensor(diag, ident[:, :].unsqueeze(1).broadcast_to([P, NT, P]),
                                  lnr[:, :].unsqueeze(2).broadcast_to([P, NT, P]), ALU.mult).then_inc(diag_made, 1)
                for half in range(2):
                    to = xw[:, :, 4 + half * HALF:4 + (half + 1) * HALF]
                    Q[half].wait_ready(dve, b, ("rstd", ln))
                    dve.tensor_tensor(to, to, Q[half].tile[:, :].unsqueeze(1).broadcast_to([P, CT, HALF]), ALU.mult)\
                        .then_inc(Q[half].free, 1)

            def window_block(b, j):
                nn = block_size(j)
                mm = nn + 2 * WIN
                link = Link(dve, dve_post, (b * NBLK + j) * 2)
                kind = 0 if j == 0 else 2 if j == NBLK - 1 else 1
                Q[1].wait_ready(dve, b, ("wv", j))
                dve.tensor_copy(vb[0:mm, :], Q[1].tile[0:mm, 0:C]).then_inc(Q[1].free, 1)
                Q[0].wait_ready(dve, b, ("ws", j))
                dve.tensor_tensor(sm[0:nn, 0:mm], Q[0].tile[0:nn, 0:mm], win_mask[0:nn, kind, 0:mm], ALU.add).then_inc(Q[0].free, 1)
                Q[0].wait_drained(dve, b, ("ws", j))
                link.done(dve.tensor_reduce(wneg[0:nn, 0:1], sm[0:nn, 0:mm], AXX, ALU.max))
                link.wait()
                dve.tensor_scalar(wneg[0:nn, 1:2], wneg[0:nn, 0:1], -WIN_SCALE, None, ALU.mult).then_inc(neg_made, 1)
                dve.wait_ge(wexp_made, b * NBLK + j + 1)
                link.done(dve.reciprocal(wden[0:nn, 1:2], wden[0:nn, 0:1]))
                link.wait()
                dve.tensor_scalar(pm[0:nn, 0:mm], pm[0:nn, 0:mm], wden[0:nn, 1:2], None, ALU.mult).then_inc(wprob_made, 1)
                Q[0].wait_ready(dve, b, ("wo", j))
                n = slice(j * BLK, j * BLK + nn)
                for m in range(CT):
                    last = dve.scalar_tensor_tensor(x2[:, m, n], Q[0].tile[:, m * P:m * P + nn], wb[:, 2, m:m + 1], x2[:, m, n],
                                                    ALU.add, ALU.add)
                last.then_inc(Q[0].free, 1)
                assert link.n == 2

            with dve.Fori(0, B) as b:
                front(b)
                heads(b)
                post(b)


def expert_phase(nc, Wr, br, W, bn, bo, t_d, n_d, feat_d, out):
    out_v = out.rearrange("b (c p) n -> b p c n", p=P)

    with ExitStack() as ctx:
        def sb(name, shape, dt=F32):
            return ctx.enter_context(nc.sbuf_tensor(name, shape, dt))

        def sem(name):
            return ctx.enter_context(nc.semaphore(name))

        wh = sb("expert_w_hi", [P, E, 3, CT, C], F32R)
        wl = sb("expert_w_lo", [P, E, 3, CT, C], F32R)
        gate = sb("gate", [P, E, N])
        gated_bo = sb("gated_output_bias", [P, CT, N])
        xf = sb("x_normed", [P, CT, N])
        xh = sb("x_hi", [P, CT, N], F32R)
        xl = sb("x_lo", [P, CT, N], F32R)
        tok = sb("tokens", [P, CT, N])
        h1h, h1l, h2h, h2l = (sb(k, [P, 2, CT, HALF], F32R) for k in ("h1_hi", "h1_lo", "h2_hi", "h2_lo"))
        z1 = sb("z1", [P, HALF])
        z2 = sb("z2", [P, HALF])
        bnp = sb("norm_params", [P, 2, 5, E, CT])
        scale = sb("norm_scale", [P, 2, E, CT])
        shift = sb("norm_shift", [P, 2, E, CT])
        half_p = sb("minus_half_p", [P, 2, E, CT])
        ident = sb("ident_b", [P, P])
        wr = sb("gate_w", [P, CT, E])
        brb = sb("gate_b", [P, E])
        bos = sb("output_bias", [E, C])
        lg = sb("logits", [P, NT, E])
        red = sb("gate_reduced", [P, 2, NT])
        wT = xf[0:E, 0, :]
        stage = xf[:, :, :].rearrange("p c n -> p (c n)").rearrange("p (r k o) -> p r k o", r=4, k=CT)

        Z1, Z2 = ([ctx.enter_context(nc.psum_tensor(f"z{l}_{m}", [P, HALF], F32)) for m in range(CT)] for l in (1, 2))
        A = [[ctx.enter_context(nc.psum_tensor(f"sum{h}_{m}", [P, HALF], F32)) for m in range(CT)] for h in range(2)]

        in_small, in_feat = sem("in_small"), sem("in_feat")
        in_w = [sem(f"in_w{r}") for r in range(4)]
        w_hi, w_lo = sem("expert_w_hi_made"), sem("expert_w_lo_made")
        ident_made, pow_asked, pow_made = sem("ident_b_made"), sem("pow_asked"), sem("pow_made")
        dve_gate, logits_made, lg_shifted, lg_exp, gate_made = (
            sem(k) for k in ("dve_gate_chain", "logits_made", "lg_shifted", "lg_exp", "gate_made"))
        turned, wT_made, spread, spread_out = (sem(k) for k in ("gate_turned", "wT_made", "gate_spread", "gate_spread_out"))

        NW = 3 * E
        with nc.Block() as block:
            @block.sync
            def _(sp):
                sp.dma_start(tok[:, :, :], feat_d).then_inc(in_feat, 16)
                sp.dma_start(wr[:, :, :], Wr.rearrange("(c p) e -> p c e", p=P)).then_inc(in_small, 16)
                sp.dma_start(brb[:, :], br.partition_broadcast(P)).then_inc(in_small, 16)
                sp.dma_start(bos[:, :], bo).then_inc(in_small, 16)
                sp.dma_start(bnp[:, :, :, :, :], bn).then_inc(in_small, 16)
                for n in range(NW):
                    if n >= 4:
                        sp.wait_ge(w_lo, n - 3)
                    sp.dma_start(stage[:, n % 4], W[n % 3, n // 3].rearrange("(k p) o -> p k o", p=P)).then_inc(in_w[n % 4], 16)

            @block.gpsimd
            def _(pool):
                pool.memset(ident[:, :], 0.0).then_inc(ident_made, 1)
                pool.memset(half_p[:, :, :, :], -0.5).then_inc(ident_made, 1)
                pool.wait_ge(ident_made, 2)
                pool.affine_select(out=ident[:, :], in_=ident[:, :], compare_op=ALU.not_equal, fill=1.0, base=0,
                                   pattern=[[-1, P]], channel_multiplier=1).then_inc(ident_made, 1)
                pool.wait_ge(pow_asked, 1)
                pool.tensor_tensor(scale[:, :, :, :], scale[:, :, :, :], half_p[:, :, :, :], ALU.pow).then_inc(pow_made, 1)

            @block.tensor
            def _(pe):
                pe.wait_ge(in_feat, 16)
                pe.wait_ge(in_small, 4 * 16)
                for t in range(NT):
                    for c in range(CT):
                        last = pe.matmul(Z1[0][:, t * E:(t + 1) * E], tok[:, c, t * P:(t + 1) * P], wr[:, c, :],
                                         start=c == 0, stop=c == CT - 1)
                last.then_inc(logits_made, 1)
                pe.wait_ge(gate_made, 1)
                pe.wait_ge(ident_made, 3)
                for t in range(NT):
                    last = pe.transpose(A[t // 4][0][0:E, (t % 4) * P:(t % 4 + 1) * P], lg[:, t, :], ident[:, :])
                last.then_inc(turned, 1)
                pe.wait_ge(wT_made, 2)
                for n in range(2 * E):
                    e, half = n // 2, n % 2
                    if n >= 2:
                        pe.wait_ge(spread_out, n - 1)
                    pe.matmul(Z2[n % 2][:, :], ident[0:E, e:e + 1].broadcast_to([E, P]), wT[:, half * HALF:(half + 1) * HALF],
                              start=True, stop=True).then_inc(spread, 1)
                for n in range(2 * CT):
                    m, half = n // 2, n % 2
                    pe.wait_ge(spread_out, 2 * E + n - 1)
                    pe.matmul(Z2[n % 2][:, :], bos[:, m * P:(m + 1) * P], wT[:, half * HALF:(half + 1) * HALF],
                              start=True, stop=True).then_inc(spread, 1)

            @block.scalar
            def _(act):
                act.wait_ge(lg_shifted, 1)
                act.activation(lg[:, :, :], lg[:, :, :], ACT.Exp).then_inc(lg_exp, 1)
                for n in range(NW):
                    act.wait_ge(in_w[n % 4], (n // 4 + 1) * 16)
                    act.activation(wh[:, n // 3, n % 3], stage[:, n % 4], ACT.Copy).then_inc(w_hi, 1)

            @block.vector
            def _(dve):
                link = Link(dve, dve_gate, 0)
                dve.wait_ge(in_small, 4 * 16)
                link.done(dve.tensor_scalar(scale[:, :, :, :], bnp[:, :, 4], BN_EPS, None, ALU.add))
                link.wait()
                dve.sem_inc(pow_asked, 1)
                link.done(dve.tensor_tensor(shift[:, :, :, :], bnp[:, :, 0], bnp[:, :, 3], ALU.subtract))
                dve.wait_ge(pow_made, 1)
                link.wait()
                link.done(dve.tensor_tensor(scale[:, :, :, :], scale[:, :, :, :], bnp[:, :, 1], ALU.mult))
                link.wait()
                link.done(dve.tensor_tensor(shift[:, :, :, :], shift[:, :, :, :], scale[:, :, :, :], ALU.mult))
                link.wait()
                link.done(dve.tensor_tensor(shift[:, :, :, :], shift[:, :, :, :], bnp[:, :, 2], ALU.add))
                dve.wait_ge(logits_made, 1)
                link.done(dve.scalar_tensor_tensor(lg[:, :, :], Z1[0][:, 0:NT * E].rearrange("p (t e) -> p t e", e=E), 1.0 / B,
                                                   brb[:, :].unsqueeze(1).broadcast_to([P, NT, E]), ALU.mult, ALU.add))
                link.wait()
                link.done(dve.tensor_reduce(red[:, 0, :], lg[:, :, :], AXX, ALU.max))
                link.wait()
                dve.tensor_tensor(lg[:, :, :], lg[:, :, :], red[:, 0, :].unsqueeze(2).broadcast_to([P, NT, E]), ALU.subtract)\
                    .then_inc(lg_shifted, 1)
                dve.wait_ge(lg_exp, 1)
                link.done(dve.tensor_reduce(red[:, 1, :], lg[:, :, :], AXX, ALU.add))
                link.wait()
                link.done(dve.reciprocal(red[:, 0, :], red[:, 1, :]))
                link.wait()
                dve.tensor_tensor(lg[:, :, :], lg[:, :, :], red[:, 0, :].unsqueeze(2).broadcast_to([P, NT, E]), ALU.mult)\
                    .then_inc(gate_made, 1)
                for n in range(NW):
                    dve.wait_ge(w_hi, n + 1)
                    dve.tensor_tensor(wl[:, n // 3, n % 3], stage[:, n % 4], wh[:, n // 3, n % 3].bitcast(F32), ALU.subtract)\
                        .then_inc(w_lo, 1)
                dve.wait_ge(turned, 1)
                dve.wait_ge(w_lo, NW)
                for half in range(2):
                    dve.tensor_copy(wT[:, half * HALF:(half + 1) * HALF], A[half][0][0:E, :]).then_inc(wT_made, 1)
                for n in range(2 * E + 2 * CT):
                    dve.wait_ge(spread, n + 1)
                    m = n // 2
                    to = gate[:, m] if m < E else gated_bo[:, m - E]
                    dve.tensor_copy(to[:, n % 2 * HALF:(n % 2 + 1) * HALF], Z2[n % 2][:, :]).then_inc(spread_out, 1)

        STEPS = 2 * E
        x_landed, t_landed = sem("x_landed_b"), sem("t_landed_b")
        out_stored = sem("out_stored")
        out_done = sem("out_done")
        xh_made, xl_made = sem("xh_made_b"), sem("xl_made_b")
        z1_ready, z2_ready = sem("z1_ready"), sem("z2_ready")
        z1_made, z2_made = sem("z1_made"), sem("z2_made")
        h1h_made, h1l_made = sem("h1h_made"), sem("h1l_made")
        h2_gated, h2h_made, h2l_made = sem("h2_gated"), sem("h2h_made"), sem("h2l_made")
        sum_ready = sem("sum_ready")
        sum_read = sem("sum_read")
        out_made = sem("out_made")

        block = ctx.enter_context(nc.Block())

        @block.sync
        def _(sp):
            with sp.Fori(0, B) as b:
                sp.wait_ge(xl_made, FREE + b * 2)
                sp.dma_start(xf[:, :, :], n_d[b]).then_inc(x_landed, 16)
                sp.wait_ge(out_done, FREE + b)
                sp.dma_start(tok[:, :, :], t_d[b]).then_inc(t_landed, 16)

        @block.gpsimd
        def _(pool):
            for s in (xl_made, h1h_made, h1l_made, z2_made, sum_read, h2l_made, z1_ready):
                pool.sem_inc(s, FREE)
            pool.sem_inc(out_done, FREE)
            with pool.Fori(0, B) as b:
                for half in range(2):
                    n = slice(half * HALF, (half + 1) * HALF)
                    pool.wait_ge(out_made, b * 2 * CT + (half + 1) * CT)
                    pool.dma_start(out_v[b, :, :, n], tok[:, :, n]).then_inc(out_stored, 16)
                pool.wait_ge(out_stored, (b + 1) * 32)
                pool.sem_inc(out_done, 1)

        @block.tensor
        def _(pe):
            def layer(tile, e, which, m, rh, rl, start, stop):
                o = slice(m * P, (m + 1) * P)
                for k in range(CT):
                    for j, (w, r) in enumerate(((wh, rh), (wl, rh), (wh, rl))):
                        last = pe.matmul(tile[:, :], w[:, e, which, k, o], r[:, k], start=start and k == 0 and j == 0,
                                         stop=stop and k == CT - 1 and j == 2)
                return last

            with pe.Fori(0, B) as b:
                for step in range(STEPS + 2):
                    if step < STEPS:
                        half, e = divmod(step, E)
                        n = slice(half * HALF, (half + 1) * HALF)
                        if e == 0:
                            pe.wait_ge(xl_made, FREE + b * 2 + half + 1)
                        for m in range(CT):
                            pe.wait_ge(h1h_made, FREE + ((b * STEPS + step - 1) * CT + m + 1 if step else b * STEPS * CT))
                            layer(Z1[m], e, 0, m, xh[:, :, n], xl[:, :, n], True, True).then_inc(z1_ready, 1)
                    if 1 <= step <= STEPS:
                        g = step - 1
                        pe.wait_ge(h1l_made, FREE + (b * STEPS + g + 1) * CT)
                        for m in range(CT):
                            pe.wait_ge(z2_made, FREE + ((b * STEPS + g - 1) * CT + m + 1 if g else b * STEPS * CT))
                            layer(Z2[m], g % E, 1, m, h1h[:, g % 2], h1l[:, g % 2], True, True).then_inc(z2_ready, 1)
                    if step >= 2:
                        g = step - 2
                        half, e = divmod(g, E)
                        pe.wait_ge(h2l_made, FREE + (b * STEPS + g + 1) * CT)
                        for m in range(CT):
                            if e == 0:
                                pe.wait_ge(sum_read, FREE + b * 2 * CT)
                            last = layer(A[half][m], e, 2, m, h2h[:, g % 2], h2l[:, g % 2], e == 0, e == E - 1)
                        if e == E - 1:
                            last.then_inc(sum_ready, 1)

        @block.scalar
        def _(act):
            with act.Fori(0, B) as b:
                for step in range(STEPS + 1):
                    if step < STEPS:
                        half, e = divmod(step, E)
                        if e == 0:
                            n = slice(half * HALF, (half + 1) * HALF)
                            if half == 0:
                                act.wait_ge(x_landed, (b + 1) * 16)
                                act.wait_ge(z1_ready, FREE + b * STEPS * CT)
                            act.activation(xh[:, :, n], xf[:, :, n], ACT.Copy).then_inc(xh_made, 1)
                        for m in range(CT):
                            c = (b * STEPS + step) * CT + m
                            act.wait_ge(z1_ready, FREE + c + 1)
                            act.wait_ge(h1l_made, FREE + c)
                            act.activation(z1[:, :], Z1[m][:, :], ACT.Relu, scale=scale[:, 0, e, m:m + 1],
                                           bias=shift[:, 0, e, m:m + 1]).then_inc(z1_made, 1)
                            act.activation(h1h[:, step % 2, m], Z1[m][:, :], ACT.Relu, scale=scale[:, 0, e, m:m + 1],
                                           bias=shift[:, 0, e, m:m + 1]).then_inc(h1h_made, 1)
                    if step:
                        g = step - 1
                        for m in range(CT):
                            c = (b * STEPS + g) * CT + m
                            act.wait_ge(z2_ready, c + 1)
                            act.wait_ge(h2l_made, FREE + c)
                            act.activation(z2[:, :], Z2[m][:, :], ACT.Relu, scale=scale[:, 1, g % E, m:m + 1],
                                           bias=shift[:, 1, g % E, m:m + 1]).then_inc(z2_made, 1)

        @block.vector
        def _(dve):
            def finish(b, half):
                n = slice(half * HALF, (half + 1) * HALF)
                dve.wait_ge(sum_ready, b * 2 + half + 1)
                if half == 0:
                    dve.wait_ge(t_landed, (b + 1) * 16)
                for m in range(CT):
                    dve.tensor_tensor(tok[:, m, n], A[half][m][:, :], tok[:, m, n], ALU.add).then_inc(sum_read, 1)
                    dve.wait_ge(sum_read, FREE + b * 2 * CT + half * CT + m + 1)
                    dve.tensor_tensor(tok[:, m, n], tok[:, m, n], gated_bo[:, m, n], ALU.add).then_inc(out_made, 1)

            with dve.Fori(0, B) as b:
                for step in range(STEPS + 1):
                    if step < STEPS:
                        half, e = divmod(step, E)
                        if e == 0:
                            n = slice(half * HALF, (half + 1) * HALF)
                            dve.wait_ge(xh_made, b * 2 + half + 1)
                            dve.tensor_tensor(xl[:, :, n], xf[:, :, n], xh[:, :, n].bitcast(F32), ALU.subtract)\
                                .then_inc(xl_made, 1)
                        for m in range(CT):
                            dve.wait_ge(h1h_made, FREE + (b * STEPS + step) * CT + m + 1)
                            dve.tensor_tensor(h1l[:, step % 2, m], z1[:, :], h1h[:, step % 2, m].bitcast(F32), ALU.subtract)\
                                .then_inc(h1l_made, 1)
                    if step:
                        g = step - 1
                        half = g // E
                        n = slice(half * HALF, (half + 1) * HALF)
                        for m in range(CT):
                            c = (b * STEPS + g) * CT + m
                            dve.wait_ge(z2_made, FREE + c + 1)
                            dve.tensor_tensor(z2[:, :], z2[:, :], gate[:, g % E, n], ALU.mult).then_inc(h2_gated, 1)
                            dve.wait_ge(h2_gated, c + 1)
                            dve.tensor_copy(h2h[:, g % 2, m], z2[:, :]).then_inc(h2h_made, 1)
                            dve.wait_ge(h2h_made, c + 1)
                            dve.tensor_tensor(h2l[:, g % 2, m], z2[:, :], h2h[:, g % 2, m].bitcast(F32), ALU.subtract)\
                                .then_inc(h2l_made, 1)
                    if step == E + 3:
                        finish(b, 0)
                finish(b, 1)


def diffusion_matrices():
    import numpy as np

    g = np.exp(-np.subtract.outer(np.arange(H), np.arange(H)).astype(np.float64) ** 2 / 2)
    a = np.kron(g, g)
    lap = np.diag(a.sum(1)) - a
    lam = np.linalg.eigvalsh(lap).max()
    hat = 2.0 / lam * lap - np.eye(N)
    cube = hat @ hat @ hat
    eye = np.eye(HH)
    fold = [np.concatenate([eye, s * eye[::-1]]) for s in (1, -1)]
    blocks = [np.kron(fy, fx) for fy in fold for fx in fold]
    return np.stack([f.T @ cube @ f / 16 for f in blocks]).astype(np.float32)


def kernel(**inputs):
    import numpy as np
    import concourse.bacc as bacc
    from concourse.bass_utils import run_bass_kernel_spmd

    i = {k: np.asarray(a) for k, a in inputs.items()}

    def channels(a):
        a = a.reshape(a.shape[:-1] + (-1, P))
        return np.moveaxis(a, -1, 0)

    arrays = {
        "x": i["x"].reshape(B, C, N),
        "qkv_wT": i["L0_conv_qkv_w"].T,
        "qkv_b": channels(i["L0_conv_qkv_b"]),
        "proj_wT": i["L0_conv_proj_w"].T,
        "proj_b": channels(i["L0_conv_proj_b"]),
        "alpha": i["L0_conv_alpha"].reshape(1),
        "window_wT": np.stack([i[f"L1_attn_W{k}"].T for k in "qkv"]),
        "window_b": channels(np.stack([i[f"L1_attn_b{k}"] for k in "qkv"])),
        "diffusion": diffusion_matrices(),
        "Wr": i["L1_ffn_Wr"],
        "br": i["L1_ffn_br"],
        "W": np.stack([i["L1_ffn_W1"], i["L1_ffn_W2"], i["L1_ffn_Wo"]]),
        "bn": channels(np.stack([np.stack([i[f"L1_ffn_{k}{l}"] for k in ("b", "g", "be", "m", "v")]) for l in (1, 2)])),
        "bo": i["L1_ffn_bo"],
    }
    arrays = {k: np.ascontiguousarray(a) for k, a in arrays.items()}
    nc = bacc.Bacc("TRN2", target_bir_lowering=False, num_devices=1)
    a = {k: nc.dram_tensor(k, v.shape, mybir.dt.from_np(v.dtype), kind="ExternalInput").ap() for k, v in arrays.items()}
    out = nc.dram_tensor("out", (B, C, N), F32, kind="ExternalOutput").ap()
    t_d = nc.dram_tensor("tokens_after_attention", (B, P, CT, N), F32, kind="Internal").ap()
    n_d = nc.dram_tensor("tokens_normed", (B, P, CT, N), F32, kind="Internal").ap()
    feat_d = nc.dram_tensor("normed_sum_over_batches", (P, CT, N), F32, kind="Internal").ap()
    attention_phase(nc, a["x"], a["qkv_wT"], a["qkv_b"], a["proj_wT"], a["proj_b"], a["alpha"], a["window_wT"],
                    a["window_b"], a["diffusion"], t_d, n_d, feat_d)
    expert_phase(nc, a["Wr"], a["br"], a["W"], a["bn"], a["bo"], t_d, n_d, feat_d, out)
    r = run_bass_kernel_spmd(nc, [arrays], core_ids=[0])
    return r.results[0]["out"].reshape(B, C, H, W)
```

```python
from contextlib import ExitStack

import concourse.bass as bass
from concourse import mybir

F32 = mybir.dt.float32
F32R = mybir.dt.float32r
ALU = mybir.AluOpType
ACT = mybir.ActivationFunctionType
AXX = mybir.AxisListType.X

P = 128
B, C, H, W = 8, 256, 32, 32
N = H * W
CT = C // P
HALF = N // 2
NH = 8
HD = C // NH
QUAD = P // HD
NT = N // P
PAIRS = NH // 2
UNITS = 2 * NT
SHIFT = 3 * HD
STACK = SHIFT + 16
GROUP = C // 32
HH, HW = H // 2, W // 2
FT = HH * HW // P
WIN = 3
NBLK = -(-N // (P - 2 * WIN))
BLK = -(-N // NBLK)
E = 8
EPS = 1e-5
BN_EPS = 1e-3
HEAD_SCALE = float(HD) ** -0.5
WIN_SCALE = float(C) ** -0.5
ALL_UNITS = PAIRS * UNITS
NEXT_QUAD_AT = 8
TURN_AT = NT + 2
DRAIN_AT = NT + 2
MIX_AT = {UNITS + 13: (0, 0), 2 * UNITS + 3: (0, 1), 3 * UNITS + 13: (1, 0)}
MIX_HI_AT = {2 * UNITS: (0, 0), 2 * UNITS + 9: (0, 1)}
MIX_LO_AT = {2 * UNITS + 4: (0, 0), 2 * UNITS + 13: (0, 1)}
FRONT_TURN_AT = 9
FOLD_AT = {6: 0, 7: 1, 8: 2, 9: 3}
DIFFUSE_AT = {11: (0, 0), 12: (0, 1), 14: (1, 0), 15: (1, 1)}
NORM_AT = 3 * UNITS


def post_stages():
    at = {k: {} for k in ("pe", "act_early", "act", "dve_early", "dve")}

    def put(who, n, stage, j):
        at[who].setdefault(n, []).append((stage, j))

    for ln, n in ((0, 0), (1, 8 + 5 * NBLK + 2)):
        put("pe", n, "mean", ln)
        put("dve_early", n + 1, "deviation", ln)
        put("act", n + 1, "square", ln)
        put("pe", n + 3, "variance", ln)
        put("dve_early", n + 4, "variance", ln)
        put("dve", n + 4, "diagonal", ln)
        put("pe", n + 6, "spread", ln)
        put("dve_early", n + 7, "normed", ln)
    for j in range(NBLK):
        n = 8 + 5 * j
        put("pe", n, "project", j)
        put("act_early", n + 1, "project", j)
        put("dve_early", n + 1, "project", j)
        put("pe", n + 2, "scores", j)
        put("dve_early", n + 3, "mask", j)
        put("act", n + 3, "exp", j)
        put("dve", n + 3, "probs", j)
        put("pe", n + 4, "turn", j)
        put("act_early", n + 5, "turn", j)
        put("pe", n + 5, "values", j)
        put("dve_early", n + 6, "residual", j)
    for who in at:
        for stages in at[who].values():
            stages.sort(key=lambda x: x[1])
        assert max(at[who]) < ALL_UNITS
    return at


POST = post_stages()


FREE, FREE_DMA = 1, 16
FRONT_LINKS = 11
HEAD_LINKS = NH
FAR = -1e30


class Uses:

    def __init__(self, ready, free, tile, keys):
        self.ready, self.free, self.tile = ready, free, tile
        self.at = {k: n for n, k in enumerate(keys)}
        self.per = len(keys)

    def wait_free(self, eng, b, key):
        eng.wait_ge(self.free, b * self.per + self.at[key] + 1)

    def wait_ready(self, eng, b, key):
        eng.wait_ge(self.ready, b * self.per + self.at[key] + 1)

    def wait_drained(self, eng, b, key):
        eng.wait_ge(self.free, b * self.per + self.at[key] + 2)


class Link:

    def __init__(self, eng, sem, base):
        self.eng, self.sem, self.base, self.n = eng, sem, base, 0

    def done(self, ins):
        self.n += 1
        ins.then_inc(self.sem, 1)

    def wait(self):
        self.eng.wait_ge(self.sem, self.base + self.n)



def attention_phase(nc, x, qkv_wT, qkv_b, proj_wT, proj_b, alpha, window_wT, window_b,
                    diffusion, t_d, n_d, feat_d):
    x_v = x.rearrange("b (c p) n -> b p c n", p=P)

    with ExitStack() as ctx:
        def sb(name, shape, dt=F32):
            return ctx.enter_context(nc.sbuf_tensor(name, shape, dt))

        def sem(name):
            return ctx.enter_context(nc.semaphore(name))

        ident = sb("ident", [P, P])
        ones = sb("ones", [P, P])
        mean_c = sb("mean_c", [P, P])
        group_mean = sb("group_mean", [P, P])
        minus_half = sb("minus_half", [P, NT])
        win_mask = sb("win_mask", [P, 3, P])
        tile_mask = sb("tile_mask", [16, NT])
        low_rows = sb("low_rows", [16, 1])
        wh = sb("qkv_w_hi", [P, CT, 3 * C], F32R)
        wl = sb("qkv_w_lo", [P, CT, 3 * C], F32R)
        ph = sb("proj_w_hi", [P, CT, C], F32R)
        pl = sb("proj_w_lo", [P, CT, C], F32R)
        mh = sb("diffusion_hi", [P, 4, FT, HH * HW], F32R)
        ml = sb("diffusion_lo", [P, 4, FT, HH * HW], F32R)
        w1 = sb("window_w", [P, 3, CT, C])
        qkb = sb("qkv_bias", [P, 6])
        pb = sb("proj_bias", [P, CT])
        vcol = sb("v_bias_scaled", [P, CT])
        wb = sb("window_bias", [P, 3, CT])
        al = sb("alphas", [P, 3])

        xin = sb("xin", [P, CT, N])
        stats = sb("stats", [P, CT, 2, 6])
        aggr = sb("aggr", [P, CT, 2])
        gstat = sb("gstat", [P, 2, CT])
        gmean = sb("gmean", [P, 2, CT])
        gtmp = sb("gtmp", [P, 2, CT])
        gvar = sb("gvar", [P, CT])
        grstd = sb("grstd", [P, CT])
        gbias = sb("gbias", [P, CT])
        xh = sb("xn_hi", [P, CT, N], F32R)
        xl = sb("xn_lo", [P, CT, N], F32R)
        ysum = sb("y_folded_or_parities", [P, 2, CT, N // 2])
        fh = sb("fold_or_mix_hi", [P, CT, N], F32R)
        fl = sb("fold_or_mix_lo", [P, CT, N], F32R)
        qk = sb("qk_parts", [P, 4, N], F32R)
        stack = [sb(f"stack{s}", [P, 2, N], F32R) for s in range(QUAD)]
        v = sb("v", [P, NT, C])
        unfold = sb("unfolded_y", [P, 2, H, HW])
        vd = sb("v_diffused", [P, CT, N])
        mx = sb("row_max", [P, 2, NT, 2])
        mx2 = sb("row_max_twice", [P, 2, 2, NT])
        th = sb("shift_hi", [16, P], F32R)
        td = sb("shift_parts", [16, P])
        at0 = -(-nc.sbuf_base // 32) * 32
        sb("room", [P, 4 * N])
        vf = [nc.alloc_sbuf_tensor_at(f"v_folded_{s}", [P, 4, FT, C], F32R, offset=at0 + k * 8192)
              for k, s in enumerate(("hi", "lo"))]
        prob = nc.alloc_sbuf_tensor_at("prob", [P, 2, 2, HALF], F32, offset=at0)
        att = nc.alloc_sbuf_tensor_at("attended", [P, N], F32, offset=at0 + 8192)
        den = nc.alloc_sbuf_tensor_at("denominators", [P, N], F32, offset=at0 + 12288)

        x2 = sb("x2", [P, CT, N])
        xw = sb("xn_padded", [P, CT, N + 8])
        sq = sb("squares_or_block", [P, CT * N])
        lnv = sb("ln_var", [P, NT])
        lnr = sb("ln_rstd", [P, NT])
        wneg = sb("win_minus_max", [P, 2])
        wden = sb("win_den", [P, 2])
        squares = sq[:, :].rearrange("p (c n) -> p c n", c=CT)
        diag = sq[:, 0:NT * P].rearrange("p (t n) -> p t n", t=NT)
        kb = sq[:, 0:256].rearrange("p (m n) -> p m n", m=CT)
        qb = sq[:, 256:512].rearrange("p (m n) -> p m n", m=CT)
        vb = sq[:, 512:768]
        sm = sq[:, 768:896]
        pm = sq[:, 896:1024]
        pt = sq[:, 1024:1152]

        bank = [ctx.enter_context(nc.psum_tensor(f"bank{k}", [P, HALF], F32)) for k in range(8)]

        def split_store(eng, hi, lo, src, s_hi, n):
            eng.tensor_copy(hi, src).then_inc(s_hi, 1)
            eng.wait_ge(s_hi, n)
            return eng.tensor_tensor(lo, src, hi.bitcast(F32), ALU.subtract)

        s_in = {k: sem(f"in_{k}") for k in ("w", "p", "m", "b", "mid")}
        s_made, s_hi, s_lo, s_al, s_vb, s_pbp, s_zero, s_fz = (
            sem(k) for k in ("const_made", "w_hi", "w_lo", "alpha_made", "vbias_made",
                             "pbias_ready", "feat_zero", "feat_zeroed"))
        with nc.Block() as block:
            @block.sync
            def _(sp):
                sp.dma_start(squares[:, :, 0:3 * C], qkv_wT.rearrange("(c p) o -> p c o", p=P)).then_inc(s_in["w"], 16)
                sp.dma_start(vd[:, :, 0:C], proj_wT.rearrange("(c p) o -> p c o", p=P)).then_inc(s_in["p"], 16)
                sp.dma_start(x2[:, :, :].rearrange("p c n -> p (c n)").rearrange("p (a u m) -> p a u m", a=4, u=FT),
                             diffusion.rearrange("a (u p) m -> p a u m", p=P)).then_inc(s_in["m"], 16)
                sp.dma_start(w1[:, :, :, :], window_wT.rearrange("a (c p) o -> p a c o", p=P)).then_inc(s_in["b"], 16)
                sp.dma_start(qkb[:, :], qkv_b).then_inc(s_in["b"], 16)
                sp.dma_start(pb[:, :], proj_b).then_inc(s_in["b"], 16)
                sp.dma_start(wb[:, :, :], window_b).then_inc(s_in["b"], 16)
                sp.dma_start(al[:, 0:1], alpha.partition_broadcast(P)).then_inc(s_in["b"], 16)
                sp.wait_ge(s_zero, 1)
                sp.dma_start(feat_d, xin[:, :, :]).then_inc(s_fz, 16)
                sp.wait_ge(s_fz, 16)

            @block.gpsimd
            def _(pool):
                link = Link(pool, s_made, 0)
                link.done(pool.memset(xin[:, :, :], 0.0))
                link.done(pool.memset(ones[:, :], 1.0))
                link.done(pool.memset(ident[:, :], 0.0))
                link.done(pool.memset(mean_c[:, :], 1.0 / C))
                link.done(pool.memset(group_mean[:, :], 1.0 / GROUP))
                link.done(pool.memset(minus_half[:, :], -0.5))
                link.done(pool.memset(win_mask[:, :, :], 0.0))
                link.done(pool.memset(tile_mask[:, :], 0.0))
                link.done(pool.memset(low_rows[:, :], 0.0))
                link.done(pool.memset(xw[:, :, :], 0.0))
                link.wait()
                pool.sem_inc(s_zero, 1)

                def cut(ap, cmp, fill, base, pattern, mult):
                    link.done(pool.affine_select(out=ap, in_=ap, compare_op=cmp, fill=fill, base=base,
                                                 pattern=pattern, channel_multiplier=mult))
                    link.wait()

                cut(ident[:, :], ALU.not_equal, 1.0, 0, [[-1, P]], 1)
                gm = group_mean[:, :].rearrange("p (g k) -> p g k", k=GROUP)
                cut(gm, ALU.is_ge, 0.0, 0, [[-GROUP, P // GROUP], [0, GROUP]], 1)
                cut(gm, ALU.is_ge, 0.0, GROUP - 1, [[GROUP, P // GROUP], [0, GROUP]], -1)
                wm = win_mask[:, :, :]
                cut(wm, ALU.is_ge, FAR, 0, [[0, 3], [1, P]], -1)
                cut(wm, ALU.is_ge, FAR, 2 * WIN, [[0, 3], [-1, P]], 1)
                cut(win_mask[:, 0, :], ALU.is_ge, FAR, -WIN, [[1, P]], 0)
                cut(win_mask[:, 2, :], ALU.is_ge, FAR, N - (NBLK - 1) * BLK + WIN - 1, [[-1, P]], 0)
                cut(tile_mask[:, :], ALU.not_equal, -1.0, 0, [[-1, NT]], 1)
                cut(tile_mask[:, :], ALU.not_equal, -1.0, -NT, [[-1, NT]], 1)
                cut(low_rows[:, :], ALU.is_ge, -1.0, NT - 1, [[0, 1]], -1)

            @block.vector
            def _(dve):
                link = Link(dve, s_hi, 0)
                for name, hi, lo, src in (
                        ("w", wh[:, :, :], wl[:, :, :], squares[:, :, 0:3 * C]),
                        ("p", ph[:, :, :], pl[:, :, :], vd[:, :, 0:C]),
                        ("m", mh[:, :, :, :], ml[:, :, :, :],
                         x2[:, :, :].rearrange("p c n -> p (c n)").rearrange("p (a u m) -> p a u m", a=4, u=FT))):
                    dve.wait_ge(s_in[name], 16)
                    link.done(dve.tensor_copy(hi, src))
                    link.wait()
                    dve.tensor_tensor(lo, src, hi.bitcast(F32), ALU.subtract).then_inc(s_lo, 1)
                dve.wait_ge(s_in["b"], 5 * 16)
                dve.tensor_scalar(al[:, 1:2], al[:, 0:1], -1.0, 1.0, ALU.mult, ALU.add).then_inc(s_al, 1)
                dve.tensor_scalar(al[:, 2:3], al[:, 0:1], 2.0, -1.0, ALU.mult, ALU.add).then_inc(s_al, 1)
                dve.wait_ge(s_al, 2)
                dve.tensor_scalar(vcol[:, :], qkb[:, 4:6], al[:, 2:3], None, ALU.mult).then_inc(s_vb, 1)
                dve.wait_ge(s_pbp, 1)
                dve.tensor_tensor(pb[:, :], bank[0][:, 0:CT], pb[:, :], ALU.add).then_inc(s_al, 1)
                dve.wait_ge(s_made, 2)
                for s in range(QUAD):
                    for h in range(NT):
                        link.done(dve.tensor_copy(stack[s][SHIFT:P, 1, h * P:(h + 1) * P], ones[SHIFT:P, :]))

            @block.tensor
            def _(pe):
                pe.wait_ge(s_vb, 1)
                pe.wait_ge(s_in["p"], 16)
                for m in range(CT):
                    for k in range(CT):
                        last = pe.matmul(bank[0][:, m:m + 1], vd[:, k, m * P:(m + 1) * P], vcol[:, k:k + 1],
                                         start=k == 0, stop=k == CT - 1)
                last.then_inc(s_pbp, 1)

        def smax_keys():
            keys = (["gn"], [])

            def rows(h, t):
                for half in range(2):
                    keys[half].append(("smax", h, t))

            for n in range(2 * NT):
                rows(n // NT, n % NT)
                if n == FRONT_TURN_AT:
                    keys[0].append(("turn", 0))
            keys[1].append(("turn", 1))
            for pair in range(PAIRS - 1):
                for u in range(UNITS):
                    rows(2 * pair + 2 + u // NT, u % NT)
                    if u == TURN_AT:
                        keys[0].append(("turn", 2 * pair + 2))
                keys[1].append(("turn", 2 * pair + 3))
            return keys

        def score_keys():
            keys = (["q0h0", "k0h0"], ["q0h1", "k0h1"])
            for g in range(4):
                keys[g % 2].append(("v", g))
            for n in range(2 * NT):
                if n in FOLD_AT:
                    keys[FOLD_AT[n] % 2].append(("fold", FOLD_AT[n]))
                if n in DIFFUSE_AT:
                    keys[DIFFUSE_AT[n][1]].append(("diffuse", *DIFFUSE_AT[n]))
            for n in range(ALL_UNITS):
                if n == NEXT_QUAD_AT:
                    for half in range(2):
                        keys[half].extend([f"q1h{half}", f"k1h{half}"])
                for ab in range(2):
                    keys[ab].append(("score", n // UNITS, n % UNITS))
            return keys

        def post_keys():
            keys = [[("proj", half) for half in range(2)] for m in range(CT)]
            for n in sorted(POST["pe"]):
                for stage, j in POST["pe"][n]:
                    if stage in ("mean", "spread"):
                        for half in range(2):
                            keys[half].append((stage, j))
                    elif stage == "project":
                        keys[0].append(("kq", j))
                        keys[1].append(("wv", j))
                    elif stage == "turn":
                        keys[1].append(("wt", j))
                    else:
                        keys[0].append(({"variance": "var", "scores": "ws", "values": "wo"}[stage], j))
            return keys

        def ring(name, first, keys):
            return [Uses(sem(f"{name}{k}_ready"), sem(f"{name}{k}_free"), bank[first + k], keys[k]) for k in range(2)]

        M = ring("max", 0, smax_keys())
        T = ring("score", 2, score_keys())
        O = ring("attend", 4, [list(range(PAIRS))] * 2)
        Q = ring("post", 6, post_keys())

        x_landed = sem("x_landed")
        stats_made = sem("stats_made")
        feat_asked = sem("feat_asked")
        gstat_made = sem("gstat_made")
        gvar_made = sem("gvar_made")
        grstd_made = sem("grstd_made")
        xn_made = sem("xn_made")
        xh_made = sem("xh_made")
        xl_made = sem("xl_made")
        fold_made = sem("fold_made")
        fh_made = sem("fh_made")
        fl_made = sem("fl_made")
        qkh_made = sem("qkh_made")
        stacked = [sem(f"stacked{s}") for s in range(QUAD)]
        vfh_made = sem("vfh_made")
        vd_made = sem("vd_made")
        rowmax_made = sem("rowmax_made")
        shift_made = sem("shift_made")
        prob_used = sem("prob_used")
        mix_made = sem("mix_made")
        mixh_made = sem("mixh_made")
        mixl_made = sem("mixl_made")
        x_again = sem("x_again")
        sq_made = sem("sq_made")
        rstd_made = sem("rstd_made")
        diag_made = sem("diag_made")
        neg_made = sem("neg_made")
        win_max_made = sem("win_max_made")
        win_den_made = sem("win_den_made")
        wexp_made = sem("wexp_made")
        wprob_made = sem("wprob_made")
        t_stored = sem("t_stored")
        n_stored = sem("n_stored")
        feat_added = sem("feat_added")
        feat_done = sem("feat_done")
        dve_front, dve_heads, dve_mix = (sem(f"dve_{k}_chain") for k in ("norm", "shift", "mix"))
        rows_folded = sem("rows_folded")
        pool_unfold = sem("pool_unfold_chain")

        def unit_of(u):
            return u // NT, u % NT

        def block_size(j):
            return min(BLK, N - j * BLK)

        block = ctx.enter_context(nc.Block())

        @block.sync
        def _(sp):
            def load(b):
                sp.dma_start(xin[:, :, :], x_v[b]).then_inc(x_landed, 16)

            def turn(b, post, ahead):
                for quad in range(2):
                    for s in range(QUAD):
                        rows = slice(HD * s, HD * (s + 1))
                        if quad == 0 and s == 0:
                            T[1].wait_drained(sp, b, "k0h1")
                        elif quad == 1 and s % 2 == 0:
                            T[1].wait_drained(sp, b, ("score", s // 2, UNITS - 1))
                        for to, parts in ((0, slice(1, 3)), (1, slice(0, 3, 2)), (2, slice(1, 4, 2))):
                            sp.dma_start(stack[s][to * HD:(to + 1) * HD, :, :].bitcast(F32), qk[rows, parts, :].bitcast(F32))\
                                .then_inc(stacked[s], 16)
                    if quad == 0 and ahead:
                        sp.wait_ge(fl_made, FREE + (b + 1) * CT)
                        load(b + 1)
                if post:
                    Q[0].wait_drained(sp, b - 1, ("wo", NBLK - 1))
                    sp.dma_start(t_d[b - 1], x2[:, :, :]).then_inc(t_stored, 16)
                    Q[1].wait_drained(sp, b - 1, ("spread", 1))
                    sp.dma_start(n_d[b - 1], xw[:, :, 4:4 + N]).then_inc(n_stored, 16)
                    sp.wait_ge(t_stored, FREE_DMA + b * 16)
                sp.dma_start(x2[:, :, :], x_v[b]).then_inc(x_again, 16)

            load(0)
            turn(0, False, True)
            with sp.Fori(1, B - 1) as b:
                turn(b, True, True)
            turn(B - 1, True, False)
            Q[0].wait_drained(sp, B - 1, ("wo", NBLK - 1))
            sp.dma_start(t_d[B - 1], x2[:, :, :]).then_inc(t_stored, 16)
            Q[1].wait_drained(sp, B - 1, ("spread", 1))
            sp.dma_start(n_d[B - 1], xw[:, :, 4:4 + N]).then_inc(n_stored, 16)
            sp.wait_ge(t_stored, FREE_DMA + B * 16)
            sp.wait_ge(n_stored, FREE_DMA + B * 16)

        @block.gpsimd
        def _(pool):
            def norm_power(b):
                pool.wait_ge(gvar_made, b + 1)
                pool.tensor_tensor(grstd[:, :], gvar[:, :], minus_half[:, 0:CT], ALU.pow).then_inc(grstd_made, 1)

            def fold_rows(b):
                pool.wait_ge(xn_made, (b + 1) * CT)
                grid = xin[:, :, :].rearrange("p c (y x) -> p c y x", y=H)
                for s, op in enumerate((ALU.add, ALU.subtract)):
                    pool.tensor_tensor(ysum[:, s].rearrange("p c (y x) -> p c y x", y=HH),
                                       grid[:, :, 0:HH, :], grid[:, :, H - 1:HH - 1:-1, :], op).then_inc(rows_folded, 1)

            def fold_columns(b):
                pool.wait_ge(rows_folded, (b + 1) * 2)
                pool.wait_ge(xl_made, (b + 1) * CT)
                for s in range(2):
                    rows = ysum[:, s].rearrange("p c (y x) -> p c y x", y=HH)
                    for r, op in enumerate((ALU.add, ALU.subtract)):
                        to = xin[:, :, (2 * s + r) * HH * HW:(2 * s + r + 1) * HH * HW]
                        pool.tensor_tensor(to.rearrange("p c (y x) -> p c y x", y=HH),
                                           rows[:, :, :, 0:HW], rows[:, :, :, W - 1:HW - 1:-1], op).then_inc(fold_made, 1)

            def unfold_diffused(b):
                link = Link(pool, pool_unfold, b * 4)
                for c in range(CT):
                    for s in range(2):
                        T[s].wait_drained(pool, b, ("diffuse", c, s))
                    plus = ysum[:, c, 0].rearrange("p (r y x) -> p r y x", r=2, y=HH)
                    minus = ysum[:, c, 1].rearrange("p (r y x) -> p r y x", r=2, y=HH)
                    link.done(pool.tensor_tensor(unfold[:, :, 0:HH, :], plus, minus, ALU.add))
                    link.done(pool.tensor_tensor(unfold[:, :, H - 1:HH - 1:-1, :], plus, minus, ALU.subtract))
                    link.wait()
                    if c == 0:
                        pool.wait_ge(mixl_made, FREE + b * 4)
                    to = vd[:, c, :].rearrange("p (y x) -> p y x", y=H)
                    pool.tensor_tensor(to[:, :, 0:HW], unfold[:, 0], unfold[:, 1], ALU.add).then_inc(vd_made, 1)
                    pool.tensor_tensor(to[:, :, W - 1:HW - 1:-1], unfold[:, 0], unfold[:, 1], ALU.subtract).then_inc(vd_made, 1)
                    if c == 0:
                        pool.wait_ge(vd_made, b * 4 + 2)

            def layer_norm_power(b, ln):
                Q[0].wait_drained(pool, b, ("var", ln))
                pool.tensor_tensor(lnr[:, :], lnv[:, :], minus_half[:, :], ALU.pow).then_inc(rstd_made, 1)

            def sum_normed(b):
                Q[1].wait_drained(pool, b, ("spread", 1))
                pool.sem_inc(feat_asked, 1)
                pool.dma_start(feat_d, xw[:, :, 4:4 + N], accum_op=ALU.add).then_inc(feat_added, 16)
                pool.wait_ge(feat_added, (b + 1) * 16)
                pool.sem_inc(feat_done, 1)

            def turn(b, post, ahead):
                unfold_diffused(b)
                if post:
                    layer_norm_power(b - 1, 0)
                if ahead:
                    norm_power(b + 1)
                    fold_rows(b + 1)
                if post:
                    layer_norm_power(b - 1, 1)
                if ahead:
                    fold_columns(b + 1)
                if post:
                    sum_normed(b - 1)

            for s in [u.free for u in M + T + O + Q] + [mixl_made, fl_made, prob_used, mix_made, rowmax_made, shift_made,
                                                     feat_done]:
                pool.sem_inc(s, FREE)
            for s in stacked + [n_stored, t_stored]:
                pool.sem_inc(s, FREE_DMA)
            norm_power(0)
            fold_rows(0)
            fold_columns(0)
            turn(0, False, True)
            with pool.Fori(1, B - 1) as b:
                turn(b, True, True)
            turn(B - 1, True, False)
            layer_norm_power(B - 1, 0)
            layer_norm_power(B - 1, 1)
            sum_normed(B - 1)

        @block.tensor
        def _(pe):
            def three(out, pairs, n):
                for k, (ah, a_l, bh, bl) in enumerate(pairs):
                    for j, (l, r) in enumerate(((ah, bh), (a_l, bh), (ah, bl))):
                        last = pe.matmul(out, l, r, start=n + k == 0 and j == 0, stop=k == len(pairs) - 1 and j == 2)
                return last

            def project_qk(b, quad):
                if quad == 0:
                    pe.wait_ge(xl_made, (b + 1) * CT)
                for which in range(2):
                    for half in range(2):
                        key = "qk"[which] + f"{quad}h{half}"
                        o = slice(which * C + quad * P, which * C + (quad + 1) * P)
                        n = slice(half * HALF, (half + 1) * HALF)
                        T[half].wait_free(pe, b, key)
                        three(T[half].tile[:, :], [(wh[:, k, o], wl[:, k, o], xh[:, k, n], xl[:, k, n]) for k in range(CT)], 0)\
                            .then_inc(T[half].ready, 1)

            def group_means(b):
                pe.wait_ge(gstat_made, b + 1)
                M[0].wait_free(pe, b, "gn")
                pe.matmul(M[0].tile[:, 0:2 * CT], group_mean[:, :], gstat[:, :, :].rearrange("p a c -> p (a c)"),
                          start=True, stop=True).then_inc(M[0].ready, 1)

            def project_v(b):
                for g in range(4):
                    T[g % 2].wait_free(pe, b, ("v", g))
                    for t in range(2):
                        n = slice((2 * g + t) * P, (2 * g + t + 1) * P)
                        last = three(T[g % 2].tile[:, t * C:(t + 1) * C],
                                     [(xh[:, k, n], xl[:, k, n], wh[:, k, 2 * C:], wl[:, k, 2 * C:]) for k in range(CT)], 0)
                    last.then_inc(T[g % 2].ready, 1)

            def project_fold(b, a):
                if a == 0:
                    pe.wait_ge(fl_made, FREE + (b + 1) * CT)
                T[a % 2].wait_free(pe, b, ("fold", a))
                for u in range(FT):
                    n = slice((a * FT + u) * P, (a * FT + u + 1) * P)
                    last = three(T[a % 2].tile[:, u * C:(u + 1) * C],
                                 [(fh[:, k, n], fl[:, k, n], wh[:, k, 2 * C:], wl[:, k, 2 * C:]) for k in range(CT)], 0)
                last.then_inc(T[a % 2].ready, 1)

            def diffuse(b, c, s):
                if c == 0 and s == 0:
                    for a in (2, 3):
                        T[a % 2].wait_drained(pe, b, ("fold", a))
                T[s].wait_free(pe, b, ("diffuse", c, s))
                for r in range(2):
                    a = 2 * s + r
                    last = three(T[s].tile[:, r * HH * HW:(r + 1) * HH * HW],
                                 [(vf[0][:, a, u, c * P:(c + 1) * P], vf[1][:, a, u, c * P:(c + 1) * P],
                                   mh[:, a, u, :], ml[:, a, u, :]) for u in range(FT)], 0)
                last.then_inc(T[s].ready, 1)

            def row_scores(b, h, t):
                s = h % QUAD
                if t == 0:
                    pe.wait_ge(stacked[s], FREE_DMA + b * 96 + (h // QUAD + 1) * 48)
                for half in range(2):
                    M[half].wait_free(pe, b, ("smax", h, t))
                    pe.matmul(M[half].tile[:, :], stack[s][0:SHIFT, 0, t * P:(t + 1) * P],
                              stack[s][0:SHIFT, 1, half * HALF:(half + 1) * HALF], start=True, stop=True)\
                        .then_inc(M[half].ready, 1)

            def turn(b, h):
                pe.wait_ge(rowmax_made, FREE + b * NH + h + 1)
                M[h % 2].wait_free(pe, b, ("turn", h))
                pe.transpose(M[h % 2].tile[0:16, 0:P], mx2[:, h % 2].rearrange("p a t -> p (a t)"), ident[:, :])\
                    .then_inc(M[h % 2].ready, 1)

            def attend(b, pair, u):
                half, t = unit_of(u)
                for ab in range(2):
                    T[ab].wait_drained(pe, b, ("score", pair, u))
                if t == 0:
                    O[half].wait_free(pe, b, pair)
                for ab in range(2):
                    h = 2 * pair + ab
                    for k, lhs in enumerate((v[:, t, h * HD:(h + 1) * HD], ones[:, 0:HD])):
                        col = (2 * ab + k) * HD
                        last = pe.matmul(O[half].tile[col:col + HD, :], lhs, prob[:, u % 2, ab, :],
                                         start=t == 0, stop=t == NT - 1, tile_position=(0, col))
                last.then_inc(prob_used, 1)

            def project_mix(b):
                pe.wait_ge(mixl_made, FREE + (b + 1) * 4)
                for half in range(2):
                    n = slice(half * HALF, (half + 1) * HALF)
                    for m in range(CT):
                        o = slice(m * P, (m + 1) * P)
                        Q[m].wait_free(pe, b, ("proj", half))
                        three(Q[m].tile[:, :], [(ph[:, k, o], pl[:, k, o], fh[:, k, n], fl[:, k, n]) for k in range(CT)], 0)\
                            .then_inc(Q[m].ready, 1)

            def scores(b, pair, u):
                half, t = unit_of(u)
                for ab in range(2):
                    s = (2 * pair + ab) % QUAD
                    if u == 0:
                        pe.wait_ge(shift_made, FREE + b * NH + 2 * pair + ab + 1)
                    T[ab].wait_free(pe, b, ("score", pair, u))
                    pe.matmul(T[ab].tile[:, :], stack[s][0:STACK, 1, t * P:(t + 1) * P],
                              stack[s][0:STACK, 0, half * HALF:(half + 1) * HALF], start=True, stop=True)\
                        .then_inc(T[ab].ready, 1)

            def post(b, n):
                for stage, j in POST["pe"].get(n, []):
                    {"mean": mean, "variance": variance, "spread": spread, "project": window_project,
                     "scores": window_scores, "turn": window_turn, "values": window_values}[stage](b, j)

            def turn_of_loop(b, with_post, ahead):
                project_qk(b, 0)
                project_v(b)
                if with_post:
                    project_mix(b - 1)
                for n in range(2 * NT):
                    row_scores(b, n // NT, n % NT)
                    if n == FRONT_TURN_AT:
                        turn(b, 0)
                    if n in FOLD_AT:
                        project_fold(b, FOLD_AT[n])
                    if n == 2 * NT - 1:
                        turn(b, 1)
                    if n in DIFFUSE_AT:
                        diffuse(b, *DIFFUSE_AT[n])
                for g in (2, 3):
                    T[g % 2].wait_drained(pe, b, ("v", g))
                for n in range(ALL_UNITS):
                    pair, u = divmod(n, UNITS)
                    if n == NEXT_QUAD_AT:
                        project_qk(b, 1)
                    scores(b, pair, u)
                    if u:
                        attend(b, pair, u - 1)
                    if pair + 1 < PAIRS:
                        row_scores(b, 2 * pair + 2 + u // NT, u % NT)
                        if u == TURN_AT:
                            turn(b, 2 * pair + 2)
                    if n == NORM_AT + 2 and ahead:
                        group_means(b + 1)
                    if with_post:
                        post(b - 1, n)
                    if u == UNITS - 1:
                        attend(b, pair, u)
                        if pair + 1 < PAIRS:
                            turn(b, 2 * pair + 3)

            def mean(b, ln):
                for half in range(2):
                    if ln == 0:
                        for m in range(CT):
                            Q[m].wait_drained(pe, b, ("proj", half))
                    elif half == 0:
                        Q[0].wait_drained(pe, b, ("wo", NBLK - 1))
                    Q[half].wait_free(pe, b, ("mean", ln))
                    for c in range(CT):
                        last = pe.matmul(Q[half].tile[:, :], mean_c[:, :], x2[:, c, half * HALF:(half + 1) * HALF],
                                         start=c == 0, stop=c == CT - 1)
                    last.then_inc(Q[half].ready, 1)

            def variance(b, ln):
                pe.wait_ge(sq_made, b * 4 + ln * 2 + 2)
                Q[0].wait_free(pe, b, ("var", ln))
                for t in range(NT):
                    for c in range(CT):
                        last = pe.matmul(Q[0].tile[:, t:t + 1], squares[:, c, t * P:(t + 1) * P], mean_c[:, 0:1],
                                         start=c == 0, stop=c == CT - 1)
                last.then_inc(Q[0].ready, 1)

            def spread(b, ln):
                pe.wait_ge(diag_made, b * 2 + ln + 1)
                for half in range(2):
                    Q[half].wait_free(pe, b, ("spread", ln))
                    pe.matmul(Q[half].tile[:, :], ones[:, :], sq[:, half * HALF:(half + 1) * HALF], start=True, stop=True)\
                        .then_inc(Q[half].ready, 1)

            def window_project(b, j):
                nn = block_size(j)
                mm = nn + 2 * WIN
                k0 = j * BLK + 4 - WIN
                if j == 0:
                    for half in range(2):
                        Q[half].wait_drained(pe, b, ("spread", 0))
                Q[0].wait_free(pe, b, ("kq", j))
                for col, which, start, n in ((0, 1, k0, mm), (2 * P, 0, k0 + WIN, nn)):
                    for m in range(CT):
                        for k in range(CT):
                            last = pe.matmul(Q[0].tile[:, col + m * P:col + m * P + n], w1[:, which, k, m * P:(m + 1) * P],
                                             xw[:, k, start:start + n], start=k == 0, stop=k == CT - 1)
                last.then_inc(Q[0].ready, 1)
                Q[1].wait_free(pe, b, ("wv", j))
                for k in range(CT):
                    last = pe.matmul(Q[1].tile[0:mm, 0:C], xw[:, k, k0:k0 + mm], w1[:, 2, k, :], start=k == 0, stop=k == CT - 1)
                last.then_inc(Q[1].ready, 1)

            def window_scores(b, j):
                nn = block_size(j)
                mm = nn + 2 * WIN
                Q[0].wait_drained(pe, b, ("kq", j))
                for k in range(CT):
                    last = pe.matmul(Q[0].tile[0:nn, 0:mm], qb[:, k, 0:nn], kb[:, k, 0:mm], start=k == 0, stop=k == CT - 1)
                last.then_inc(Q[0].ready, 1)

            def window_turn(b, j):
                nn = block_size(j)
                mm = nn + 2 * WIN
                pe.wait_ge(wprob_made, b * NBLK + j + 1)
                Q[1].wait_free(pe, b, ("wt", j))
                pe.transpose(Q[1].tile[0:mm, 0:nn], pm[0:nn, 0:mm], ident[0:nn, 0:nn]).then_inc(Q[1].ready, 1)

            def window_values(b, j):
                nn = block_size(j)
                mm = nn + 2 * WIN
                Q[1].wait_drained(pe, b, ("wt", j))
                Q[0].wait_free(pe, b, ("wo", j))
                for m in range(CT):
                    last = pe.matmul(Q[0].tile[:, m * P:m * P + nn], vb[0:mm, m * P:(m + 1) * P], pt[0:mm, 0:nn],
                                     start=True, stop=True)
                last.then_inc(Q[0].ready, 1)

            group_means(0)
            turn_of_loop(0, False, True)
            with pe.Fori(1, B - 1) as b:
                turn_of_loop(b, True, True)
            turn_of_loop(B - 1, True, False)
            project_mix(B - 1)
            for n in range(ALL_UNITS):
                post(B - 1, n)

        @block.scalar
        def _(act):
            def qk_hi(b, quad):
                if quad == 1:
                    for s in range(QUAD):
                        act.wait_ge(stacked[s], FREE_DMA + b * 96 + 48)
                else:
                    for s in range(QUAD):
                        act.wait_ge(stacked[s], FREE_DMA + b * 96)
                for which in range(2):
                    for half in range(2):
                        T[half].wait_ready(act, b, "qk"[which] + f"{quad}h{half}")
                        col = 2 * which + quad
                        act.activation(qk[:, 1 + which, half * HALF:(half + 1) * HALF], T[half].tile[:, :], ACT.Identity,
                                       bias=qkb[:, col:col + 1]).then_inc(qkh_made, 1)

            def split_normed(b):
                for c in range(CT):
                    act.wait_ge(xn_made, b * CT + c + 1)
                    act.activation(xh[:, c, :], xin[:, c, :], ACT.Copy).then_inc(xh_made, 1)

            def copy_v(b, g):
                if g == 0:
                    act.wait_ge(prob_used, FREE + b * ALL_UNITS)
                T[g % 2].wait_ready(act, b, ("v", g))
                act.activation(v[:, 2 * g:2 * g + 2, :].rearrange("p t o -> p (t o)"), T[g % 2].tile[:, :], ACT.Copy)\
                    .then_inc(T[g % 2].free, 1)

            def fold_hi(b, with_post):
                if with_post:
                    Q[1].wait_ready(act, b - 1, ("proj", 1))
                act.wait_ge(fold_made, (b + 1) * 4)
                for c in range(CT):
                    act.activation(fh[:, c, :], xin[:, c, :], ACT.Copy).then_inc(fh_made, 1)

            def vf_hi(b, a):
                if a == 0:
                    act.wait_ge(mixl_made, FREE + b * 4)
                T[a % 2].wait_ready(act, b, ("fold", a))
                act.activation(vf[0][:, a].rearrange("p u o -> p (u o)"), T[a % 2].tile[:, :], ACT.Copy).then_inc(vfh_made, 1)

            def copy_diffused(b, c, s):
                T[s].wait_ready(act, b, ("diffuse", c, s))
                act.activation(ysum[:, c, s], T[s].tile[:, :], ACT.Copy, scale=al[:, 1:2]).then_inc(T[s].free, 1)

            def drain_attended(b, pair, half):
                act.wait_ge(prob_used, FREE + b * ALL_UNITS + pair * UNITS + (half + 1) * NT)
                n = slice(half * HALF, (half + 1) * HALF)
                if pair % 2 == 0:
                    act.wait_ge(mix_made, FREE + b * 4 + pair)
                for ab in range(2):
                    to = HD * ((2 * pair + ab) % QUAD)
                    act.activation(att[to:to + HD, n], O[half].tile[2 * ab * HD:(2 * ab + 1) * HD, :], ACT.Copy,
                                   scale=al[2 * ab * HD:(2 * ab + 1) * HD, 0:1])
                    last = act.activation(den[to:to + HD, n], O[half].tile[(2 * ab + 1) * HD:(2 * ab + 2) * HD, :], ACT.Copy)
                last.then_inc(O[half].free, 1)

            def mix_hi(b, quad, half):
                act.wait_ge(mix_made, FREE + b * 4 + quad * 2 + half + 1)
                n = slice(half * HALF, (half + 1) * HALF)
                act.activation(fh[:, quad, n], vd[:, quad, n], ACT.Copy).then_inc(mixh_made, 1)

            def exps(b, pair, u):
                n = b * ALL_UNITS + pair * UNITS + u
                for ab in range(2):
                    T[ab].wait_ready(act, b, ("score", pair, u))
                    if ab == 0:
                        act.wait_ge(prob_used, FREE + (n - 1 if pair or u else n))
                    act.activation(prob[:, u % 2, ab, :], T[ab].tile[:, :], ACT.Exp, scale=HEAD_SCALE)\
                        .then_inc(T[ab].free, 1)

            def post(b, who, n):
                for stage, j in POST[who].get(n, []):
                    {"square": square, "project": window_project, "exp": window_exp, "turn": window_turn}[stage](b, j)

            def turn_of_loop(b, with_post, ahead):
                qk_hi(b, 0)
                if with_post:
                    mix_hi(b - 1, 1, 0)
                for g in range(4):
                    copy_v(b, g)
                if with_post:
                    mix_hi(b - 1, 1, 1)
                fold_hi(b, with_post)
                for n in range(2 * NT):
                    if n in FOLD_AT:
                        vf_hi(b, FOLD_AT[n])
                    if n in DIFFUSE_AT:
                        copy_diffused(b, *DIFFUSE_AT[n])
                for n in range(ALL_UNITS):
                    pair, u = divmod(n, UNITS)
                    if n == NEXT_QUAD_AT:
                        qk_hi(b, 1)
                    if n in MIX_HI_AT:
                        mix_hi(b, *MIX_HI_AT[n])
                    if with_post:
                        post(b - 1, "act_early", n)
                    exps(b, pair, u)
                    if u == DRAIN_AT:
                        drain_attended(b, pair, 0)
                    if n == NORM_AT + 5 and ahead:
                        split_normed(b + 1)
                    if with_post:
                        post(b - 1, "act", n)
                    if u == UNITS - 1:
                        drain_attended(b, pair, 1)

            def square(b, ln):
                for half in range(2):
                    Q[half].wait_drained(act, b, ("mean", ln))
                    n = slice(half * HALF, (half + 1) * HALF)
                    act.activation(squares[:, :, n], xw[:, :, 4 + half * HALF:4 + (half + 1) * HALF], ACT.Square)\
                        .then_inc(sq_made, 1)

            def window_project(b, j):
                nn = block_size(j)
                mm = nn + 2 * WIN
                Q[0].wait_ready(act, b, ("kq", j))
                for col, which, to, n in ((0, 1, kb, mm), (2 * P, 0, qb, nn)):
                    for m in range(CT):
                        last = act.activation(to[:, m, 0:n], Q[0].tile[:, col + m * P:col + m * P + n], ACT.Identity,
                                              bias=wb[:, which, m:m + 1])
                last.then_inc(Q[0].free, 1)

            def window_exp(b, j):
                nn = block_size(j)
                mm = nn + 2 * WIN
                act.wait_ge(neg_made, b * NBLK + j + 1)
                act.activation(pm[0:nn, 0:mm], sm[0:nn, 0:mm], ACT.Exp, scale=WIN_SCALE, bias=wneg[0:nn, 1:2],
                               accum_out=wden[0:nn, 0:1]).then_inc(wexp_made, 1)

            def window_turn(b, j):
                nn = block_size(j)
                mm = nn + 2 * WIN
                Q[1].wait_ready(act, b, ("wt", j))
                act.activation(pt[0:mm, 0:nn], Q[1].tile[0:mm, 0:nn], ACT.Copy).then_inc(Q[1].free, 1)

            split_normed(0)
            turn_of_loop(0, False, True)
            with act.Fori(1, B - 1) as b:
                turn_of_loop(b, True, True)
            turn_of_loop(B - 1, True, False)
            for half in range(2):
                mix_hi(B - 1, 1, half)
            for n in range(ALL_UNITS):
                post(B - 1, "act_early", n)
                post(B - 1, "act", n)

        @block.vector
        def _(dve):
            def qk_lo(b, quad):
                for which in range(2):
                    for half in range(2):
                        n = slice(half * HALF, (half + 1) * HALF)
                        dve.wait_ge(qkh_made, b * 8 + quad * 4 + which * 2 + half + 1)
                        col = 2 * which + quad
                        dve.scalar_tensor_tensor(qk[:, 3 * which, n], T[half].tile[:, :], qkb[:, col:col + 1],
                                                 qk[:, 1 + which, n].bitcast(F32), ALU.add, ALU.subtract)\
                            .then_inc(T[half].free, 1)

            def channel_stats(b):
                link = norm_link(b)
                dve.wait_ge(x_landed, (b + 1) * 16)
                for c in range(CT):
                    for half in range(2):
                        link.done(dve.bn_stats(stats[:, c, half, :], xin[:, c, half * HALF:(half + 1) * HALF]))
                link.wait()
                dve.sem_inc(stats_made, 1)
                for c in range(CT):
                    link.done(dve.bn_aggr(aggr[:, c, :], stats[:, c, :, :].rearrange("p h s -> p (h s)")))
                link.wait()
                link.done(dve.tensor_copy(gstat[:, 0, :], aggr[:, :, 0]))
                link.done(dve.tensor_tensor(gtmp[:, 0, :], aggr[:, :, 0], aggr[:, :, 0], ALU.mult))
                link.wait()
                dve.tensor_tensor(gstat[:, 1, :], gtmp[:, 0, :], aggr[:, :, 1], ALU.add).then_inc(gstat_made, 1)
                assert link.n == 8

            def norm_link(b, n=0):
                link = Link(dve, dve_front, b * FRONT_LINKS)
                link.n = n
                return link

            def group_stats(b):
                link = norm_link(b, 8)
                M[0].wait_ready(dve, b, "gn")
                dve.tensor_copy(gmean[:, :, :], M[0].tile[:, 0:2 * CT].rearrange("p (a c) -> p a c", a=2)).then_inc(M[0].free, 1)
                M[0].wait_drained(dve, b, "gn")
                link.done(dve.tensor_tensor(gtmp[:, 0, :], gmean[:, 0, :], gmean[:, 0, :], ALU.mult))
                link.wait()
                link.done(dve.tensor_tensor(gtmp[:, 1, :], gmean[:, 1, :], gtmp[:, 0, :], ALU.subtract))
                link.wait()
                dve.tensor_scalar(gvar[:, :], gtmp[:, 1, :], 0.0, EPS, ALU.max, ALU.add).then_inc(gvar_made, 1)
                assert link.n == 10

            def norm(b):
                link = norm_link(b, 10)
                dve.wait_ge(grstd_made, b + 1)
                link.done(dve.scalar_tensor_tensor(gbias[:, :], gmean[:, 0, :], -1.0, grstd[:, :], ALU.mult, ALU.mult))
                link.wait()
                for c in range(CT):
                    dve.tensor_scalar(xin[:, c, :], xin[:, c, :], grstd[:, c:c + 1], gbias[:, c:c + 1], ALU.mult, ALU.add)\
                        .then_inc(xn_made, 1)
                assert link.n == FRONT_LINKS

            def split_normed(b):
                for c in range(CT):
                    dve.wait_ge(xh_made, b * CT + c + 1)
                    dve.tensor_tensor(xl[:, c, :], xin[:, c, :], xh[:, c, :].bitcast(F32), ALU.subtract).then_inc(xl_made, 1)

            def fold_lo(b):
                for c in range(CT):
                    dve.wait_ge(fh_made, b * CT + c + 1)
                    dve.tensor_tensor(fl[:, c, :], xin[:, c, :], fh[:, c, :].bitcast(F32), ALU.subtract).then_inc(fl_made, 1)

            def vf_lo(b, a):
                dve.wait_ge(vfh_made, b * 4 + a + 1)
                dve.tensor_tensor(vf[1][:, a].rearrange("p u o -> p (u o)"), T[a % 2].tile[:, :],
                                  vf[0][:, a].rearrange("p u o -> p (u o)").bitcast(F32), ALU.subtract)\
                    .then_inc(T[a % 2].free, 1)

            def row_max(b, h, t):
                for half in range(2):
                    M[half].wait_ready(dve, b, ("smax", h, t))
                    if t == 0 and half == 0:
                        dve.wait_ge(rowmax_made, FREE + b * NH + h)
                    dve.tensor_reduce(mx[:, h % 2, t, half:half + 1], M[half].tile[:, :], AXX, ALU.max)\
                        .then_inc(M[half].free, 1)
                if t == NT - 1:
                    for half in range(2):
                        M[half].wait_drained(dve, b, ("smax", h, t))
                    both = [mx[:, h % 2, :, half].unsqueeze(1).broadcast_to([P, 2, NT]) for half in range(2)]
                    dve.tensor_tensor(mx2[:, h % 2], both[0], both[1], ALU.max).then_inc(rowmax_made, 1)

            def shift(b, h):
                link = Link(dve, dve_heads, b * HEAD_LINKS + h)
                tile = M[h % 2].tile[0:16, 0:P]
                M[h % 2].wait_ready(dve, b, ("turn", h))
                dve.wait_ge(shift_made, FREE + b * NH + h)
                link.done(dve.tensor_copy(th[:, :], tile))
                link.wait()
                dve.scalar_tensor_tensor(td[:, :], th[:, :].bitcast(F32), low_rows[:, 0:1], tile, ALU.mult, ALU.add)\
                    .then_inc(M[h % 2].free, 1)
                M[h % 2].wait_drained(dve, b, ("turn", h))
                to = stack[h % QUAD][SHIFT:STACK, 0, :].rearrange("p (t n) -> p t n", t=NT)
                dve.tensor_tensor(to, td[:, :].unsqueeze(1).broadcast_to([16, NT, P]),
                                  tile_mask[:, :].unsqueeze(2).broadcast_to([16, NT, P]), ALU.mult).then_inc(shift_made, 1)

            def mix(b, quad, half):
                n = slice(half * HALF, (half + 1) * HALF)
                link = Link(dve, dve_mix, b * 8 + (quad * 2 + half) * 2)
                O[half].wait_drained(dve, b, 2 * quad + 1)
                link.done(dve.reciprocal(den[:, n], den[:, n]))
                link.wait()
                link.done(dve.tensor_tensor(att[:, n], att[:, n], den[:, n], ALU.mult))
                link.wait()
                dve.wait_ge(vd_made, (b + 1) * 4)
                dve.tensor_tensor(vd[:, quad, n], att[:, n], vd[:, quad, n], ALU.add).then_inc(mix_made, 1)

            def mix_lo(b, quad, half):
                n = slice(half * HALF, (half + 1) * HALF)
                dve.wait_ge(mixh_made, b * 4 + quad * 2 + half + 1)
                dve.tensor_tensor(fl[:, quad, n], vd[:, quad, n], fh[:, quad, n].bitcast(F32), ALU.subtract).then_inc(mixl_made, 1)

            def residual(b):
                for half in range(2):
                    n = slice(half * HALF, (half + 1) * HALF)
                    for m in range(CT):
                        Q[m].wait_ready(dve, b, ("proj", half))
                        if half == 0 and m == 0:
                            dve.wait_ge(x_again, (b + 1) * 16)
                        dve.scalar_tensor_tensor(x2[:, m, n], Q[m].tile[:, :], pb[:, m:m + 1], x2[:, m, n], ALU.add, ALU.add)\
                            .then_inc(Q[m].free, 1)

            def mix_tail(b):
                mix(b, 1, 1)
                for half in range(2):
                    mix_lo(b, 1, half)

            def post(b, who, n):
                for stage, j in POST[who].get(n, []):
                    {"deviation": deviation, "variance": variance, "diagonal": diagonal, "normed": normed,
                     "project": window_project, "mask": window_mask, "probs": window_probs,
                     "residual": window_residual}[stage](b, j)

            def turn_of_loop(b, with_post, ahead):
                qk_lo(b, 0)
                if with_post:
                    mix_tail(b - 1)
                    residual(b - 1)
                for n in range(2 * NT):
                    row_max(b, n // NT, n % NT)
                    if n == FRONT_TURN_AT:
                        shift(b, 0)
                    if n == 2:
                        fold_lo(b)
                    if n in FOLD_AT:
                        vf_lo(b, FOLD_AT[n])
                shift(b, 1)
                for n in range(ALL_UNITS):
                    pair, u = divmod(n, UNITS)
                    if n == NEXT_QUAD_AT:
                        qk_lo(b, 1)
                    if n in MIX_AT:
                        mix(b, *MIX_AT[n])
                    if n in MIX_LO_AT:
                        mix_lo(b, *MIX_LO_AT[n])
                    if with_post:
                        post(b - 1, "dve_early", n)
                    if pair + 1 < PAIRS:
                        row_max(b, 2 * pair + 2 + u // NT, u % NT)
                        if u == TURN_AT:
                            shift(b, 2 * pair + 2)
                    if ahead:
                        if n == NORM_AT:
                            channel_stats(b + 1)
                        if n == NORM_AT + 3:
                            group_stats(b + 1)
                        if n == NORM_AT + 4:
                            norm(b + 1)
                        if n == NORM_AT + 6:
                            split_normed(b + 1)
                    if with_post:
                        post(b - 1, "dve", n)
                    if u == UNITS - 1 and pair + 1 < PAIRS:
                        shift(b, 2 * pair + 3)

            def deviation(b, ln):
                for half in range(2):
                    n = slice(half * HALF, (half + 1) * HALF)
                    to = xw[:, :, 4 + half * HALF:4 + (half + 1) * HALF]
                    Q[half].wait_ready(dve, b, ("mean", ln))
                    if ln == 0 and half == 0:
                        dve.wait_ge(n_stored, FREE_DMA + b * 16)
                        dve.wait_ge(feat_done, FREE + b)
                    dve.tensor_tensor(to, x2[:, :, n], Q[half].tile[:, :].unsqueeze(1).broadcast_to([P, CT, HALF]),
                                      ALU.subtract).then_inc(Q[half].free, 1)

            def variance(b, ln):
                Q[0].wait_ready(dve, b, ("var", ln))
                dve.tensor_scalar(lnv[:, :], Q[0].tile[:, 0:NT], EPS, None, ALU.add).then_inc(Q[0].free, 1)

            def diagonal(b, ln):
                dve.wait_ge(rstd_made, b * 2 + ln + 1)
                dve.tensor_tensor(diag, ident[:, :].unsqueeze(1).broadcast_to([P, NT, P]),
                                  lnr[:, :].unsqueeze(2).broadcast_to([P, NT, P]), ALU.mult).then_inc(diag_made, 1)

            def normed(b, ln):
                for half in range(2):
                    to = xw[:, :, 4 + half * HALF:4 + (half + 1) * HALF]
                    Q[half].wait_ready(dve, b, ("spread", ln))
                    dve.tensor_tensor(to, to, Q[half].tile[:, :].unsqueeze(1).broadcast_to([P, CT, HALF]), ALU.mult)\
                        .then_inc(Q[half].free, 1)

            def window_project(b, j):
                mm = block_size(j) + 2 * WIN
                Q[1].wait_ready(dve, b, ("wv", j))
                dve.tensor_copy(vb[0:mm, :], Q[1].tile[0:mm, 0:C]).then_inc(Q[1].free, 1)

            def window_mask(b, j):
                nn = block_size(j)
                mm = nn + 2 * WIN
                kind = 0 if j == 0 else 2 if j == NBLK - 1 else 1
                Q[0].wait_ready(dve, b, ("ws", j))
                dve.tensor_tensor(sm[0:nn, 0:mm], Q[0].tile[0:nn, 0:mm], win_mask[0:nn, kind, 0:mm], ALU.add).then_inc(Q[0].free, 1)
                Q[0].wait_drained(dve, b, ("ws", j))
                dve.tensor_reduce(wneg[0:nn, 0:1], sm[0:nn, 0:mm], AXX, ALU.max).then_inc(win_max_made, 1)
                dve.wait_ge(win_max_made, b * NBLK + j + 1)
                dve.tensor_scalar(wneg[0:nn, 1:2], wneg[0:nn, 0:1], -WIN_SCALE, None, ALU.mult).then_inc(neg_made, 1)

            def window_probs(b, j):
                nn = block_size(j)
                mm = nn + 2 * WIN
                dve.wait_ge(wexp_made, b * NBLK + j + 1)
                dve.reciprocal(wden[0:nn, 1:2], wden[0:nn, 0:1]).then_inc(win_den_made, 1)
                dve.wait_ge(win_den_made, b * NBLK + j + 1)
                dve.tensor_scalar(pm[0:nn, 0:mm], pm[0:nn, 0:mm], wden[0:nn, 1:2], None, ALU.mult).then_inc(wprob_made, 1)

            def window_residual(b, j):
                nn = block_size(j)
                n = slice(j * BLK, j * BLK + nn)
                Q[0].wait_ready(dve, b, ("wo", j))
                for m in range(CT):
                    last = dve.scalar_tensor_tensor(x2[:, m, n], Q[0].tile[:, m * P:m * P + nn], wb[:, 2, m:m + 1], x2[:, m, n],
                                                    ALU.add, ALU.add)
                last.then_inc(Q[0].free, 1)

            channel_stats(0)
            group_stats(0)
            norm(0)
            split_normed(0)
            turn_of_loop(0, False, True)
            with dve.Fori(1, B - 1) as b:
                turn_of_loop(b, True, True)
            turn_of_loop(B - 1, True, False)
            mix_tail(B - 1)
            residual(B - 1)
            for n in range(ALL_UNITS):
                post(B - 1, "dve_early", n)
                post(B - 1, "dve", n)


def expert_phase(nc, Wr, br, W, bn, bo, t_d, n_d, feat_d, out):
    out_v = out.rearrange("b (c p) n -> b p c n", p=P)

    with ExitStack() as ctx:
        def sb(name, shape, dt=F32):
            return ctx.enter_context(nc.sbuf_tensor(name, shape, dt))

        def sem(name):
            return ctx.enter_context(nc.semaphore(name))

        wh = sb("expert_w_hi", [P, E, 3, CT, C], F32R)
        wl = sb("expert_w_lo", [P, E, 3, CT, C], F32R)
        gate = sb("gate", [P, E, N])
        gated_bo = sb("gated_output_bias", [P, CT, N])
        xf = sb("x_normed", [P, CT, N])
        xh = sb("x_hi", [P, CT, N], F32R)
        xl = sb("x_lo", [P, CT, N], F32R)
        tok = sb("tokens", [P, CT, N])
        h1h, h1l, h2h, h2l = (sb(k, [P, 2, CT, HALF], F32R) for k in ("h1_hi", "h1_lo", "h2_hi", "h2_lo"))
        z1 = sb("z1", [P, HALF])
        z2 = sb("z2", [P, HALF])
        bnp = sb("norm_params", [P, 2, 5, E, CT])
        scale = sb("norm_scale", [P, 2, E, CT])
        shift = sb("norm_shift", [P, 2, E, CT])
        half_p = sb("minus_half_p", [P, 2, E, CT])
        ident = sb("ident_b", [P, P])
        wr = sb("gate_w", [P, CT, E])
        brb = sb("gate_b", [P, E])
        bos = sb("output_bias", [E, C])
        lg = sb("logits", [P, NT, E])
        red = sb("gate_reduced", [P, 2, NT])
        wT = xf[0:E, 0, :]
        stage = xf[:, :, :].rearrange("p c n -> p (c n)").rearrange("p (r k o) -> p r k o", r=4, k=CT)

        Z1, Z2 = ([ctx.enter_context(nc.psum_tensor(f"z{l}_{m}", [P, HALF], F32)) for m in range(CT)] for l in (1, 2))
        A = [[ctx.enter_context(nc.psum_tensor(f"sum{h}_{m}", [P, HALF], F32)) for m in range(CT)] for h in range(2)]

        in_small, in_feat = sem("in_small"), sem("in_feat")
        in_w = [sem(f"in_w{r}") for r in range(4)]
        w_hi, w_lo = sem("expert_w_hi_made"), sem("expert_w_lo_made")
        ident_made, pow_asked, pow_made = sem("ident_b_made"), sem("pow_asked"), sem("pow_made")
        dve_gate, logits_made, lg_shifted, lg_exp, gate_made = (
            sem(k) for k in ("dve_gate_chain", "logits_made", "lg_shifted", "lg_exp", "gate_made"))
        turned, wT_made, spread, spread_out = (sem(k) for k in ("gate_turned", "wT_made", "gate_spread", "gate_spread_out"))

        NW = 3 * E
        with nc.Block() as block:
            @block.sync
            def _(sp):
                sp.dma_start(tok[:, :, :], feat_d).then_inc(in_feat, 16)
                sp.dma_start(wr[:, :, :], Wr.rearrange("(c p) e -> p c e", p=P)).then_inc(in_small, 16)
                sp.dma_start(brb[:, :], br.partition_broadcast(P)).then_inc(in_small, 16)
                sp.dma_start(bos[:, :], bo).then_inc(in_small, 16)
                sp.dma_start(bnp[:, :, :, :, :], bn).then_inc(in_small, 16)
                for n in range(NW):
                    if n >= 4:
                        sp.wait_ge(w_lo, n - 3)
                    sp.dma_start(stage[:, n % 4], W[n % 3, n // 3].rearrange("(k p) o -> p k o", p=P)).then_inc(in_w[n % 4], 16)

            @block.gpsimd
            def _(pool):
                pool.memset(ident[:, :], 0.0).then_inc(ident_made, 1)
                pool.memset(half_p[:, :, :, :], -0.5).then_inc(ident_made, 1)
                pool.wait_ge(ident_made, 2)
                pool.affine_select(out=ident[:, :], in_=ident[:, :], compare_op=ALU.not_equal, fill=1.0, base=0,
                                   pattern=[[-1, P]], channel_multiplier=1).then_inc(ident_made, 1)
                pool.wait_ge(pow_asked, 1)
                pool.tensor_tensor(scale[:, :, :, :], scale[:, :, :, :], half_p[:, :, :, :], ALU.pow).then_inc(pow_made, 1)

            @block.tensor
            def _(pe):
                pe.wait_ge(in_feat, 16)
                pe.wait_ge(in_small, 4 * 16)
                for t in range(NT):
                    for c in range(CT):
                        last = pe.matmul(Z1[0][:, t * E:(t + 1) * E], tok[:, c, t * P:(t + 1) * P], wr[:, c, :],
                                         start=c == 0, stop=c == CT - 1)
                last.then_inc(logits_made, 1)
                pe.wait_ge(gate_made, 1)
                pe.wait_ge(ident_made, 3)
                for t in range(NT):
                    last = pe.transpose(A[t // 4][0][0:E, (t % 4) * P:(t % 4 + 1) * P], lg[:, t, :], ident[:, :])
                last.then_inc(turned, 1)
                pe.wait_ge(wT_made, 2)
                for n in range(2 * E):
                    e, half = n // 2, n % 2
                    if n >= 2:
                        pe.wait_ge(spread_out, n - 1)
                    pe.matmul(Z2[n % 2][:, :], ident[0:E, e:e + 1].broadcast_to([E, P]), wT[:, half * HALF:(half + 1) * HALF],
                              start=True, stop=True).then_inc(spread, 1)
                for n in range(2 * CT):
                    m, half = n // 2, n % 2
                    pe.wait_ge(spread_out, 2 * E + n - 1)
                    pe.matmul(Z2[n % 2][:, :], bos[:, m * P:(m + 1) * P], wT[:, half * HALF:(half + 1) * HALF],
                              start=True, stop=True).then_inc(spread, 1)

            @block.scalar
            def _(act):
                act.wait_ge(lg_shifted, 1)
                act.activation(lg[:, :, :], lg[:, :, :], ACT.Exp).then_inc(lg_exp, 1)
                for n in range(NW):
                    act.wait_ge(in_w[n % 4], (n // 4 + 1) * 16)
                    act.activation(wh[:, n // 3, n % 3], stage[:, n % 4], ACT.Copy).then_inc(w_hi, 1)

            @block.vector
            def _(dve):
                link = Link(dve, dve_gate, 0)
                dve.wait_ge(in_small, 4 * 16)
                link.done(dve.tensor_scalar(scale[:, :, :, :], bnp[:, :, 4], BN_EPS, None, ALU.add))
                link.wait()
                dve.sem_inc(pow_asked, 1)
                link.done(dve.tensor_tensor(shift[:, :, :, :], bnp[:, :, 0], bnp[:, :, 3], ALU.subtract))
                dve.wait_ge(pow_made, 1)
                link.wait()
                link.done(dve.tensor_tensor(scale[:, :, :, :], scale[:, :, :, :], bnp[:, :, 1], ALU.mult))
                link.wait()
                link.done(dve.tensor_tensor(shift[:, :, :, :], shift[:, :, :, :], scale[:, :, :, :], ALU.mult))
                link.wait()
                link.done(dve.tensor_tensor(shift[:, :, :, :], shift[:, :, :, :], bnp[:, :, 2], ALU.add))
                dve.wait_ge(logits_made, 1)
                link.done(dve.scalar_tensor_tensor(lg[:, :, :], Z1[0][:, 0:NT * E].rearrange("p (t e) -> p t e", e=E), 1.0 / B,
                                                   brb[:, :].unsqueeze(1).broadcast_to([P, NT, E]), ALU.mult, ALU.add))
                link.wait()
                link.done(dve.tensor_reduce(red[:, 0, :], lg[:, :, :], AXX, ALU.max))
                link.wait()
                dve.tensor_tensor(lg[:, :, :], lg[:, :, :], red[:, 0, :].unsqueeze(2).broadcast_to([P, NT, E]), ALU.subtract)\
                    .then_inc(lg_shifted, 1)
                dve.wait_ge(lg_exp, 1)
                link.done(dve.tensor_reduce(red[:, 1, :], lg[:, :, :], AXX, ALU.add))
                link.wait()
                link.done(dve.reciprocal(red[:, 0, :], red[:, 1, :]))
                link.wait()
                dve.tensor_tensor(lg[:, :, :], lg[:, :, :], red[:, 0, :].unsqueeze(2).broadcast_to([P, NT, E]), ALU.mult)\
                    .then_inc(gate_made, 1)
                for n in range(NW):
                    dve.wait_ge(w_hi, n + 1)
                    dve.tensor_tensor(wl[:, n // 3, n % 3], stage[:, n % 4], wh[:, n // 3, n % 3].bitcast(F32), ALU.subtract)\
                        .then_inc(w_lo, 1)
                dve.wait_ge(turned, 1)
                dve.wait_ge(w_lo, NW)
                for half in range(2):
                    dve.tensor_copy(wT[:, half * HALF:(half + 1) * HALF], A[half][0][0:E, :]).then_inc(wT_made, 1)
                for n in range(2 * E + 2 * CT):
                    dve.wait_ge(spread, n + 1)
                    m = n // 2
                    to = gate[:, m] if m < E else gated_bo[:, m - E]
                    dve.tensor_copy(to[:, n % 2 * HALF:(n % 2 + 1) * HALF], Z2[n % 2][:, :]).then_inc(spread_out, 1)

        STEPS = 2 * E
        x_landed, t_landed = sem("x_landed_b"), sem("t_landed_b")
        out_stored = sem("out_stored")
        out_done = sem("out_done")
        xh_made, xl_made = sem("xh_made_b"), sem("xl_made_b")
        z1_ready, z2_ready = sem("z1_ready"), sem("z2_ready")
        z1_made, z2_made = sem("z1_made"), sem("z2_made")
        h1h_made, h1l_made = sem("h1h_made"), sem("h1l_made")
        h2_gated, h2h_made, h2l_made = sem("h2_gated"), sem("h2h_made"), sem("h2l_made")
        sum_ready = sem("sum_ready")
        sum_read = sem("sum_read")
        out_made = sem("out_made")

        block = ctx.enter_context(nc.Block())

        @block.sync
        def _(sp):
            with sp.Fori(0, B) as b:
                sp.wait_ge(xl_made, FREE + b * 2)
                sp.dma_start(xf[:, :, :], n_d[b]).then_inc(x_landed, 16)
                sp.wait_ge(out_done, FREE + b)
                sp.dma_start(tok[:, :, :], t_d[b]).then_inc(t_landed, 16)

        @block.gpsimd
        def _(pool):
            for s in (xl_made, h1h_made, h1l_made, z2_made, sum_read, h2l_made, z1_ready):
                pool.sem_inc(s, FREE)
            pool.sem_inc(out_done, FREE)
            with pool.Fori(0, B) as b:
                for half in range(2):
                    n = slice(half * HALF, (half + 1) * HALF)
                    pool.wait_ge(out_made, b * 2 * CT + (half + 1) * CT)
                    pool.dma_start(out_v[b, :, :, n], tok[:, :, n]).then_inc(out_stored, 16)
                pool.wait_ge(out_stored, (b + 1) * 32)
                pool.sem_inc(out_done, 1)

        @block.tensor
        def _(pe):
            def layer(tile, e, which, m, rh, rl, start, stop):
                o = slice(m * P, (m + 1) * P)
                for k in range(CT):
                    for j, (w, r) in enumerate(((wh, rh), (wl, rh), (wh, rl))):
                        last = pe.matmul(tile[:, :], w[:, e, which, k, o], r[:, k], start=start and k == 0 and j == 0,
                                         stop=stop and k == CT - 1 and j == 2)
                return last

            with pe.Fori(0, B) as b:
                for step in range(STEPS + 2):
                    if step < STEPS:
                        half, e = divmod(step, E)
                        n = slice(half * HALF, (half + 1) * HALF)
                        if e == 0:
                            pe.wait_ge(xl_made, FREE + b * 2 + half + 1)
                        for m in range(CT):
                            pe.wait_ge(h1h_made, FREE + ((b * STEPS + step - 1) * CT + m + 1 if step else b * STEPS * CT))
                            layer(Z1[m], e, 0, m, xh[:, :, n], xl[:, :, n], True, True).then_inc(z1_ready, 1)
                    if 1 <= step <= STEPS:
                        g = step - 1
                        pe.wait_ge(h1l_made, FREE + (b * STEPS + g + 1) * CT)
                        for m in range(CT):
                            pe.wait_ge(z2_made, FREE + ((b * STEPS + g - 1) * CT + m + 1 if g else b * STEPS * CT))
                            layer(Z2[m], g % E, 1, m, h1h[:, g % 2], h1l[:, g % 2], True, True).then_inc(z2_ready, 1)
                    if step >= 2:
                        g = step - 2
                        half, e = divmod(g, E)
                        pe.wait_ge(h2l_made, FREE + (b * STEPS + g + 1) * CT)
                        for m in range(CT):
                            if e == 0:
                                pe.wait_ge(sum_read, FREE + b * 2 * CT)
                            last = layer(A[half][m], e, 2, m, h2h[:, g % 2], h2l[:, g % 2], e == 0, e == E - 1)
                        if e == E - 1:
                            last.then_inc(sum_ready, 1)

        @block.scalar
        def _(act):
            with act.Fori(0, B) as b:
                for step in range(STEPS + 1):
                    if step < STEPS:
                        half, e = divmod(step, E)
                        if e == 0:
                            n = slice(half * HALF, (half + 1) * HALF)
                            if half == 0:
                                act.wait_ge(x_landed, (b + 1) * 16)
                                act.wait_ge(z1_ready, FREE + b * STEPS * CT)
                            act.activation(xh[:, :, n], xf[:, :, n], ACT.Copy).then_inc(xh_made, 1)
                        for m in range(CT):
                            c = (b * STEPS + step) * CT + m
                            act.wait_ge(z1_ready, FREE + c + 1)
                            act.wait_ge(h1l_made, FREE + c)
                            act.activation(z1[:, :], Z1[m][:, :], ACT.Relu, scale=scale[:, 0, e, m:m + 1],
                                           bias=shift[:, 0, e, m:m + 1]).then_inc(z1_made, 1)
                            act.activation(h1h[:, step % 2, m], Z1[m][:, :], ACT.Relu, scale=scale[:, 0, e, m:m + 1],
                                           bias=shift[:, 0, e, m:m + 1]).then_inc(h1h_made, 1)
                    if step:
                        g = step - 1
                        for m in range(CT):
                            c = (b * STEPS + g) * CT + m
                            act.wait_ge(z2_ready, c + 1)
                            act.wait_ge(h2l_made, FREE + c)
                            act.activation(z2[:, :], Z2[m][:, :], ACT.Relu, scale=scale[:, 1, g % E, m:m + 1],
                                           bias=shift[:, 1, g % E, m:m + 1]).then_inc(z2_made, 1)

        @block.vector
        def _(dve):
            def finish(b, half):
                n = slice(half * HALF, (half + 1) * HALF)
                dve.wait_ge(sum_ready, b * 2 + half + 1)
                if half == 0:
                    dve.wait_ge(t_landed, (b + 1) * 16)
                for m in range(CT):
                    dve.tensor_tensor(tok[:, m, n], A[half][m][:, :], tok[:, m, n], ALU.add).then_inc(sum_read, 1)
                    dve.wait_ge(sum_read, FREE + b * 2 * CT + half * CT + m + 1)
                    dve.tensor_tensor(tok[:, m, n], tok[:, m, n], gated_bo[:, m, n], ALU.add).then_inc(out_made, 1)

            with dve.Fori(0, B) as b:
                for step in range(STEPS + 1):
                    if step < STEPS:
                        half, e = divmod(step, E)
                        if e == 0:
                            n = slice(half * HALF, (half + 1) * HALF)
                            dve.wait_ge(xh_made, b * 2 + half + 1)
                            dve.tensor_tensor(xl[:, :, n], xf[:, :, n], xh[:, :, n].bitcast(F32), ALU.subtract)\
                                .then_inc(xl_made, 1)
                        for m in range(CT):
                            dve.wait_ge(h1h_made, FREE + (b * STEPS + step) * CT + m + 1)
                            dve.tensor_tensor(h1l[:, step % 2, m], z1[:, :], h1h[:, step % 2, m].bitcast(F32), ALU.subtract)\
                                .then_inc(h1l_made, 1)
                    if step:
                        g = step - 1
                        half = g // E
                        n = slice(half * HALF, (half + 1) * HALF)
                        for m in range(CT):
                            c = (b * STEPS + g) * CT + m
                            dve.wait_ge(z2_made, FREE + c + 1)
                            dve.tensor_tensor(z2[:, :], z2[:, :], gate[:, g % E, n], ALU.mult).then_inc(h2_gated, 1)
                            dve.wait_ge(h2_gated, c + 1)
                            dve.tensor_copy(h2h[:, g % 2, m], z2[:, :]).then_inc(h2h_made, 1)
                            dve.wait_ge(h2h_made, c + 1)
                            dve.tensor_tensor(h2l[:, g % 2, m], z2[:, :], h2h[:, g % 2, m].bitcast(F32), ALU.subtract)\
                                .then_inc(h2l_made, 1)
                    if step == E + 3:
                        finish(b, 0)
                finish(b, 1)


def diffusion_matrices():
    import numpy as np

    g = np.exp(-np.subtract.outer(np.arange(H), np.arange(H)).astype(np.float64) ** 2 / 2)
    a = np.kron(g, g)
    lap = np.diag(a.sum(1)) - a
    lam = np.linalg.eigvalsh(lap).max()
    hat = 2.0 / lam * lap - np.eye(N)
    cube = hat @ hat @ hat
    eye = np.eye(HH)
    fold = [np.concatenate([eye, s * eye[::-1]]) for s in (1, -1)]
    blocks = [np.kron(fy, fx) for fy in fold for fx in fold]
    return np.stack([f.T @ cube @ f / 16 for f in blocks]).astype(np.float32)


def kernel(**inputs):
    import numpy as np
    import concourse.bacc as bacc
    from concourse.bass_utils import run_bass_kernel_spmd

    i = {k: np.asarray(a) for k, a in inputs.items()}

    def channels(a):
        a = a.reshape(a.shape[:-1] + (-1, P))
        return np.moveaxis(a, -1, 0)

    arrays = {
        "x": i["x"].reshape(B, C, N),
        "qkv_wT": i["L0_conv_qkv_w"].T,
        "qkv_b": channels(i["L0_conv_qkv_b"]),
        "proj_wT": i["L0_conv_proj_w"].T,
        "proj_b": channels(i["L0_conv_proj_b"]),
        "alpha": i["L0_conv_alpha"].reshape(1),
        "window_wT": np.stack([i[f"L1_attn_W{k}"].T for k in "qkv"]),
        "window_b": channels(np.stack([i[f"L1_attn_b{k}"] for k in "qkv"])),
        "diffusion": diffusion_matrices(),
        "Wr": i["L1_ffn_Wr"],
        "br": i["L1_ffn_br"],
        "W": np.stack([i["L1_ffn_W1"], i["L1_ffn_W2"], i["L1_ffn_Wo"]]),
        "bn": channels(np.stack([np.stack([i[f"L1_ffn_{k}{l}"] for k in ("b", "g", "be", "m", "v")]) for l in (1, 2)])),
        "bo": i["L1_ffn_bo"],
    }
    arrays = {k: np.ascontiguousarray(a) for k, a in arrays.items()}
    nc = bacc.Bacc("TRN2", target_bir_lowering=False, num_devices=1)
    a = {k: nc.dram_tensor(k, v.shape, mybir.dt.from_np(v.dtype), kind="ExternalInput").ap() for k, v in arrays.items()}
    out = nc.dram_tensor("out", (B, C, N), F32, kind="ExternalOutput").ap()
    t_d = nc.dram_tensor("tokens_after_attention", (B, P, CT, N), F32, kind="Internal").ap()
    n_d = nc.dram_tensor("tokens_normed", (B, P, CT, N), F32, kind="Internal").ap()
    feat_d = nc.dram_tensor("normed_sum_over_batches", (P, CT, N), F32, kind="Internal").ap()
    attention_phase(nc, a["x"], a["qkv_wT"], a["qkv_b"], a["proj_wT"], a["proj_b"], a["alpha"], a["window_wT"],
                    a["window_b"], a["diffusion"], t_d, n_d, feat_d)
    expert_phase(nc, a["Wr"], a["br"], a["W"], a["bn"], a["bo"], t_d, n_d, feat_d, out)
    r = run_bass_kernel_spmd(nc, [arrays], core_ids=[0])
    return r.results[0]["out"].reshape(B, C, H, W)
```

```python
from contextlib import ExitStack

import numpy as np

import concourse.bass as bass
from concourse import mybir

F32 = mybir.dt.float32
F32R = mybir.dt.float32r
ALU = mybir.AluOpType
ACT = mybir.ActivationFunctionType
AXX = mybir.AxisListType.X

P = 128
B, C, H, W = 8, 256, 32, 32
N = H * W
CT = C // P
HALF = N // 2
NH = 8
HD = C // NH
QUAD = P // HD
NT = N // P
PAIRS = NH // 2
UNITS = 2 * NT
SHIFT = 3 * HD
STACK = SHIFT + 16
GROUP = C // 32
HH, HW = H // 2, W // 2
FT = HH * HW // P
WIN = 3
NBLK = -(-N // (P - 2 * WIN))
BLK = -(-N // NBLK)
E = 8
EPS = 1e-5
BN_EPS = 1e-3
HEAD_SCALE = float(HD) ** -0.5
WIN_SCALE = float(C) ** -0.5
ALL_UNITS = PAIRS * UNITS
TURN_AT = NT + 1
LAST_TURN_AT = UNITS - 2
QK = ((0, 0), (0, 1), (1, 0), (1, 1))
SECOND_QUAD_AT = dict(zip((0, 2, 4, 7), QK))
FIRST_QUAD_AT = dict(zip((2 * UNITS + 1, 2 * UNITS + 3, 2 * UNITS + 5, 2 * UNITS + 10), QK))
DRAIN_AT = {NT + 1: 0, 0: 1}
RECIP_AT = {UNITS + 10: (0, 0), 2 * UNITS + 1: (0, 1), 3 * UNITS + 10: (1, 0)}
RECIPS = 4
RECIP = HALF // RECIPS
MIX_AT = {n + RECIPS: half for n, half in RECIP_AT.items()}
MIX_HI_AT = {2 * UNITS - 1: (0, 0), 2 * UNITS + 6: (0, 1)}
MIX_LO_AT = {2 * UNITS: (0, 0), 2 * UNITS + 7: (0, 1)}
UNFOLD_ROWS_AT = {0: 0, UNITS: 1}
UNFOLD_COLUMNS_AT = {NT: 0, UNITS + 1: 1}
STATS_AT = UNITS - 1
MEANS_AT = STATS_AT + 1
NORMED_AT = {STATS_AT + 4: 0, STATS_AT + 5: 1}
XL_AT = {UNITS + NT: 0, UNITS + NT + 1: 1}
FOLD_ROWS_AT = {2 * UNITS: 0, 2 * UNITS + 1: 1}
FOLD_COLUMNS_AT = {2 * UNITS + NT: 0, 3 * UNITS: 1}
FOLD_HI_AT = {3 * UNITS + 4: 0, 3 * UNITS + 6: 1}
FOLD_LO_AT = {3 * UNITS + NT: 0, 3 * UNITS + NT + 1: 1}

HALVES = 2 * PAIRS
LAST_NORM_AT = 7 + 5 * NBLK + 3


def post_stages():
    at = {k: {} for k in ("pe", "act_early", "act", "dve_early", "dve")}

    def put(who, n, stage, j):
        at[who].setdefault(n, []).append((stage, j))

    for ln, n in ((0, 0), (1, LAST_NORM_AT)):
        for half in range(2):
            put("pe", n + half, "mean", (ln, half))
            put("dve_early", n + half + 1, "deviation", (ln, half))
            put("act", n + half + 1, "square", (ln, half))
            put("pe", n + half + 6, "spread", (ln, half))
            put("dve_early", n + half + 7, "normed", (ln, half))
        put("pe", n + 4, "variance", (ln, 0))
        put("dve_early", n + 5, "variance", (ln, 0))
    for j in range(NBLK):
        n = 7 + 5 * j
        put("pe", n, "project_k", (j,))
        put("pe", n + 1, "project_q", (j,))
        put("act_early", n + 2, "project", (j,))
        put("pe", n + 2, "project_v", (j,))
        put("act_early", n + 3, "project_v", (j,))
        put("pe", n + 3, "scores", (j,))
        put("dve_early", n + 4, "mask", (j,))
        put("act", n + 4, "exp", (j,))
        put("dve", n + 4, "probs", (j,))
        put("pe", n + 5, "turn", (j,))
        put("act_early", n + 6, "turn", (j,))
        put("pe", n + 6, "values", (j,))
        put("dve_early", n + 7, "residual", (j,))
    for who in at:
        for stages in at[who].values():
            stages.sort(key=lambda stage: stage[1])
        assert max(at[who]) < ALL_UNITS
    return at


LAST_POST_NORM_AT = 9 + 3 * NBLK + 4
EARLY_LOGITS_AT = LAST_POST_NORM_AT + 4


def last_post_stages():
    at = {k: {} for k in ("pe", "act", "dve")}

    def put(who, n, stage, *j):
        at[who].setdefault(n, []).append((stage, j))

    for ln, n in ((0, 0), (1, LAST_POST_NORM_AT)):
        for half in range(2):
            put("pe", n + half, "mean", ln, half)
            put("dve", n + half, "deviation", ln, half)
            put("act", n + half, "square", ln, half)
        put("pe", n + 2, "variance", ln, 0)
        put("dve", n + 2, "variance", ln, 0)
        for half in range(2):
            put("pe", n + half + 4, "spread", ln, half)
            put("dve", n + half + 4, "normed", ln, half)
    for j in range(NBLK):
        n = 9 + 3 * j
        put("pe", n - 1, "project_k", j)
        put("pe", n - 1, "project_q", j)
        put("act", n, "project", j)
        put("pe", n, "project_v", j)
        put("pe", n + 1, "scores", j)
        put("act", n + 1, "project_v", j)
        put("dve", n + 2, "mask", j)
        put("act", n + 2, "exp", j)
        put("dve", n + 2, "probs", j)
        put("pe", n + 3, "turn", j)
        put("act", n + 3, "turn", j)
        put("pe", n + 3, "values", j)
        put("dve", n + 4, "residual", j)
    for n in at["act"]:
        at["act"][n].sort(key=lambda stage: stage[0] == "turn")
    for n in at["pe"]:
        at["pe"][n].sort(key=lambda stage: stage[1])
    return at


POST, LAST_POST = post_stages(), last_post_stages()
WEIGHTS_AT = {9 + 3 * e + 1: e for e in range(E)}


ROW_TILES = ((2, 1, 0, 2, 1, 1, 2, 1, 1, 1, 0, 1, 1, 2, 0, 0),
             (0, 1, 1, 2, 1, 1, 2, 1, 1, 1, 0, 2, 2, 1, 0, 0),
             (0, 1, 1, 2, 1, 1, 1, 2, 1, 0, 0, 2, 2, 2, 0, 0),
             (0, 2, 1, 2, 2, 2, 0, 2, 1, 0, 0, 2, 1, 1, 0, 0))
ROWS = [[range(sum(tiles[:u]), sum(tiles[:u + 1])) for u in range(UNITS)] for tiles in ROW_TILES]
assert all(sum(tiles) == 2 * NT and sum(tiles[:TURN_AT]) >= NT and not sum(tiles[LAST_TURN_AT:]) for tiles in ROW_TILES)

FREE, FREE_DMA = 1, 16
FRONT_LINKS = 11
HEAD_LINKS = NH
FAR = -1e30


class Uses:

    def __init__(self, ready, free, tile, keys, last_keys=None):
        self.ready, self.free, self.tile = ready, free, tile
        self.at = {k: n for n, k in enumerate(keys)}
        self.last = {k: n for n, k in enumerate(last_keys or keys)}
        self.per = len(keys)

    def before(self, b, key):
        at = self.last if isinstance(b, int) and b == B - 1 else self.at
        return b * self.per + at[key]

    def wait_free(self, eng, b, key):
        eng.wait_ge(self.free, self.before(b, key) + 1)

    def wait_ready(self, eng, b, key):
        eng.wait_ge(self.ready, self.before(b, key) + 1)

    def wait_drained(self, eng, b, key):
        eng.wait_ge(self.free, self.before(b, key) + 2)


class Link:

    def __init__(self, eng, sem, base):
        self.eng, self.sem, self.base, self.n = eng, sem, base, 0

    def done(self, ins):
        self.n += 1
        ins.then_inc(self.sem, 1)

    def wait(self):
        self.eng.wait_ge(self.sem, self.base + self.n)


def attention_phase(nc, expert_w, expert_w_at, logits, experts, Wr, x, qkv_wT, qkv_b, proj_wT, proj_b, alpha, window_wT, window_b,
                    diffusion, t_d, n_d, feat_d):
    x_v = x.rearrange("b (c p) n -> b p c n", p=P)

    with ExitStack() as ctx:
        def sb(name, shape, dt=F32):
            return ctx.enter_context(nc.sbuf_tensor(name, shape, dt))

        def sb_at(name, shape, dt=F32):
            at = -(-nc.sbuf_base // 32) * 32
            return sb(name, shape, dt), at

        def over(name, shape, dt, at):
            return nc.alloc_sbuf_tensor_at(name, shape, dt, offset=at)

        under_weights = [expert_w_at]

        def under(name, shape, dt=F32):
            at = under_weights[0]
            under_weights[0] += 4 * int(np.prod(shape[1:]))
            assert under_weights[0] <= expert_w_at + 2 * 4 * E * 3 * CT * C
            return over(name, shape, dt, at), at

        def sem(name):
            return ctx.enter_context(nc.semaphore(name))

        ident = sb("ident", [P, P])
        ones = sb("ones", [P, P])
        mean_c = sb("mean_c", [P, P])
        group_mean = sb("group_mean", [P, P])
        minus_half = sb("minus_half", [P, NT])
        win_mask = sb("win_mask", [P, 3, P])
        tile_mask = sb("tile_mask", [16, NT])
        low_rows = sb("low_rows", [16, 1])
        wh = sb("qkv_w_hi", [P, CT, 3 * C], F32R)
        wl = sb("qkv_w_lo", [P, CT, 3 * C], F32R)
        ph = sb("proj_w_hi", [P, CT, C], F32R)
        pl = sb("proj_w_lo", [P, CT, C], F32R)
        mh = sb("diffusion_hi", [P, 4, FT, HH * HW], F32R)
        ml = sb("diffusion_lo", [P, 4, FT, HH * HW], F32R)
        w1 = sb("window_w", [P, 3, CT, C])
        qkb = sb("qkv_bias", [P, 6])
        pb = sb("proj_bias", [P, CT])
        vcol = sb("v_bias_scaled", [P, CT])
        wb = sb("window_bias", [P, 3, CT])
        al = sb("alphas", [P, 3])

        xin, xin_at = under("xin", [P, CT, N])
        stats = sb("stats", [P, CT, 2, 6])
        aggr = sb("aggr", [P, CT, 2])
        gstat = sb("gstat", [P, 2, CT])
        gmean = sb("gmean", [P, 2, CT])
        gtmp = sb("gtmp", [P, 2, CT])
        gvar = sb("gvar", [P, CT])
        grstd = sb("grstd", [P, CT])
        gbias = sb("gbias", [P, CT])
        xh, _ = under("xn_hi", [P, CT, N], F32R)
        xl, _ = under("xn_lo", [P, CT, N], F32R)
        ysum, ysum_at = under("y_folded_or_parities", [P, 2, CT, N // 2])
        foldh = over("fold_hi", [P, CT, N], F32R, ysum_at)
        foldl = over("fold_lo", [P, CT, N], F32R, xin_at)
        split, _ = under("mix_parts", [P, 2, CT, N], F32R)
        fh, fl = split[:, 0], split[:, 1]
        qk, _ = under("qk_parts", [P, 4, N], F32R)
        stack = [under(f"stack{s}", [P, 2, N], F32R)[0] for s in range(QUAD)]
        v = sb("v", [P, NT, C])
        unfold = sb("unfolded_y", [P, 2, H, HW])
        vd = sb("v_diffused", [P, CT, N])
        mx = sb("row_max", [P, 2, NT, 2])
        mx2 = sb("row_max_twice", [P, 2, 2, NT])
        th = sb("shift_hi", [16, P], F32R)
        td = sb("shift_parts", [16, P])
        _, room_at = sb_at("room", [P, 6 * N])
        vf = [over(f"v_folded_{part}", [P, 4, FT, C], F32R, room_at + k * 8192) for k, part in enumerate(("hi", "lo"))]
        prob = over("prob", [P, 4, 2, HALF], F32, room_at)
        att = over("attended", [P, N], F32, room_at + 16384)
        den = over("denominators", [P, N], F32, room_at + 20480)
        stage = over("weight_stage", [P, 4, 3, CT, C], F32, room_at)
        wr = sb("gate_w", [P, CT, E])
        feat = vd

        x2 = sb("x2", [P, CT, N])
        xw = sb("xn_padded", [P, CT, N + 8])
        sq = sb("squares_or_block", [P, CT * N])
        lnv = sb("ln_var", [P, NT])
        lnr = sb("ln_rstd", [P, NT])
        wneg = sb("win_minus_max", [P, 2])
        wden = sb("win_den", [P, 2])
        squares = sq[:, :].rearrange("p (c n) -> p c n", c=CT)
        diag = sq[:, 0:NT * P].rearrange("p (t n) -> p t n", t=NT)
        kb = sq[:, 0:256].rearrange("p (m n) -> p m n", m=CT)
        qb = sq[:, 256:512].rearrange("p (m n) -> p m n", m=CT)
        vb = sq[:, 512:768]
        sm = sq[:, 768:896]
        pm = sq[:, 896:1024]
        pt = sq[:, 1024:1152]

        bank = [ctx.enter_context(nc.psum_tensor(f"bank{k}", [P, HALF], F32)) for k in range(8)]

        x_landed = sem("x_landed")
        arrived = {k: sem(f"in_{k}") for k in ("qkv_w", "proj_w", "diffusion", "small")}
        consts_made, hi_parts_made, lo_parts_made, alphas_made, vcol_made, bias_projected, zeros_made, feat_zeroed = (
            sem(k) for k in ("consts_made", "hi_parts_made", "lo_parts_made", "alphas_made", "vcol_made",
                             "bias_projected", "zeros_made", "feat_zeroed"))
        with nc.Block() as block:
            @block.sync
            def _(sp):
                sp.dma_start(xin[:, :, :], x_v[0]).then_inc(x_landed, 16)
                sp.dma_start(squares[:, :, 0:3 * C], qkv_wT.rearrange("(c p) o -> p c o", p=P)).then_inc(arrived["qkv_w"], 16)
                sp.dma_start(vd[:, :, 0:C], proj_wT.rearrange("(c p) o -> p c o", p=P)).then_inc(arrived["proj_w"], 16)
                sp.dma_start(x2[:, :, :].rearrange("p c n -> p (c n)").rearrange("p (a u m) -> p a u m", a=4, u=FT),
                             diffusion.rearrange("a (u p) m -> p a u m", p=P)).then_inc(arrived["diffusion"], 16)
                sp.dma_start(w1[:, :, :, :], window_wT.rearrange("a (c p) o -> p a c o", p=P)).then_inc(arrived["small"], 16)
                sp.dma_start(qkb[:, :], qkv_b).then_inc(arrived["small"], 16)
                sp.dma_start(pb[:, :], proj_b).then_inc(arrived["small"], 16)
                sp.dma_start(wb[:, :, :], window_b).then_inc(arrived["small"], 16)
                sp.dma_start(al[:, 0:1], alpha.partition_broadcast(P)).then_inc(arrived["small"], 16)
                sp.wait_ge(zeros_made, 1)
                sp.dma_start(feat_d, xw[:, :, 0:N]).then_inc(feat_zeroed, 16)
                sp.wait_ge(feat_zeroed, 16)

            @block.gpsimd
            def _(pool):
                link = Link(pool, consts_made, 0)
                link.done(pool.memset(ones[:, :], 1.0))
                link.done(pool.memset(ident[:, :], 0.0))
                link.done(pool.memset(mean_c[:, :], 1.0 / C))
                link.done(pool.memset(group_mean[:, :], 1.0 / GROUP))
                link.done(pool.memset(minus_half[:, :], -0.5))
                link.done(pool.memset(win_mask[:, :, :], 0.0))
                link.done(pool.memset(tile_mask[:, :], 0.0))
                link.done(pool.memset(low_rows[:, :], 0.0))
                link.done(pool.memset(xw[:, :, :], 0.0))
                link.wait()
                pool.sem_inc(zeros_made, 1)

                def cut(ap, cmp, fill, base, pattern, mult):
                    link.done(pool.affine_select(out=ap, in_=ap, compare_op=cmp, fill=fill, base=base,
                                                 pattern=pattern, channel_multiplier=mult))
                    link.wait()

                cut(ident[:, :], ALU.not_equal, 1.0, 0, [[-1, P]], 1)
                gm = group_mean[:, :].rearrange("p (g k) -> p g k", k=GROUP)
                cut(gm, ALU.is_ge, 0.0, 0, [[-GROUP, P // GROUP], [0, GROUP]], 1)
                cut(gm, ALU.is_ge, 0.0, GROUP - 1, [[GROUP, P // GROUP], [0, GROUP]], -1)
                wm = win_mask[:, :, :]
                cut(wm, ALU.is_ge, FAR, 0, [[0, 3], [1, P]], -1)
                cut(wm, ALU.is_ge, FAR, 2 * WIN, [[0, 3], [-1, P]], 1)
                cut(win_mask[:, 0, :], ALU.is_ge, FAR, -WIN, [[1, P]], 0)
                cut(win_mask[:, 2, :], ALU.is_ge, FAR, N - (NBLK - 1) * BLK + WIN - 1, [[-1, P]], 0)
                cut(tile_mask[:, :], ALU.not_equal, -1.0, 0, [[-1, NT]], 1)
                cut(tile_mask[:, :], ALU.not_equal, -1.0, -NT, [[-1, NT]], 1)
                cut(low_rows[:, :], ALU.is_ge, -1.0, NT - 1, [[0, 1]], -1)

            @block.vector
            def _(dve):
                link = Link(dve, hi_parts_made, 0)
                for name, hi, lo, src in (
                        ("qkv_w", wh[:, :, :], wl[:, :, :], squares[:, :, 0:3 * C]),
                        ("proj_w", ph[:, :, :], pl[:, :, :], vd[:, :, 0:C]),
                        ("diffusion", mh[:, :, :, :], ml[:, :, :, :],
                         x2[:, :, :].rearrange("p c n -> p (c n)").rearrange("p (a u m) -> p a u m", a=4, u=FT))):
                    dve.wait_ge(arrived[name], 16)
                    link.done(dve.tensor_copy(hi, src))
                    link.wait()
                    dve.tensor_tensor(lo, src, hi.bitcast(F32), ALU.subtract).then_inc(lo_parts_made, 1)
                dve.wait_ge(arrived["small"], 5 * 16)
                dve.tensor_scalar(al[:, 1:2], al[:, 0:1], -1.0, 1.0, ALU.mult, ALU.add).then_inc(alphas_made, 1)
                dve.tensor_scalar(al[:, 2:3], al[:, 0:1], 2.0, -1.0, ALU.mult, ALU.add).then_inc(alphas_made, 1)
                dve.wait_ge(alphas_made, 2)
                dve.tensor_scalar(vcol[:, :], qkb[:, 4:6], al[:, 2:3], None, ALU.mult).then_inc(vcol_made, 1)
                dve.wait_ge(bias_projected, 1)
                dve.tensor_tensor(pb[:, :], bank[0][:, 0:CT], pb[:, :], ALU.add).then_inc(alphas_made, 1)
                dve.wait_ge(consts_made, 1)
                for s in range(QUAD):
                    to = stack[s][SHIFT:P, 1, :].rearrange("p (t n) -> p t n", t=NT)
                    link.done(dve.tensor_copy(to, ones[SHIFT:P, :].unsqueeze(1).broadcast_to([P - SHIFT, NT, P])))

            @block.tensor
            def _(pe):
                pe.wait_ge(vcol_made, 1)
                pe.wait_ge(arrived["proj_w"], 16)
                for m in range(CT):
                    for k in range(CT):
                        last = pe.matmul(bank[0][:, m:m + 1], vd[:, k, m * P:(m + 1) * P], vcol[:, k:k + 1],
                                         start=k == 0, stop=k == CT - 1)
                last.then_inc(bias_projected, 1)

        def max_keys():
            keys = ([], [])
            for pair in range(PAIRS):
                for u in range(UNITS):
                    if u == TURN_AT:
                        keys[0].append(("turn", 2 * pair))
                    if u == LAST_TURN_AT:
                        keys[1].append(("turn", 2 * pair + 1))
                    for r in ROWS[pair - 1][u]:
                        for half in range(2):
                            keys[half].append(("rows", 2 * pair + r // NT, r % NT))
            return keys

        def score_keys():
            keys = ([], [])
            for g in range(4):
                keys[g % 2].append(("v", g))
            for a in range(4):
                keys[a % 2].append(("fold", a))
            for c in range(CT):
                for s in range(2):
                    keys[s].append(("diffuse", c, s))
            for n in range(ALL_UNITS):
                for ab in range(2):
                    keys[ab].append(("score", n // UNITS, n % UNITS))
            return keys

        def post_keys(stages):
            keys = [[("proj", half) for half in range(2)] for m in range(CT)]
            for n in sorted(stages):
                for stage, (j, *half) in stages[n]:
                    if stage in ("mean", "spread"):
                        keys[half[0]].append((stage, j))
                    elif stage == "project_k":
                        keys[j % 2].append(("kq", j))
                    elif stage == "project_v":
                        keys[(j + 1) % 2].append(("wv", j))
                    elif stage == "variance":
                        keys[0].append(("var", j))
                    else:
                        keys[j % 2].extend([({"scores": "ws", "turn": "wt", "values": "wo"}[stage], j)] if stage != "project_q" else [])
            return keys

        def ring(name, first, keys, last_keys=(None, None)):
            return [Uses(sem(f"{name}{k}_ready"), sem(f"{name}{k}_free"), bank[first + k], keys[k], last_keys[k])
                    for k in range(2)]

        M = ring("max", 0, max_keys())
        T = ring("score", 2, score_keys())
        O = bank[4:6]
        K = [Uses(sem(f"quad{k}_ready"), sem(f"quad{k}_free"), O[k], keys)
             for k, keys in enumerate((["means", (0, *QK[3])], [(0, *j) for j in QK[:3]] + [(1, *j) for j in QK]))]
        Q = ring("post", 6, post_keys(POST["pe"]), post_keys(LAST_POST["pe"]))

        stats_made = sem("stats_made")
        feat_asked = sem("feat_asked")
        gstat_made = sem("gstat_made")
        gvar_made = sem("gvar_made")
        grstd_made = sem("grstd_made")
        xn_made = sem("xn_made")
        xh_made = sem("xh_made")
        xl_made = sem("xl_made")
        fold_made = sem("fold_made")
        fh_made = sem("fh_made")
        fl_made = sem("fl_made")
        qkh_made = sem("qkh_made")
        stacked = [sem(f"stacked{s}") for s in range(QUAD)]
        vfh_made = sem("vfh_made")
        vd_made = sem("vd_made")
        rowmax_made = sem("rowmax_made")
        shift_made = sem("shift_made")
        prob_used = sem("prob_used")
        attended_out = sem("attended_out")
        scaled_made = sem("scaled_made")
        mix_made = sem("mix_made")
        mixh_made = sem("mixh_made")
        mixl_made = sem("mixl_made")
        x_again = sem("x_again")
        sq_made = sem("sq_made")
        sq_summed = sem("sq_summed")
        rstd_made = sem("rstd_made")
        diag_made = sem("diag_made")
        neg_made = sem("neg_made")
        win_max_made = sem("win_max_made")
        win_den_made = sem("win_den_made")
        wexp_made = sem("wexp_made")
        wprob_made = sem("wprob_made")
        t_stored = sem("t_stored")
        n_stored = sem("n_stored")
        feat_added = sem("feat_added")
        feat_done = sem("feat_done")
        feat_in = sem("feat_in")
        logits_made = sem("logits_made")
        logits_out = sem("logits_out")
        w_in = [sem(f"expert_w_in{r}") for r in range(4)]
        w_hi, w_lo = sem("expert_w_hi"), sem("expert_w_lo")
        inverted = sem("inverted_sums")
        dve_front, dve_heads = (sem(f"dve_{k}_chain") for k in ("norm", "shift"))
        rows_folded = sem("rows_folded")
        pool_unfold = sem("pool_unfold_chain")

        def unit_of(u):
            return u // NT, u % NT

        def half_leaving(n):
            pair, u = divmod(n, UNITS)
            if u not in DRAIN_AT or (DRAIN_AT[u] and not pair):
                return None
            return 2 * pair - DRAIN_AT[u]

        def next_pair(b, pair):
            return (b, 2 * pair + 2) if pair + 1 < PAIRS else (b + 1, 0)

        def mix_on(eng, b, quad, half):
            n = slice(half * HALF, (half + 1) * HALF)
            before = b * 4 + quad * 2 + half
            eng.wait_ge(mix_made, FREE + before)
            eng.wait_ge(attended_out, FREE + 2 * (b * HALVES + 4 * quad + 2 + half + 1))
            eng.wait_ge(inverted, (before + 1) * RECIPS)
            eng.tensor_tensor(att[:, n], att[:, n], den[:, n], ALU.mult).then_inc(scaled_made, 1)
            eng.wait_ge(scaled_made, before + 1)
            eng.wait_ge(vd_made, b * 4 + 2 * (quad + 1))
            eng.tensor_tensor(vd[:, quad, n], att[:, n], vd[:, quad, n], ALU.add).then_inc(mix_made, 1)

        def mix_lo_on(eng, b, quad, half):
            n = slice(half * HALF, (half + 1) * HALF)
            before = b * 4 + quad * 2 + half
            eng.wait_ge(mixh_made, before + 1)
            eng.wait_ge(mixl_made, FREE + before)
            eng.tensor_tensor(fl[:, quad, n], vd[:, quad, n], fh[:, quad, n].bitcast(F32), ALU.subtract).then_inc(mixl_made, 1)

        def first_key(j):
            return j * BLK + 4 - WIN

        def block_size(j):
            return min(BLK, N - j * BLK)

        block = ctx.enter_context(nc.Block())

        @block.sync
        def _(sp):
            def load(b):
                sp.dma_start(xin[:, :, :], x_v[b]).then_inc(x_landed, 16)

            def stack_up(b, quad, s):
                rows = slice(HD * s, HD * (s + 1))
                for to, parts in ((0, slice(1, 3)), (1, slice(0, 3, 2)), (2, slice(1, 4, 2))):
                    sp.dma_start(stack[s][to * HD:(to + 1) * HD, :, :].bitcast(F32), qk[rows, parts, :].bitcast(F32))\
                        .then_inc(stacked[s], 16)

            def turn(b, post, ahead):
                if ahead:
                    T[1].wait_drained(sp, b, ("fold", 3))
                    load(b + 1)
                for pair in range(2):
                    T[1].wait_drained(sp, b, ("score", pair, UNITS - 1))
                    for s in (2 * pair, 2 * pair + 1):
                        stack_up(b, 1, s)
                for pair in range(2, PAIRS):
                    if ahead:
                        T[1].wait_drained(sp, b, ("score", pair, UNITS - 1))
                        for s in (2 * pair - QUAD, 2 * pair - QUAD + 1):
                            stack_up(b + 1, 0, s)
                    if post and pair == 2:
                        Q[(NBLK - 1) % 2].wait_drained(sp, b - 1, ("wo", NBLK - 1))
                        sp.dma_start(t_d[b - 1], x2[:, :, :]).then_inc(t_stored, 16)
                if post:
                    Q[1].wait_drained(sp, b - 1, ("spread", 1))
                    sp.dma_start(n_d[b - 1], xw[:, :, 4:4 + N]).then_inc(n_stored, 16)
                    sp.wait_ge(t_stored, FREE_DMA + b * 16)
                sp.dma_start(x2[:, :, :], x_v[b]).then_inc(x_again, 16)

            K[0].wait_drained(sp, 0, (0, 1, 1))
            for s in range(QUAD):
                stack_up(0, 0, s)
            turn(0, False, True)
            with sp.Fori(1, B - 1) as b:
                turn(b, True, True)
            turn(B - 1, True, False)
            sp.wait_ge(mixl_made, FREE + B * 4)
            sp.dma_start(wr[:, :, :], Wr.rearrange("(c p) e -> p c e", p=P)).then_inc(feat_in, 16)
            for e in range(E):
                if e >= 4:
                    sp.wait_ge(w_lo, e - 3)
                for which in range(3):
                    sp.dma_start(stage[:, e % 4, which], experts[which, e].rearrange("(k p) o -> p k o", p=P)).then_inc(w_in[e % 4], 16)
            sp.wait_ge(feat_done, FREE + B - 1)
            sp.dma_start(feat[:, :, :], feat_d).then_inc(feat_in, 16)
            Q[(NBLK - 1) % 2].wait_drained(sp, B - 1, ("wo", NBLK - 1))
            sp.dma_start(t_d[B - 1], x2[:, :, :]).then_inc(t_stored, 16)
            Q[1].wait_drained(sp, B - 1, ("spread", 1))
            sp.dma_start(n_d[B - 1], xw[:, :, 4:4 + N]).then_inc(n_stored, 16)
            sp.wait_ge(t_stored, FREE_DMA + B * 16)
            sp.wait_ge(n_stored, FREE_DMA + B * 16)

        @block.gpsimd
        def _(pool):
            def split_normed(b, c):
                pool.wait_ge(xh_made, b * CT + c + 1)
                pool.tensor_tensor(xl[:, c, :], xin[:, c, :], xh[:, c, :].bitcast(F32), ALU.subtract).then_inc(xl_made, 1)

            def fold_lo(b, c):
                pool.wait_ge(fh_made, b * CT + c + 1)
                pool.tensor_tensor(foldl[:, c, :], xin[:, c, :], foldh[:, c, :].bitcast(F32), ALU.subtract).then_inc(fl_made, 1)

            def norm_power(b):
                pool.wait_ge(gvar_made, b + 1)
                pool.tensor_tensor(grstd[:, :], gvar[:, :], minus_half[:, 0:CT], ALU.pow).then_inc(grstd_made, 1)

            def fold_rows(b, s):
                pool.wait_ge(xn_made, (b + 1) * CT)
                grid = xin[:, :, :].rearrange("p c (y x) -> p c y x", y=H)
                pool.tensor_tensor(ysum[:, s].rearrange("p c (y x) -> p c y x", y=HH), grid[:, :, 0:HH, :],
                                   grid[:, :, H - 1:HH - 1:-1, :], (ALU.add, ALU.subtract)[s]).then_inc(rows_folded, 1)

            def fold_columns(b, s):
                pool.wait_ge(rows_folded, (b + 1) * 2)
                pool.wait_ge(xl_made, (b + 1) * CT)
                rows = ysum[:, s].rearrange("p c (y x) -> p c y x", y=HH)
                for r, op in enumerate((ALU.add, ALU.subtract)):
                    to = xin[:, :, (2 * s + r) * HH * HW:(2 * s + r + 1) * HH * HW]
                    pool.tensor_tensor(to.rearrange("p c (y x) -> p c y x", y=HH),
                                       rows[:, :, :, 0:HW], rows[:, :, :, W - 1:HW - 1:-1], op).then_inc(fold_made, 1)

            def unfold_rows(b, c):
                link = Link(pool, pool_unfold, b * 4 + 2 * c)
                for s in range(2):
                    T[s].wait_drained(pool, b, ("diffuse", c, s))
                if c:
                    pool.wait_ge(vd_made, b * 4 + 2)
                plus = ysum[:, c, 0].rearrange("p (r y x) -> p r y x", r=2, y=HH)
                minus = ysum[:, c, 1].rearrange("p (r y x) -> p r y x", r=2, y=HH)
                link.done(pool.tensor_tensor(unfold[:, :, 0:HH, :], plus, minus, ALU.add))
                link.done(pool.tensor_tensor(unfold[:, :, H - 1:HH - 1:-1, :], plus, minus, ALU.subtract))

            def unfold_columns(b, c):
                pool.wait_ge(pool_unfold, b * 4 + 2 * c + 2)
                if c == 0:
                    pool.wait_ge(mixl_made, FREE + b * 4)
                to = vd[:, c, :].rearrange("p (y x) -> p y x", y=H)
                pool.tensor_tensor(to[:, :, 0:HW], unfold[:, 0], unfold[:, 1], ALU.add).then_inc(vd_made, 1)
                pool.tensor_tensor(to[:, :, W - 1:HW - 1:-1], unfold[:, 0], unfold[:, 1], ALU.subtract).then_inc(vd_made, 1)

            def sum_squares(b, ln):
                for half in range(2):
                    n = slice(half * HALF, (half + 1) * HALF)
                    pool.wait_ge(sq_made, b * 4 + ln * 2 + half + 1)
                    pool.tensor_tensor(squares[:, 0, n], squares[:, 0, n], squares[:, 1, n], ALU.add).then_inc(sq_summed, 1)

            def layer_norm_power(b, ln):
                Q[0].wait_drained(pool, b, ("var", ln))
                pool.tensor_tensor(lnr[:, :], lnv[:, :], minus_half[:, :], ALU.pow).then_inc(rstd_made, 1)
                pool.wait_ge(rstd_made, b * 2 + ln + 1)
                pool.tensor_tensor(diag, ident[:, :].unsqueeze(1).broadcast_to([P, NT, P]),
                                   lnr[:, :].unsqueeze(2).broadcast_to([P, NT, P]), ALU.mult).then_inc(diag_made, 1)

            def sum_normed(b):
                Q[1].wait_drained(pool, b, ("spread", 1))
                pool.sem_inc(feat_asked, 1)
                pool.dma_start(feat_d, xw[:, :, 4:4 + N], accum_op=ALU.add).then_inc(feat_added, 16)
                pool.wait_ge(feat_added, (b + 1) * 16)
                pool.sem_inc(feat_done, 1)

            def turn(b, post, ahead):
                for n in range(ALL_UNITS):
                    if n in UNFOLD_ROWS_AT:
                        unfold_rows(b, UNFOLD_ROWS_AT[n])
                    if n in UNFOLD_COLUMNS_AT:
                        unfold_columns(b, UNFOLD_COLUMNS_AT[n])
                    for ln, at in enumerate((2, LAST_NORM_AT + 2)):
                        if n == at and post:
                            sum_squares(b - 1, ln)
                        if n == at + 3 and post:
                            layer_norm_power(b - 1, ln)
                    if n in MIX_AT:
                        mix_on(pool, b, *MIX_AT[n])
                    if n in MIX_LO_AT:
                        mix_lo_on(pool, b, *MIX_LO_AT[n])
                    if n == MEANS_AT + 2 and ahead:
                        norm_power(b + 1)
                    if n in XL_AT and ahead:
                        split_normed(b + 1, XL_AT[n])
                    if n in FOLD_LO_AT and ahead:
                        fold_lo(b + 1, FOLD_LO_AT[n])
                    if n in FOLD_ROWS_AT and ahead:
                        fold_rows(b + 1, FOLD_ROWS_AT[n])
                    if n in FOLD_COLUMNS_AT and ahead:
                        fold_columns(b + 1, FOLD_COLUMNS_AT[n])
                if post:
                    sum_normed(b - 1)

            for s in [u.free for u in M + T + Q + K] + [mixl_made, prob_used, mix_made, rowmax_made, shift_made,
                                                 attended_out, feat_done]:
                pool.sem_inc(s, FREE)
            for s in stacked + [n_stored, t_stored]:
                pool.sem_inc(s, FREE_DMA)
            norm_power(0)
            for c in range(CT):
                split_normed(0, c)
            for s in range(2):
                fold_rows(0, s)
            for s in range(2):
                fold_columns(0, s)
            for c in range(CT):
                fold_lo(0, c)
            turn(0, False, True)
            with pool.Fori(1, B - 1) as b:
                turn(b, True, True)
            turn(B - 1, True, False)
            sum_squares(B - 1, 0)
            layer_norm_power(B - 1, 0)
            for e in range(E):
                pool.wait_ge(w_hi, e + 1)
                pool.tensor_tensor(expert_w[1][:, e], stage[:, e % 4], expert_w[0][:, e].bitcast(F32), ALU.subtract)\
                    .then_inc(w_lo, 1)
            sum_squares(B - 1, 1)
            layer_norm_power(B - 1, 1)

        @block.tensor
        def _(pe):
            def three(out, pairs, n):
                for k, (ah, a_l, bh, bl) in enumerate(pairs):
                    for j, (l, r) in enumerate(((ah, bh), (a_l, bh), (ah, bl))):
                        last = pe.matmul(out, l, r, start=n + k == 0 and j == 0, stop=k == len(pairs) - 1 and j == 2)
                return last

            def project_qk(b, quad, which, half):
                use = K[0] if (quad, which, half) == (0, 1, 1) else K[1]
                o = slice(which * C + quad * P, which * C + (quad + 1) * P)
                n = slice(half * HALF, (half + 1) * HALF)
                use.wait_free(pe, b, (quad, which, half))
                three(use.tile[:, :], [(wh[:, k, o], wl[:, k, o], xh[:, k, n], xl[:, k, n]) for k in range(CT)], 0)\
                    .then_inc(use.ready, 1)

            def group_means(b):
                pe.wait_ge(gstat_made, b + 1)
                K[0].wait_free(pe, b, "means")
                pe.matmul(K[0].tile[:, 0:2 * CT], group_mean[:, :], gstat[:, :, :].rearrange("p a c -> p (a c)"),
                          start=True, stop=True).then_inc(K[0].ready, 1)

            def project_v(b, g):
                T[g % 2].wait_free(pe, b, ("v", g))
                for t in range(2):
                    n = slice((2 * g + t) * P, (2 * g + t + 1) * P)
                    last = three(T[g % 2].tile[:, t * C:(t + 1) * C],
                                 [(xh[:, k, n], xl[:, k, n], wh[:, k, 2 * C:], wl[:, k, 2 * C:]) for k in range(CT)], 0)
                last.then_inc(T[g % 2].ready, 1)

            def project_fold(b, a):
                if a == 0:
                    pe.wait_ge(fl_made, (b + 1) * CT)
                T[a % 2].wait_free(pe, b, ("fold", a))
                for u in range(FT):
                    n = slice((a * FT + u) * P, (a * FT + u + 1) * P)
                    last = three(T[a % 2].tile[:, u * C:(u + 1) * C],
                                 [(foldh[:, k, n], foldl[:, k, n], wh[:, k, 2 * C:], wl[:, k, 2 * C:]) for k in range(CT)], 0)
                last.then_inc(T[a % 2].ready, 1)

            def diffuse(b, c, s):
                if c == 0 and s == 0:
                    for a in (2, 3):
                        T[a % 2].wait_drained(pe, b, ("fold", a))
                T[s].wait_free(pe, b, ("diffuse", c, s))
                for r in range(2):
                    a = 2 * s + r
                    last = three(T[s].tile[:, r * HH * HW:(r + 1) * HH * HW],
                                 [(vf[0][:, a, u, c * P:(c + 1) * P], vf[1][:, a, u, c * P:(c + 1) * P],
                                   mh[:, a, u, :], ml[:, a, u, :]) for u in range(FT)], 0)
                last.then_inc(T[s].ready, 1)

            def row_scores(b, h, t):
                s = h % QUAD
                if t == 0:
                    pe.wait_ge(stacked[s], FREE_DMA + b * 96 + (h // QUAD + 1) * 48)
                for half in range(2):
                    M[half].wait_free(pe, b, ("rows", h, t))
                    pe.matmul(M[half].tile[:, :], stack[s][0:SHIFT, 0, t * P:(t + 1) * P],
                              stack[s][0:SHIFT, 1, half * HALF:(half + 1) * HALF], start=True, stop=True)\
                        .then_inc(M[half].ready, 1)

            def turn(b, h):
                pe.wait_ge(rowmax_made, FREE + b * NH + h + 1)
                M[h % 2].wait_free(pe, b, ("turn", h))
                pe.transpose(M[h % 2].tile[0:16, 0:P], mx2[:, h % 2].rearrange("p a t -> p (a t)"), ident[:, :])\
                    .then_inc(M[h % 2].ready, 1)

            def attend(b, pair, u, ahead):
                half, t = unit_of(u)
                k = 2 * pair + half
                for ab in range(2):
                    T[ab].wait_drained(pe, b, ("score", pair, u))
                if t == 0:
                    pe.wait_ge(attended_out, FREE + 2 * (b * HALVES + max(k - 1, 0)))
                    if k == 1:
                        K[1].wait_drained(pe, b, (1, 1, 1))
                    if k == 2 and ahead:
                        K[0].wait_drained(pe, b + 1, "means")
                    if k == 5 and ahead:
                        K[1].wait_drained(pe, b + 1, (0, 1, 0))
                for i in range(2):
                    for ab in range(2):
                        h = 2 * pair + ab
                        col = (ab + 2 * ((pair + i) % 2)) * HD
                        last = pe.matmul(O[half][col:col + HD, :], ones[:, 0:HD] if i else v[:, t, h * HD:(h + 1) * HD],
                                         prob[:, u % 4, ab, :], start=t == 0, stop=t == NT - 1, tile_position=(0, col))
                last.then_inc(prob_used, 1)

            def project_mix(b):
                for half in range(2):
                    pe.wait_ge(mixl_made, FREE + b * 4 + half + 3)
                    n = slice(half * HALF, (half + 1) * HALF)
                    for m in range(CT):
                        o = slice(m * P, (m + 1) * P)
                        Q[m].wait_free(pe, b, ("proj", half))
                        three(Q[m].tile[:, :], [(ph[:, k, o], pl[:, k, o], fh[:, k, n], fl[:, k, n]) for k in range(CT)], 0)\
                            .then_inc(Q[m].ready, 1)

            def scores(b, pair, u):
                half, t = unit_of(u)
                for ab in range(2):
                    s = (2 * pair + ab) % QUAD
                    if u == 0:
                        pe.wait_ge(shift_made, FREE + b * NH + 2 * pair + ab + 1)
                    T[ab].wait_free(pe, b, ("score", pair, u))
                    pe.matmul(T[ab].tile[:, :], stack[s][0:STACK, 1, t * P:(t + 1) * P],
                              stack[s][0:STACK, 0, half * HALF:(half + 1) * HALF], start=True, stop=True)\
                        .then_inc(T[ab].ready, 1)

            def post(b, n, stages=POST["pe"]):
                for stage, j in stages.get(n, []):
                    {"mean": mean, "variance": variance, "spread": spread, "project_k": window_project_k,
                     "project_q": window_project_q, "project_v": window_project_v,
                     "scores": window_scores, "turn": window_turn, "values": window_values}[stage](b, *j)

            def turn_of_loop(b, with_post, ahead):
                if with_post:
                    for j in range(4):
                        project_v(b, j)
                    for j in range(4):
                        project_fold(b, j)
                    project_mix(b - 1)
                    for j in range(4):
                        diffuse(b, j // 2, j % 2)
                for g in (2, 3):
                    T[g % 2].wait_drained(pe, b, ("v", g))
                for n in range(ALL_UNITS):
                    pair, u = divmod(n, UNITS)
                    if n == 3 * UNITS - 1 and ahead:
                        K[0].wait_drained(pe, b + 1, (0, 1, 1))
                    if pair + 1 < PAIRS or ahead:
                        to = next_pair(b, pair)
                        for r in ROWS[pair][u][:-1]:
                            row_scores(to[0], to[1] + r // NT, r % NT)
                    scores(b, pair, u)
                    if u:
                        attend(b, pair, u - 1, ahead)
                    if pair + 1 < PAIRS or ahead:
                        to = next_pair(b, pair)
                        if u == TURN_AT:
                            turn(*to)
                        if u == LAST_TURN_AT:
                            turn(to[0], to[1] + 1)
                        for r in ROWS[pair][u][-1:]:
                            row_scores(to[0], to[1] + r // NT, r % NT)
                    if n in SECOND_QUAD_AT:
                        if n == 0:
                            pe.wait_ge(attended_out, FREE + 2 * b * HALVES)
                        project_qk(b, 1, *SECOND_QUAD_AT[n])
                    if ahead:
                        if n == MEANS_AT:
                            pe.wait_ge(attended_out, FREE + 2 * (b * HALVES + 1))
                            group_means(b + 1)
                        if n in FIRST_QUAD_AT:
                            if FIRST_QUAD_AT[n] == (0, 0):
                                pe.wait_ge(xl_made, (b + 2) * CT)
                                pe.wait_ge(attended_out, FREE + 2 * (b * HALVES + 4))
                            if FIRST_QUAD_AT[n] == (1, 1):
                                pe.wait_ge(attended_out, FREE + 2 * (b * HALVES + 5))
                            project_qk(b + 1, 0, *FIRST_QUAD_AT[n])
                    if with_post:
                        post(b - 1, n)
                    if u == UNITS - 1:
                        attend(b, pair, u, ahead)

            def mean(b, ln, half):
                if ln == 0:
                    for m in range(CT):
                        Q[m].wait_drained(pe, b, ("proj", half))
                elif half == 0:
                    Q[(NBLK - 1) % 2].wait_drained(pe, b, ("wo", NBLK - 1))
                Q[half].wait_free(pe, b, ("mean", ln))
                for c in range(CT):
                    last = pe.matmul(Q[half].tile[:, :], mean_c[:, :], x2[:, c, half * HALF:(half + 1) * HALF],
                                     start=c == 0, stop=c == CT - 1)
                last.then_inc(Q[half].ready, 1)

            def variance(b, ln, _):
                pe.wait_ge(sq_summed, b * 4 + ln * 2 + 2)
                Q[0].wait_free(pe, b, ("var", ln))
                for t in range(NT):
                    last = pe.matmul(Q[0].tile[:, t:t + 1], squares[:, 0, t * P:(t + 1) * P], mean_c[:, 0:1],
                                     start=True, stop=True)
                last.then_inc(Q[0].ready, 1)

            def spread(b, ln, half):
                if half == 0:
                    pe.wait_ge(diag_made, b * 2 + ln + 1)
                Q[half].wait_free(pe, b, ("spread", ln))
                pe.matmul(Q[half].tile[:, :], ones[:, :], sq[:, half * HALF:(half + 1) * HALF], start=True, stop=True)\
                    .then_inc(Q[half].ready, 1)

            def window_project(b, j, col, which, start, n):
                for m in range(CT):
                    for k in range(CT):
                        last = pe.matmul(Q[j % 2].tile[:, col + m * P:col + m * P + n], w1[:, which, k, m * P:(m + 1) * P],
                                         xw[:, k, start:start + n], start=k == 0, stop=k == CT - 1)
                return last

            def window_project_k(b, j):
                if j == 0:
                    Q[0].wait_drained(pe, b, ("spread", 0))
                Q[j % 2].wait_free(pe, b, ("kq", j))
                window_project(b, j, 0, 1, first_key(j), block_size(j) + 2 * WIN)

            def window_project_q(b, j):
                window_project(b, j, 2 * P, 0, first_key(j) + WIN, block_size(j)).then_inc(Q[j % 2].ready, 1)

            def window_project_v(b, j):
                mm = block_size(j) + 2 * WIN
                k0 = first_key(j)
                if j == 0:
                    Q[1].wait_drained(pe, b, ("spread", 0))
                bank_v = Q[(j + 1) % 2]
                bank_v.wait_free(pe, b, ("wv", j))
                for k in range(CT):
                    last = pe.matmul(bank_v.tile[0:mm, 0:C], xw[:, k, k0:k0 + mm], w1[:, 2, k, :], start=k == 0, stop=k == CT - 1)
                last.then_inc(bank_v.ready, 1)

            def window_scores(b, j):
                nn = block_size(j)
                mm = nn + 2 * WIN
                Q[j % 2].wait_drained(pe, b, ("kq", j))
                for k in range(CT):
                    last = pe.matmul(Q[j % 2].tile[0:nn, 0:mm], qb[:, k, 0:nn], kb[:, k, 0:mm], start=k == 0, stop=k == CT - 1)
                last.then_inc(Q[j % 2].ready, 1)

            def window_turn(b, j):
                nn = block_size(j)
                mm = nn + 2 * WIN
                pe.wait_ge(wprob_made, b * NBLK + j + 1)
                Q[j % 2].wait_free(pe, b, ("wt", j))
                pe.transpose(Q[j % 2].tile[0:mm, 0:nn], pm[0:nn, 0:mm], ident[0:nn, 0:nn]).then_inc(Q[j % 2].ready, 1)

            def window_values(b, j):
                nn = block_size(j)
                mm = nn + 2 * WIN
                Q[j % 2].wait_drained(pe, b, ("wt", j))
                Q[j % 2].wait_free(pe, b, ("wo", j))
                for m in range(CT):
                    last = pe.matmul(Q[j % 2].tile[:, m * P:m * P + nn], vb[0:mm, m * P:(m + 1) * P], pt[0:mm, 0:nn],
                                     start=True, stop=True)
                last.then_inc(Q[j % 2].ready, 1)

            group_means(0)
            pe.wait_ge(xl_made, CT)
            for j in QK:
                project_qk(0, 0, *j)
            for u in range(UNITS):
                if u == TURN_AT:
                    turn(0, 0)
                if u == LAST_TURN_AT:
                    turn(0, 1)
                for r in ROWS[PAIRS - 1][u]:
                    row_scores(0, r // NT, r % NT)
                if u // 4 < 3:
                    {0: project_v, 1: project_fold, 2: lambda b, j: diffuse(b, j // 2, j % 2)}[u // 4](0, u % 4)
            turn_of_loop(0, False, True)
            with pe.Fori(1, B - 1) as b:
                turn_of_loop(b, True, True)
            turn_of_loop(B - 1, True, False)
            project_mix(B - 1)

            def logits_of(part, tokens):
                for t in range(NT):
                    for c in range(CT):
                        last = pe.matmul(M[part].tile[:, t * E:(t + 1) * E], tokens[:, c, t * P:(t + 1) * P], wr[:, c, :],
                                         start=c == 0, stop=c == CT - 1)
                return last

            for n in sorted(LAST_POST["pe"]):
                if n == EARLY_LOGITS_AT:
                    pe.wait_ge(feat_in, 2 * 16)
                    logits_of(0, feat)
                post(B - 1, n, LAST_POST["pe"])
            for half in range(2):
                Q[half].wait_drained(pe, B - 1, ("spread", 1))
            last = logits_of(1, xw[:, :, 4:4 + N])
            last.then_inc(logits_made, 1)

        @block.scalar
        def _(act):
            def qk_hi(b, quad, which, half):
                if (which, half) == (0, 0):
                    for s in range(QUAD):
                        act.wait_ge(stacked[s], FREE_DMA + b * 96 + quad * 48)
                use = K[0] if (quad, which, half) == (0, 1, 1) else K[1]
                use.wait_ready(act, b, (quad, which, half))
                col = 2 * which + quad
                act.activation(qk[:, 1 + which, half * HALF:(half + 1) * HALF], use.tile[:, :], ACT.Identity,
                               bias=qkb[:, col:col + 1]).then_inc(qkh_made, 1)

            def norm(b, c):
                act.wait_ge(dve_front, (b + 1) * FRONT_LINKS)
                act.activation(xin[:, c, :], xin[:, c, :], ACT.Identity, scale=grstd[:, c:c + 1],
                               bias=gbias[:, c:c + 1]).then_inc(xn_made, 1)

            def split_normed(b, c):
                act.wait_ge(xn_made, b * CT + c + 1)
                act.activation(xh[:, c, :], xin[:, c, :], ACT.Copy).then_inc(xh_made, 1)

            def copy_v(b, g):
                if g == 0:
                    act.wait_ge(prob_used, FREE + b * ALL_UNITS)
                T[g % 2].wait_ready(act, b, ("v", g))
                act.activation(v[:, 2 * g:2 * g + 2, :].rearrange("p t o -> p (t o)"), T[g % 2].tile[:, :], ACT.Copy)\
                    .then_inc(T[g % 2].free, 1)

            def fold_hi(b, c):
                act.wait_ge(fold_made, (b + 1) * 4)
                act.activation(foldh[:, c, :], xin[:, c, :], ACT.Copy).then_inc(fh_made, 1)

            def vf_hi(b, a):
                if a == 0:
                    act.wait_ge(prob_used, FREE + b * ALL_UNITS)
                T[a % 2].wait_ready(act, b, ("fold", a))
                act.activation(vf[0][:, a].rearrange("p u o -> p (u o)"), T[a % 2].tile[:, :], ACT.Copy).then_inc(vfh_made, 1)

            def copy_diffused(b, c, s):
                T[s].wait_ready(act, b, ("diffuse", c, s))
                act.activation(ysum[:, c, s], T[s].tile[:, :], ACT.Copy, scale=al[:, 1:2]).then_inc(T[s].free, 1)

            def drain_attended(b, k):
                pair, half = divmod(k, 2)
                n = slice(half * HALF, (half + 1) * HALF)
                act.wait_ge(prob_used, FREE + (b * HALVES + k + 1) * NT)
                if pair % 2 == 0:
                    act.wait_ge(mix_made, FREE + b * 4 + (1 + half if pair else 0))
                here, other = (slice(2 * HD * q, 2 * HD * (q + 1)) for q in (pair % 2, (pair + 1) % 2))
                act.activation(den[here, n], O[half][other, :], ACT.Copy).then_inc(attended_out, 1)
                act.activation(att[here, n], O[half][here, :], ACT.Copy, scale=al[here, 0:1]).then_inc(attended_out, 1)

            def mix_hi(b, quad, half):
                act.wait_ge(mix_made, FREE + b * 4 + quad * 2 + half + 1)
                n = slice(half * HALF, (half + 1) * HALF)
                act.activation(fh[:, quad, n], vd[:, quad, n], ACT.Copy).then_inc(mixh_made, 1)

            def exps(b, pair, u):
                act.wait_ge(prob_used, FREE + b * ALL_UNITS + max(pair * UNITS + u - 3, 0))
                for ab in range(2):
                    T[ab].wait_ready(act, b, ("score", pair, u))
                    act.activation(prob[:, u % 4, ab, :], T[ab].tile[:, :], ACT.Exp, scale=HEAD_SCALE)\
                        .then_inc(T[ab].free, 1)

            def post(b, who, n, stages=POST):
                for stage, j in stages[who].get(n, []):
                    {"square": square, "project": window_project, "project_v": window_project_v, "exp": window_exp, "turn": window_turn}[stage](b, *j)

            def turn_of_loop(b, with_post, ahead):
                if with_post:
                    drain_attended(b - 1, HALVES - 1)
                    for j in range(4):
                        copy_v(b, j)
                    mix_hi(b - 1, 1, 0)
                    for j in range(4):
                        vf_hi(b, j)
                        if j == 0:
                            mix_hi(b - 1, 1, 1)
                    for j in range(4):
                        copy_diffused(b, j // 2, j % 2)
                for n in range(ALL_UNITS):
                    pair, u = divmod(n, UNITS)
                    if n - 1 in SECOND_QUAD_AT:
                        qk_hi(b, 1, *SECOND_QUAD_AT[n - 1])
                    if n - 1 in FIRST_QUAD_AT and ahead:
                        qk_hi(b + 1, 0, *FIRST_QUAD_AT[n - 1])
                    if n in MIX_HI_AT:
                        mix_hi(b, *MIX_HI_AT[n])
                    if with_post:
                        post(b - 1, "act_early", n)
                    exps(b, pair, u)
                    k = half_leaving(n)
                    if k is not None:
                        drain_attended(b, k)
                    if ahead:
                        if n - 1 in NORMED_AT:
                            split_normed(b + 1, NORMED_AT[n - 1])
                        if n in NORMED_AT:
                            norm(b + 1, NORMED_AT[n])
                        if n in FOLD_HI_AT:
                            fold_hi(b + 1, FOLD_HI_AT[n])
                    if with_post:
                        post(b - 1, "act", n)

            def square(b, ln, half):
                Q[half].wait_drained(act, b, ("mean", ln))
                n = slice(half * HALF, (half + 1) * HALF)
                act.activation(squares[:, :, n], xw[:, :, 4 + half * HALF:4 + (half + 1) * HALF], ACT.Square)\
                    .then_inc(sq_made, 1)

            def window_project(b, j):
                nn = block_size(j)
                mm = nn + 2 * WIN
                Q[j % 2].wait_ready(act, b, ("kq", j))
                for col, which, to, n in ((0, 1, kb, mm), (2 * P, 0, qb, nn)):
                    for m in range(CT):
                        last = act.activation(to[:, m, 0:n], Q[j % 2].tile[:, col + m * P:col + m * P + n], ACT.Identity,
                                              bias=wb[:, which, m:m + 1])
                last.then_inc(Q[j % 2].free, 1)

            def window_project_v(b, j):
                mm = block_size(j) + 2 * WIN
                bank_v = Q[(j + 1) % 2]
                bank_v.wait_ready(act, b, ("wv", j))
                act.activation(vb[0:mm, :], bank_v.tile[0:mm, 0:C], ACT.Copy).then_inc(bank_v.free, 1)

            def window_exp(b, j):
                nn = block_size(j)
                mm = nn + 2 * WIN
                act.wait_ge(neg_made, b * NBLK + j + 1)
                act.activation(pm[0:nn, 0:mm], sm[0:nn, 0:mm], ACT.Exp, scale=WIN_SCALE, bias=wneg[0:nn, 1:2],
                               accum_out=wden[0:nn, 0:1]).then_inc(wexp_made, 1)

            def window_turn(b, j):
                nn = block_size(j)
                mm = nn + 2 * WIN
                Q[j % 2].wait_ready(act, b, ("wt", j))
                act.activation(pt[0:mm, 0:nn], Q[j % 2].tile[0:mm, 0:nn], ACT.Copy).then_inc(Q[j % 2].free, 1)

            def weights_hi(e):
                if e == 0:
                    Q[1].wait_ready(act, B - 1, ("proj", 1))
                act.wait_ge(w_in[e % 4], (e // 4 + 1) * 3 * 16)
                act.activation(expert_w[0][:, e], stage[:, e % 4], ACT.Copy).then_inc(w_hi, 1)

            for c in range(CT):
                norm(0, c)
            for c in range(CT):
                split_normed(0, c)
            for j in QK:
                qk_hi(0, 0, *j)
            for c in range(CT):
                fold_hi(0, c)
            for j in range(4):
                copy_v(0, j)
            for j in range(4):
                vf_hi(0, j)
            for j in range(4):
                copy_diffused(0, j // 2, j % 2)
            turn_of_loop(0, False, True)
            with act.Fori(1, B - 1) as b:
                turn_of_loop(b, True, True)
            turn_of_loop(B - 1, True, False)
            drain_attended(B - 1, HALVES - 1)
            for half in range(2):
                mix_hi(B - 1, 1, half)
            for n in sorted(LAST_POST["act"]):
                post(B - 1, "act", n, LAST_POST)
                if n in WEIGHTS_AT:
                    weights_hi(WEIGHTS_AT[n])

        @block.vector
        def _(dve):
            def qk_lo(b, quad, which, half):
                use = K[0] if (quad, which, half) == (0, 1, 1) else K[1]
                n = slice(half * HALF, (half + 1) * HALF)
                dve.wait_ge(qkh_made, b * 8 + quad * 4 + which * 2 + half + 1)
                col = 2 * which + quad
                dve.scalar_tensor_tensor(qk[:, 3 * which, n], use.tile[:, :], qkb[:, col:col + 1],
                                         qk[:, 1 + which, n].bitcast(F32), ALU.add, ALU.subtract).then_inc(use.free, 1)

            def channel_stats(b, c):
                link = norm_link(b, 2 * c)
                if c == 0:
                    dve.wait_ge(x_landed, (b + 1) * 16)
                for half in range(2):
                    link.done(dve.bn_stats(stats[:, c, half, :], xin[:, c, half * HALF:(half + 1) * HALF]))

            def channel_means(b):
                link = norm_link(b, 2 * CT)
                link.wait()
                dve.sem_inc(stats_made, 1)
                for c in range(CT):
                    link.done(dve.bn_aggr(aggr[:, c, :], stats[:, c, :, :].rearrange("p h s -> p (h s)")))
                link.wait()
                link.done(dve.tensor_copy(gstat[:, 0, :], aggr[:, :, 0]))
                link.done(dve.tensor_tensor(gtmp[:, 0, :], aggr[:, :, 0], aggr[:, :, 0], ALU.mult))
                link.wait()
                dve.tensor_tensor(gstat[:, 1, :], gtmp[:, 0, :], aggr[:, :, 1], ALU.add).then_inc(gstat_made, 1)
                assert link.n == 8

            def norm_link(b, n=0):
                link = Link(dve, dve_front, b * FRONT_LINKS)
                link.n = n
                return link

            def group_stats(b):
                link = norm_link(b, 8)
                K[0].wait_ready(dve, b, "means")
                dve.tensor_copy(gmean[:, :, :], K[0].tile[:, 0:2 * CT].rearrange("p (a c) -> p a c", a=2)).then_inc(K[0].free, 1)
                K[0].wait_drained(dve, b, "means")
                link.done(dve.tensor_tensor(gtmp[:, 0, :], gmean[:, 0, :], gmean[:, 0, :], ALU.mult))
                link.wait()
                link.done(dve.tensor_tensor(gtmp[:, 1, :], gmean[:, 1, :], gtmp[:, 0, :], ALU.subtract))
                link.wait()
                dve.tensor_scalar(gvar[:, :], gtmp[:, 1, :], 0.0, EPS, ALU.max, ALU.add).then_inc(gvar_made, 1)
                assert link.n == 10

            def group_offset(b):
                link = norm_link(b, 10)
                dve.wait_ge(grstd_made, b + 1)
                link.done(dve.scalar_tensor_tensor(gbias[:, :], gmean[:, 0, :], -1.0, grstd[:, :], ALU.mult, ALU.mult))
                assert link.n == FRONT_LINKS

            def vf_lo(b, a):
                dve.wait_ge(vfh_made, b * 4 + a + 1)
                dve.tensor_tensor(vf[1][:, a].rearrange("p u o -> p (u o)"), T[a % 2].tile[:, :],
                                  vf[0][:, a].rearrange("p u o -> p (u o)").bitcast(F32), ALU.subtract)\
                    .then_inc(T[a % 2].free, 1)

            def row_max(b, h, t):
                for half in range(2):
                    M[half].wait_ready(dve, b, ("rows", h, t))
                    if t == 0 and half == 0:
                        dve.wait_ge(rowmax_made, FREE + b * NH + h)
                    dve.tensor_reduce(mx[:, h % 2, t, half:half + 1], M[half].tile[:, :], AXX, ALU.max)\
                        .then_inc(M[half].free, 1)
                if t == NT - 1:
                    for half in range(2):
                        M[half].wait_drained(dve, b, ("rows", h, t))
                    both = [mx[:, h % 2, :, half].unsqueeze(1).broadcast_to([P, 2, NT]) for half in range(2)]
                    dve.tensor_tensor(mx2[:, h % 2], both[0], both[1], ALU.max).then_inc(rowmax_made, 1)

            def shift(b, h):
                link = Link(dve, dve_heads, b * HEAD_LINKS + h)
                tile = M[h % 2].tile[0:16, 0:P]
                M[h % 2].wait_ready(dve, b, ("turn", h))
                dve.wait_ge(shift_made, FREE + b * NH + h)
                link.done(dve.tensor_copy(th[:, :], tile))
                link.wait()
                dve.scalar_tensor_tensor(td[:, :], th[:, :].bitcast(F32), low_rows[:, 0:1], tile, ALU.mult, ALU.add)\
                    .then_inc(M[h % 2].free, 1)
                M[h % 2].wait_drained(dve, b, ("turn", h))
                to = stack[h % QUAD][SHIFT:STACK, 0, :].rearrange("p (t n) -> p t n", t=NT)
                dve.tensor_tensor(to, td[:, :].unsqueeze(1).broadcast_to([16, NT, P]),
                                  tile_mask[:, :].unsqueeze(2).broadcast_to([16, NT, P]), ALU.mult).then_inc(shift_made, 1)

            def invert_sums(b, quad, half, piece):
                n = slice(half * HALF + piece * RECIP, half * HALF + (piece + 1) * RECIP)
                if piece == 0:
                    dve.wait_ge(attended_out, FREE + 2 * (b * HALVES + 4 * quad + 2 + half + 1))
                dve.reciprocal(den[:, n], den[:, n]).then_inc(inverted, 1)

            def residual(b):
                for half in range(2):
                    n = slice(half * HALF, (half + 1) * HALF)
                    for m in range(CT):
                        Q[m].wait_ready(dve, b, ("proj", half))
                        if half == 0 and m == 0:
                            dve.wait_ge(x_again, (b + 1) * 16)
                        dve.scalar_tensor_tensor(x2[:, m, n], Q[m].tile[:, :], pb[:, m:m + 1], x2[:, m, n], ALU.add, ALU.add)\
                            .then_inc(Q[m].free, 1)

            def post(b, who, n, stages=POST):
                for stage, j in stages[who].get(n, []):
                    {"deviation": deviation, "variance": variance, "normed": normed,
                     "mask": window_mask, "probs": window_probs,
                     "residual": window_residual}[stage](b, *j)

            def turn_of_loop(b, with_post, ahead):
                if with_post:
                    for piece in range(RECIPS):
                        invert_sums(b - 1, 1, 1, piece)
                    mix_on(dve, b - 1, 1, 1)
                    mix_lo_on(dve, b - 1, 1, 0)
                    for j in range(4):
                        vf_lo(b, j)
                        if j == 0:
                            mix_lo_on(dve, b - 1, 1, 1)
                    residual(b - 1)
                for n in range(ALL_UNITS):
                    pair, u = divmod(n, UNITS)
                    if pair + 1 < PAIRS or ahead:
                        to = next_pair(b, pair)
                        for r in ROWS[pair][u][:-1]:
                            row_max(to[0], to[1] + r // NT, r % NT)
                    if n - 1 in SECOND_QUAD_AT:
                        qk_lo(b, 1, *SECOND_QUAD_AT[n - 1])
                    if n - 1 in FIRST_QUAD_AT and ahead:
                        qk_lo(b + 1, 0, *FIRST_QUAD_AT[n - 1])
                    if n == MEANS_AT + 1 and ahead:
                        group_stats(b + 1)
                    for k in range(RECIPS):
                        if n - k in RECIP_AT:
                            invert_sums(b, *RECIP_AT[n - k], k)
                    if with_post:
                        post(b - 1, "dve_early", n)
                    if pair + 1 < PAIRS or ahead:
                        to = next_pair(b, pair)
                        if u == TURN_AT:
                            shift(*to)
                        if u == LAST_TURN_AT:
                            shift(to[0], to[1] + 1)
                        for r in ROWS[pair][u][-1:]:
                            row_max(to[0], to[1] + r // NT, r % NT)
                    if ahead:
                        if n == STATS_AT:
                            for c in range(CT):
                                channel_stats(b + 1, c)
                            channel_means(b + 1)
                        if n == MEANS_AT + 2:
                            group_offset(b + 1)
                    if with_post:
                        post(b - 1, "dve", n)

            def deviation(b, ln, half):
                n = slice(half * HALF, (half + 1) * HALF)
                to = xw[:, :, 4 + half * HALF:4 + (half + 1) * HALF]
                Q[half].wait_ready(dve, b, ("mean", ln))
                if ln == 0 and half == 0:
                    dve.wait_ge(n_stored, FREE_DMA + b * 16)
                    dve.wait_ge(feat_done, FREE + b)
                dve.tensor_tensor(to, x2[:, :, n], Q[half].tile[:, :].unsqueeze(1).broadcast_to([P, CT, HALF]),
                                  ALU.subtract).then_inc(Q[half].free, 1)

            def variance(b, ln, _):
                Q[0].wait_ready(dve, b, ("var", ln))
                dve.tensor_scalar(lnv[:, :], Q[0].tile[:, 0:NT], EPS, None, ALU.add).then_inc(Q[0].free, 1)

            def normed(b, ln, half):
                to = xw[:, :, 4 + half * HALF:4 + (half + 1) * HALF]
                Q[half].wait_ready(dve, b, ("spread", ln))
                dve.tensor_tensor(to, to, Q[half].tile[:, :].unsqueeze(1).broadcast_to([P, CT, HALF]), ALU.mult)\
                    .then_inc(Q[half].free, 1)

            def window_mask(b, j):
                nn = block_size(j)
                mm = nn + 2 * WIN
                kind = 0 if j == 0 else 2 if j == NBLK - 1 else 1
                Q[j % 2].wait_ready(dve, b, ("ws", j))
                dve.tensor_tensor(sm[0:nn, 0:mm], Q[j % 2].tile[0:nn, 0:mm], win_mask[0:nn, kind, 0:mm], ALU.add).then_inc(Q[j % 2].free, 1)
                Q[j % 2].wait_drained(dve, b, ("ws", j))
                dve.tensor_reduce(wneg[0:nn, 0:1], sm[0:nn, 0:mm], AXX, ALU.max).then_inc(win_max_made, 1)
                dve.wait_ge(win_max_made, b * NBLK + j + 1)
                dve.tensor_scalar(wneg[0:nn, 1:2], wneg[0:nn, 0:1], -WIN_SCALE, None, ALU.mult).then_inc(neg_made, 1)

            def window_probs(b, j):
                nn = block_size(j)
                mm = nn + 2 * WIN
                dve.wait_ge(wexp_made, b * NBLK + j + 1)
                dve.reciprocal(wden[0:nn, 1:2], wden[0:nn, 0:1]).then_inc(win_den_made, 1)
                dve.wait_ge(win_den_made, b * NBLK + j + 1)
                dve.tensor_scalar(pm[0:nn, 0:mm], pm[0:nn, 0:mm], wden[0:nn, 1:2], None, ALU.mult).then_inc(wprob_made, 1)

            def window_residual(b, j):
                nn = block_size(j)
                n = slice(j * BLK, j * BLK + nn)
                Q[j % 2].wait_ready(dve, b, ("wo", j))
                for m in range(CT):
                    last = dve.scalar_tensor_tensor(x2[:, m, n], Q[j % 2].tile[:, m * P:m * P + nn], wb[:, 2, m:m + 1], x2[:, m, n],
                                                    ALU.add, ALU.add)
                last.then_inc(Q[j % 2].free, 1)

            for c in range(CT):
                channel_stats(0, c)
            channel_means(0)
            group_stats(0)
            group_offset(0)
            for j in QK:
                qk_lo(0, 0, *j)
            for u in range(UNITS):
                if u == TURN_AT:
                    shift(0, 0)
                if u == LAST_TURN_AT:
                    shift(0, 1)
                for r in ROWS[PAIRS - 1][u]:
                    row_max(0, r // NT, r % NT)
                if u // 4 == 1:
                    vf_lo(0, u % 4)
            turn_of_loop(0, False, True)
            with dve.Fori(1, B - 1) as b:
                turn_of_loop(b, True, True)
            turn_of_loop(B - 1, True, False)
            for piece in range(RECIPS):
                invert_sums(B - 1, 1, 1, piece)
            mix_on(dve, B - 1, 1, 1)
            for half in range(2):
                mix_lo_on(dve, B - 1, 1, half)
            residual(B - 1)
            for n in sorted(LAST_POST["dve"]):
                post(B - 1, "dve", n, LAST_POST)
            dve.wait_ge(logits_made, 1)
            parts = [M[k].tile[:, 0:NT * E].rearrange("p (t e) -> p t e", e=E) for k in range(2)]
            dve.tensor_copy(logits[:, :, :], parts[0]).then_inc(logits_out, 1)
            dve.wait_ge(logits_out, 1)
            dve.tensor_tensor(logits[:, :, :], logits[:, :, :], parts[1], ALU.add).then_inc(logits_out, 1)
            dve.wait_ge(logits_out, 2)


def expert_phase(nc, expert_w, lg, br, bn, bo, t_d, n_d, out):
    out_v = out.rearrange("b (c p) n -> b p c n", p=P)

    with ExitStack() as ctx:
        def sb(name, shape, dt=F32):
            return ctx.enter_context(nc.sbuf_tensor(name, shape, dt))

        def sem(name):
            return ctx.enter_context(nc.semaphore(name))

        wh, wl = expert_w
        gate = sb("gate", [P, E, N])
        gated_bo = sb("gated_output_bias", [P, CT, N])
        xf = sb("x_normed", [P, CT, N])
        xh = sb("x_hi", [P, CT, N], F32R)
        xl = sb("x_lo", [P, CT, N], F32R)
        tok = sb("tokens", [P, CT, N])
        h1h, h1l, h2h, h2l = (sb(k, [P, 2, CT, HALF], F32R) for k in ("h1_hi", "h1_lo", "h2_hi", "h2_lo"))
        z1 = sb("z1", [P, HALF])
        z2 = sb("z2", [P, HALF])
        bnp = sb("norm_params", [P, 2, 5, E, CT])
        scale = sb("norm_scale", [P, 2, E, CT])
        shift = sb("norm_shift", [P, 2, E, CT])
        half_p = sb("minus_half_p", [P, 2, E, CT])
        ident = sb("ident_b", [P, P])
        brb = sb("gate_b", [P, E])
        bos = sb("output_bias", [E, C])
        red = sb("gate_reduced", [P, 2, NT])
        gate_parts = [t[0:E, 0, :, :] for t in (h1h, h1l)]
        bias_parts = [t[0:E, 0, 0, 0:C] for t in (h2h, h2l)]
        units = h2h[0:E, 1, 0, 0:E]

        Z1, Z2 = ([ctx.enter_context(nc.psum_tensor(f"z{l}_{m}", [P, HALF], F32)) for m in range(CT)] for l in (1, 2))
        A = [[ctx.enter_context(nc.psum_tensor(f"sum{h}_{m}", [P, HALF], F32)) for m in range(CT)] for h in range(2)]

        in_small = sem("in_small")
        x_landed = sem("x_landed_b")
        ident_made, pow_asked, pow_made = sem("ident_b_made"), sem("pow_asked"), sem("pow_made")
        dve_gate, lg_shifted, lg_exp, gate_made = (
            sem(k) for k in ("dve_gate_chain", "lg_shifted", "lg_exp", "gate_made"))
        turned, gate_hi, gate_parts_made, bias_split, spread = (
            sem(k) for k in ("gate_turned", "gate_hi", "gate_parts_made", "bias_split", "gate_spread"))
        spread_out = [sem(f"gate_spread_out{k}") for k in range(2)]
        SPREADS = 2 * E + 2 * CT

        def spread_to(n):
            m = n // 2
            to = gate[:, m] if m < E else gated_bo[:, m - E]
            return to[:, n % 2 * HALF:(n % 2 + 1) * HALF]

        with nc.Block() as block:
            @block.sync
            def _(sp):
                sp.dma_start(brb[:, :], br.partition_broadcast(P)).then_inc(in_small, 16)
                sp.dma_start(bos[:, :], bo).then_inc(in_small, 16)
                sp.dma_start(bnp[:, :, :, :, :], bn).then_inc(in_small, 16)
                sp.dma_start(xf[:, :, :], n_d[0]).then_inc(x_landed, 16)

            @block.gpsimd
            def _(pool):
                pool.memset(ident[:, :], 0.0).then_inc(ident_made, 1)
                pool.memset(half_p[:, :, :, :], -0.5).then_inc(ident_made, 1)
                pool.wait_ge(ident_made, 2)
                pool.affine_select(out=ident[:, :], in_=ident[:, :], compare_op=ALU.not_equal, fill=1.0, base=0,
                                   pattern=[[-1, P]], channel_multiplier=1).then_inc(ident_made, 1)
                pool.wait_ge(pow_asked, 1)
                pool.tensor_tensor(scale[:, :, :, :], scale[:, :, :, :], half_p[:, :, :, :], ALU.pow).then_inc(pow_made, 1)

            @block.tensor
            def _(pe):
                pe.wait_ge(in_small, 3 * 16)
                pe.wait_ge(gate_made, 1)
                pe.wait_ge(ident_made, 3)
                for t in range(NT):
                    last = pe.transpose(A[t // 4][0][0:E, (t % 4) * P:(t % 4 + 1) * P], lg[:, t, :], ident[:, :])
                last.then_inc(turned, 1)
                pe.wait_ge(gate_parts_made, 2)
                pe.wait_ge(bias_split, 3)
                gh, gl = gate_parts
                for n in range(SPREADS):
                    m, half = n // 2, n % 2
                    if n >= 2:
                        pe.wait_ge(spread_out[n % 2], n // 2)
                    if m < E:
                        one = units[:, m:m + 1].broadcast_to([E, P])
                        pairs = ((one, gh), (one, gl))
                    else:
                        bh, bl = (part[:, (m - E) * P:(m - E + 1) * P] for part in bias_parts)
                        pairs = ((bh, gh), (bl, gh), (bh, gl))
                    for j, (l, g) in enumerate(pairs):
                        last = pe.matmul(Z2[n % 2][:, :], l, g[:, half], start=j == 0, stop=j == len(pairs) - 1)
                    last.then_inc(spread, 1)

            @block.scalar
            def _(act):
                act.wait_ge(lg_shifted, 1)
                act.activation(lg[:, :, :], lg[:, :, :], ACT.Exp).then_inc(lg_exp, 1)
                for n in range(1, SPREADS, 2):
                    act.wait_ge(spread, n + 1)
                    act.activation(spread_to(n), Z2[1][:, :], ACT.Copy).then_inc(spread_out[1], 1)

            @block.vector
            def _(dve):
                link = Link(dve, dve_gate, 0)
                dve.wait_ge(in_small, 3 * 16)
                link.done(dve.tensor_scalar(scale[:, :, :, :], bnp[:, :, 4], BN_EPS, None, ALU.add))
                link.wait()
                dve.sem_inc(pow_asked, 1)
                link.done(dve.scalar_tensor_tensor(lg[:, :, :], lg[:, :, :], 1.0 / B,
                                                   brb[:, :].unsqueeze(1).broadcast_to([P, NT, E]), ALU.mult, ALU.add))
                link.wait()
                link.done(dve.tensor_reduce(red[:, 0, :], lg[:, :, :], AXX, ALU.max))
                link.wait()
                dve.tensor_tensor(lg[:, :, :], lg[:, :, :], red[:, 0, :].unsqueeze(2).broadcast_to([P, NT, E]), ALU.subtract)\
                    .then_inc(lg_shifted, 1)
                dve.wait_ge(lg_exp, 1)
                link.done(dve.tensor_reduce(red[:, 1, :], lg[:, :, :], AXX, ALU.add))
                link.wait()
                link.done(dve.reciprocal(red[:, 0, :], red[:, 1, :]))
                link.wait()
                dve.tensor_tensor(lg[:, :, :], lg[:, :, :], red[:, 0, :].unsqueeze(2).broadcast_to([P, NT, E]), ALU.mult)\
                    .then_inc(gate_made, 1)
                dve.tensor_copy(bias_parts[0], bos[:, :]).then_inc(bias_split, 1)
                dve.wait_ge(ident_made, 3)
                dve.tensor_copy(units, ident[0:E, 0:E]).then_inc(bias_split, 1)
                dve.wait_ge(bias_split, 1)
                dve.tensor_tensor(bias_parts[1], bos[:, :], bias_parts[0].bitcast(F32), ALU.subtract).then_inc(bias_split, 1)
                dve.wait_ge(turned, 1)
                for half in range(2):
                    dve.tensor_copy(gate_parts[0][:, half], A[half][0][0:E, :]).then_inc(gate_hi, 1)
                    dve.wait_ge(gate_hi, half + 1)
                    dve.tensor_tensor(gate_parts[1][:, half], A[half][0][0:E, :], gate_parts[0][:, half].bitcast(F32),
                                      ALU.subtract).then_inc(gate_parts_made, 1)
                for n in range(0, SPREADS, 2):
                    dve.wait_ge(spread, n + 1)
                    dve.tensor_copy(spread_to(n), Z2[0][:, :]).then_inc(spread_out[0], 1)
                link.done(dve.tensor_tensor(shift[:, :, :, :], bnp[:, :, 0], bnp[:, :, 3], ALU.subtract))
                dve.wait_ge(pow_made, 1)
                link.wait()
                link.done(dve.tensor_tensor(scale[:, :, :, :], scale[:, :, :, :], bnp[:, :, 1], ALU.mult))
                link.wait()
                link.done(dve.tensor_tensor(shift[:, :, :, :], shift[:, :, :, :], scale[:, :, :, :], ALU.mult))
                link.wait()
                link.done(dve.tensor_tensor(shift[:, :, :, :], shift[:, :, :, :], bnp[:, :, 2], ALU.add))

        STEPS = 2 * E
        X_SPLIT_AT = {4: 1, STEPS - 4: 0}
        FINISH_AT = {3: 1, E + 3: 0}
        t_landed = sem("t_landed_b")
        out_stored = sem("out_stored")
        out_done = sem("out_done")
        xh_made, xl_made = sem("xh_made_b"), sem("xl_made_b")
        z1_ready, z2_ready = sem("z1_ready"), sem("z2_ready")
        z1_made, z2_made = sem("z1_made"), sem("z2_made")
        h1h_made, h1l_made = sem("h1h_made"), sem("h1l_made")
        h2_gated, h2h_made, h2l_made = sem("h2_gated"), sem("h2h_made"), sem("h2l_made")
        sum_ready = sem("sum_ready")
        sum_read = sem("sum_read")
        out_made = sem("out_made")

        def tokens_of(half):
            return slice(half * HALF, (half + 1) * HALF)

        block = ctx.enter_context(nc.Block())

        @block.sync
        def _(sp):
            def turn(b, ahead):
                sp.wait_ge(out_done, FREE + b)
                sp.dma_start(tok[:, :, :], t_d[b]).then_inc(t_landed, 16)
                if ahead:
                    sp.wait_ge(xl_made, FREE + (b + 1) * 2)
                    sp.dma_start(xf[:, :, :], n_d[b + 1]).then_inc(x_landed, 16)

            with sp.Fori(0, B - 1) as b:
                turn(b, True)
            turn(B - 1, False)

        @block.gpsimd
        def _(pool):
            def store(b, half):
                pool.wait_ge(out_made, b * 2 * CT + (half + 1) * CT)
                pool.dma_start(out_v[b, :, :, tokens_of(half)], tok[:, :, tokens_of(half)]).then_inc(out_stored, 16)

            for s in (out_done, h1h_made, h1l_made, z2_made, sum_read, h2l_made, z1_ready, xl_made):
                pool.sem_inc(s, FREE)
            with pool.Fori(0, B) as b:
                for half in range(2):
                    store(b, half)
                pool.wait_ge(out_stored, (b + 1) * 32)
                pool.sem_inc(out_done, 1)

        @block.tensor
        def _(pe):
            def layer(tile, e, which, m, rh, rl, start, stop):
                o = slice(m * P, (m + 1) * P)
                for k in range(CT):
                    for j, (w, r) in enumerate(((wh, rh), (wl, rh), (wh, rl))):
                        last = pe.matmul(tile[:, :], w[:, e, which, k, o], r[:, k], start=start and k == 0 and j == 0,
                                         stop=stop and k == CT - 1 and j == 2)
                return last

            def first(b, step, begun):
                half, e = divmod(step, E)
                n = tokens_of(half)
                if e == 0:
                    pe.wait_ge(xl_made, FREE + b * 2 + half + 1)
                for m in range(CT):
                    if begun:
                        pe.wait_ge(h1h_made, FREE + (b * STEPS + step - 1) * CT + m + 1)
                    layer(Z1[m], e, 0, m, xh[:, :, n], xl[:, :, n], True, True).then_inc(z1_ready, 1)

            def second(b, step, begun):
                done = b * STEPS + step
                pe.wait_ge(h1l_made, FREE + done * CT)
                for m in range(CT):
                    if begun:
                        pe.wait_ge(z2_made, FREE + (done - 2) * CT + m + 1)
                    layer(Z2[m], (step - 1) % E, 1, m, h1h[:, (step - 1) % 2], h1l[:, (step - 1) % 2], True, True)\
                        .then_inc(z2_ready, 1)

            def third(b, step, begun):
                half, e = divmod((step - 2) % STEPS, E)
                pe.wait_ge(h2l_made, FREE + (b * STEPS + step - 1) * CT)
                if e == 0 and begun:
                    pe.wait_ge(sum_read, FREE + (b * 2 + half - 1) * CT)
                for m in range(CT):
                    last = layer(A[half][m], e, 2, m, h2h[:, step % 2], h2l[:, step % 2], e == 0, e == E - 1)
                if e == E - 1:
                    last.then_inc(sum_ready, 1)

            def turn(b, after):
                for step in range(STEPS):
                    first(b, step, after or step >= 1)
                    if after or step >= 1:
                        second(b, step, after or step >= 2)
                    if after or step >= 2:
                        third(b, step, after)

            turn(0, False)
            with pe.Fori(1, B) as b:
                turn(b, True)
            second(B, 0, True)
            for step in range(2):
                third(B, step, True)

        @block.scalar
        def _(act):
            def split_x(b, half):
                n = tokens_of(half)
                if half == 0:
                    act.wait_ge(x_landed, (b + 1) * 16)
                act.wait_ge(z1_ready, FREE + (b * STEPS - (0 if half else E)) * CT)
                act.activation(xh[:, :, n], xf[:, :, n], ACT.Copy).then_inc(xh_made, 1)

            def first(b, step):
                e = step % E
                for m in range(CT):
                    c = (b * STEPS + step) * CT + m
                    act.wait_ge(z1_ready, FREE + c + 1)
                    act.wait_ge(h1l_made, FREE + c)
                    act.activation(z1[:, :], Z1[m][:, :], ACT.Relu, scale=scale[:, 0, e, m:m + 1],
                                   bias=shift[:, 0, e, m:m + 1]).then_inc(z1_made, 1)
                    act.activation(h1h[:, step % 2, m], Z1[m][:, :], ACT.Relu, scale=scale[:, 0, e, m:m + 1],
                                   bias=shift[:, 0, e, m:m + 1]).then_inc(h1h_made, 1)

            def second(b, step):
                e = (step - 1) % E
                for m in range(CT):
                    c = (b * STEPS + step - 1) * CT + m
                    act.wait_ge(z2_ready, c + 1)
                    act.wait_ge(h2l_made, FREE + c)
                    act.activation(z2[:, :], Z2[m][:, :], ACT.Relu, scale=scale[:, 1, e, m:m + 1],
                                   bias=shift[:, 1, e, m:m + 1]).then_inc(z2_made, 1)

            def turn(b, after, ahead):
                for step in range(STEPS):
                    first(b, step)
                    if after or step >= 1:
                        second(b, step)
                    if X_SPLIT_AT.get(step) == 1:
                        split_x(b, 1)
                    if X_SPLIT_AT.get(step) == 0 and ahead:
                        split_x(b + 1, 0)

            act.wait_ge(x_landed, 16)
            act.activation(xh[:, :, tokens_of(0)], xf[:, :, tokens_of(0)], ACT.Copy).then_inc(xh_made, 1)
            turn(0, False, True)
            with act.Fori(1, B - 1) as b:
                turn(b, True, True)
            turn(B - 1, True, False)
            second(B, 0)

        @block.vector
        def _(dve):
            def split_x(b, half):
                n = tokens_of(half)
                dve.wait_ge(xh_made, b * 2 + half + 1)
                dve.tensor_tensor(xl[:, :, n], xf[:, :, n], xh[:, :, n].bitcast(F32), ALU.subtract).then_inc(xl_made, 1)

            def first(b, step):
                for m in range(CT):
                    dve.wait_ge(h1h_made, FREE + (b * STEPS + step) * CT + m + 1)
                    dve.tensor_tensor(h1l[:, step % 2, m], z1[:, :], h1h[:, step % 2, m].bitcast(F32), ALU.subtract)\
                        .then_inc(h1l_made, 1)

            def second(b, step):
                half, e = divmod((step - 1) % STEPS, E)
                slot = (step - 1) % 2
                for m in range(CT):
                    c = (b * STEPS + step - 1) * CT + m
                    dve.wait_ge(z2_made, FREE + c + 1)
                    dve.tensor_tensor(z2[:, :], z2[:, :], gate[:, e, tokens_of(half)], ALU.mult).then_inc(h2_gated, 1)
                    dve.wait_ge(h2_gated, c + 1)
                    dve.tensor_copy(h2h[:, slot, m], z2[:, :]).then_inc(h2h_made, 1)
                    dve.wait_ge(h2h_made, c + 1)
                    dve.tensor_tensor(h2l[:, slot, m], z2[:, :], h2h[:, slot, m].bitcast(F32), ALU.subtract)\
                        .then_inc(h2l_made, 1)

            def finish(b, half):
                n = tokens_of(half)
                dve.wait_ge(sum_ready, b * 2 + half + 1)
                if half == 0:
                    dve.wait_ge(t_landed, (b + 1) * 16)
                for m in range(CT):
                    dve.tensor_tensor(tok[:, m, n], A[half][m][:, :], tok[:, m, n], ALU.add).then_inc(sum_read, 1)
                    dve.wait_ge(sum_read, FREE + b * 2 * CT + half * CT + m + 1)
                    dve.tensor_tensor(tok[:, m, n], tok[:, m, n], gated_bo[:, m, n], ALU.add).then_inc(out_made, 1)

            def turn(b, after, ahead):
                for step in range(STEPS):
                    first(b, step)
                    if after or step >= 1:
                        second(b, step)
                    if X_SPLIT_AT.get(step) == 1:
                        split_x(b, 1)
                    if X_SPLIT_AT.get(step) == 0 and ahead:
                        split_x(b + 1, 0)
                    if FINISH_AT.get(step) == 0:
                        finish(b, 0)
                    if FINISH_AT.get(step) == 1 and after:
                        finish(b - 1, 1)

            split_x(0, 0)
            turn(0, False, True)
            with dve.Fori(1, B - 1) as b:
                turn(b, True, True)
            turn(B - 1, True, False)
            second(B, 0)
            finish(B - 1, 1)


def build(nc, a, t_d, n_d, feat_d, out):
    at = -(-nc.sbuf_base // 32) * 32
    with ExitStack() as ctx:
        w = [ctx.enter_context(nc.sbuf_tensor(f"expert_w_{part}", [P, E, 3, CT, C], F32R)) for part in ("hi", "lo")]
        logits = ctx.enter_context(nc.sbuf_tensor("logits", [P, NT, E], F32))
        attention_phase(nc, w, at, logits, a["W"], a["Wr"], a["x"], a["qkv_wT"], a["qkv_b"], a["proj_wT"], a["proj_b"], a["alpha"],
                        a["window_wT"], a["window_b"], a["diffusion"], t_d, n_d, feat_d)
        expert_phase(nc, w, logits, a["br"], a["bn"], a["bo"], t_d, n_d, out)


def diffusion_matrices():
    g = np.exp(-np.subtract.outer(np.arange(H), np.arange(H)).astype(np.float64) ** 2 / 2)
    a = np.kron(g, g)
    lap = np.diag(a.sum(1)) - a
    lam = np.linalg.eigvalsh(lap).max()
    hat = 2.0 / lam * lap - np.eye(N)
    cube = hat @ hat @ hat
    eye = np.eye(HH)
    fold = [np.concatenate([eye, s * eye[::-1]]) for s in (1, -1)]
    blocks = [np.kron(fy, fx) for fy in fold for fx in fold]
    return np.stack([f.T @ cube @ f / 16 for f in blocks]).astype(np.float32)


def kernel(**inputs):
    import concourse.bacc as bacc
    from concourse.bass_utils import run_bass_kernel_spmd

    i = {k: np.asarray(a) for k, a in inputs.items()}

    def channels(a):
        a = a.reshape(a.shape[:-1] + (-1, P))
        return np.moveaxis(a, -1, 0)

    arrays = {
        "x": i["x"].reshape(B, C, N),
        "qkv_wT": i["L0_conv_qkv_w"].T,
        "qkv_b": channels(i["L0_conv_qkv_b"]),
        "proj_wT": i["L0_conv_proj_w"].T,
        "proj_b": channels(i["L0_conv_proj_b"]),
        "alpha": i["L0_conv_alpha"].reshape(1),
        "window_wT": np.stack([i[f"L1_attn_W{k}"].T for k in "qkv"]),
        "window_b": channels(np.stack([i[f"L1_attn_b{k}"] for k in "qkv"])),
        "diffusion": diffusion_matrices(),
        "Wr": i["L1_ffn_Wr"],
        "br": i["L1_ffn_br"],
        "W": np.stack([i["L1_ffn_W1"], i["L1_ffn_W2"], i["L1_ffn_Wo"]]),
        "bn": channels(np.stack([np.stack([i[f"L1_ffn_{k}{l}"] for k in ("b", "g", "be", "m", "v")]) for l in (1, 2)])),
        "bo": i["L1_ffn_bo"],
    }
    arrays = {k: np.ascontiguousarray(a) for k, a in arrays.items()}
    nc = bacc.Bacc("TRN2", target_bir_lowering=False, num_devices=1)
    a = {k: nc.dram_tensor(k, v.shape, mybir.dt.from_np(v.dtype), kind="ExternalInput").ap() for k, v in arrays.items()}
    out = nc.dram_tensor("out", (B, C, N), F32, kind="ExternalOutput").ap()
    t_d = nc.dram_tensor("tokens_after_attention", (B, P, CT, N), F32, kind="Internal").ap()
    n_d = nc.dram_tensor("tokens_normed", (B, P, CT, N), F32, kind="Internal").ap()
    feat_d = nc.dram_tensor("normed_sum_over_batches", (P, CT, N), F32, kind="Internal").ap()
    build(nc, a, t_d, n_d, feat_d, out)
    r = run_bass_kernel_spmd(nc, [arrays], core_ids=[0])
    return r.results[0]["out"].reshape(B, C, H, W)
```
